# Optimizing a Trainium2 kernel written in Bass

```python
import numpy as np
import jax
import jax.numpy as jnp

def _softmax(x, axis=-1):
    return jax.nn.softmax(x, axis=axis)

def _gelu(x):
    return jax.nn.gelu(x, approximate=True)

def _silu(x):
    return jax.nn.silu(x)

def _sigmoid(x):
    return jax.nn.sigmoid(x)

def _layernorm(x, axis=-1, eps=1e-05):
    m = jnp.mean(x, axis=axis, keepdims=True)
    v = jnp.var(x, axis=axis, keepdims=True)
    return (x - m) / jnp.sqrt(v + eps)

def _scatter_add(tgt, idx, src, axis=0):
    return tgt.at[idx].add(src)

def _segment_sum(src, seg, n):
    return jax.ops.segment_sum(src, seg, n)
kernel_name = 'mk_decoder_postln_d1_seqx_r8_24f122'

def setup_inputs(seed: int=0):
    np.random.seed(seed)
    _w = jnp.asarray

    def _rec_inputs():
        import jax
        import jax.numpy as jnp
        _rk = jax.random.key(seed)
        x = 7.22e-05 + 1 * jax.random.normal(jax.random.fold_in(_rk, 1), (16, 128, 256), jnp.float32)
        _lenS = 128 - jax.random.randint(jax.random.fold_in(_rk, 7), (16,), 0, max(1, 128 // 4) + 1, jnp.int32)
        _lenS2 = 128 - jax.random.randint(jax.random.fold_in(_rk, 8), (16,), 0, max(1, 128 // 4) + 1, jnp.int32)
        _ctx_512P = jax.random.normal(jax.random.fold_in(_rk, 11), (16, 16, 64), jnp.float32)
        _ctx_512c = jax.random.dirichlet(jax.random.fold_in(_rk, 511), 0.3 * jnp.ones((16,), jnp.float32), (16, 128))
        _ctx_512t = jnp.einsum('bsk,bkd->bsd', _ctx_512c, _ctx_512P)
        _ctx_512t = _ctx_512t * jax.lax.rsqrt(jnp.mean(jnp.square(_ctx_512t)) + 1e-12) * 0.953939
        ctx_512 = -0.000514642 + 1.00011 * (_ctx_512t + 0.3 * jax.random.normal(jax.random.fold_in(_rk, 611), (16, 128, 64), jnp.float32))
        return (x, ctx_512)
    x, ctx_512 = _rec_inputs()

    def _L0_attn_setup():
        import jax, jax.numpy as jnp
        import numpy as np
        D_MODEL = 256
        HEADS = 16
        HEAD_DIM = D_MODEL // HEADS
        key = jax.random.key(seed)
        k1, k2, k3 = jax.random.split(key, 3)
        B, S = (1, 256)
        x = jax.random.normal(k1, (B, S, D_MODEL), dtype=jnp.float32)
        Wqkv_w = jax.random.normal(k2, (D_MODEL + 2 * HEAD_DIM, D_MODEL), dtype=jnp.float32) * D_MODEL ** (-0.5)
        Wqkv_b = jnp.zeros((D_MODEL + 2 * HEAD_DIM,), dtype=jnp.float32)
        out_w = jax.random.normal(k3, (D_MODEL, D_MODEL), dtype=jnp.float32) * D_MODEL ** (-0.5)
        out_b = jnp.zeros((D_MODEL,), dtype=jnp.float32)
        return {'x': x, 'Wqkv_w': Wqkv_w, 'Wqkv_b': Wqkv_b, 'out_w': out_w, 'out_b': out_b}
    _L0_attn_all = _L0_attn_setup()
    _L0_attn_in = {k: v for k, v in _L0_attn_all.items() if k in ('Wqkv_w', 'Wqkv_b', 'out_w', 'out_b')}
    del _L0_attn_all

    def _L0_xattn_setup():
        import jax, jax.numpy as jnp
        import numpy as np
        import math
        NUM_Q_HEADS = 32
        NUM_KV_HEADS = 8
        key = jax.random.key(seed)
        k1, k2, k3 = jax.random.split(key, 3)
        B, S, E = (2, 256, 256)
        kv_E = NUM_KV_HEADS * (E // NUM_Q_HEADS)
        q = jax.random.normal(k1, (B, S, E), dtype=jnp.float32)
        k = jax.random.normal(k2, (B, S, kv_E), dtype=jnp.float32)
        v = jax.random.normal(k3, (B, S, kv_E), dtype=jnp.float32)
        return {'q': q, 'k': k, 'v': v}
    _L0_xattn_all = _L0_xattn_setup()
    _L0_xattn_in = {k: v for k, v in _L0_xattn_all.items() if k in ()}
    del _L0_xattn_all

    def _L0_ffn_setup():
        import jax, jax.numpy as jnp
        import numpy as np
        H, I, E, K = (256, 512, 8, 2)
        B, S = (1, 256)

        def _silu_mul(gu):
            d = gu.shape[-1] // 2
            return jax.nn.silu(gu[..., :d]) * gu[..., d:]
        key = jax.random.key(seed)
        ks = jax.random.split(key, 6)
        w_scale = 0.02
        return {'x': jax.random.normal(ks[0], (B, S, H), jnp.float32), 'gate_w': jax.random.normal(ks[1], (H, E), jnp.float32) * w_scale, 'base_gate_up': jax.random.normal(ks[2], (H, 2 * I), jnp.float32) * w_scale, 'base_down': jax.random.normal(ks[3], (I, H), jnp.float32) * w_scale, 'expert_gate_up': jax.random.normal(ks[4], (E, H, 2 * I), jnp.float32) * w_scale, 'expert_down': jax.random.normal(ks[5], (E, I, H), jnp.float32) * w_scale}
    _L0_ffn_all = _L0_ffn_setup()
    _L0_ffn_in = {k: v for k, v in _L0_ffn_all.items() if k in ('gate_w', 'base_gate_up', 'base_down', 'expert_gate_up', 'expert_down')}
    del _L0_ffn_all
    return {'x': x, 'ctx_512': ctx_512, 'L0_attn_Wqkv_w': _L0_attn_in['Wqkv_w'], 'L0_attn_Wqkv_b': _L0_attn_in['Wqkv_b'], 'L0_attn_out_w': _L0_attn_in['out_w'], 'L0_attn_out_b': _L0_attn_in['out_b'], 'L0_ffn_gate_w': _L0_ffn_in['gate_w'], 'L0_ffn_base_gate_up': _L0_ffn_in['base_gate_up'], 'L0_ffn_base_down': _L0_ffn_in['base_down'], 'L0_ffn_expert_gate_up': _L0_ffn_in['expert_gate_up'], 'L0_ffn_expert_down': _L0_ffn_in['expert_down']}

def reference(x, ctx_512, L0_attn_Wqkv_w, L0_attn_Wqkv_b, L0_attn_out_w, L0_attn_out_b, L0_ffn_gate_w, L0_ffn_base_gate_up, L0_ffn_base_down, L0_ffn_expert_gate_up, L0_ffn_expert_down):
    import jax
    import jax.numpy as jnp

    def _L0_attn_ref(x, Wqkv_w, Wqkv_b, out_w, out_b):
        import jax, jax.numpy as jnp
        import numpy as np
        D_MODEL = 256
        HEADS = 16
        HEAD_DIM = D_MODEL // HEADS
        B, S, _ = x.shape
        qkv = jnp.einsum('bsd,ed->bse', x, Wqkv_w) + Wqkv_b
        q = qkv[..., :D_MODEL]
        k = qkv[..., D_MODEL:D_MODEL + HEAD_DIM]
        v = qkv[..., D_MODEL + HEAD_DIM:]
        q = q.reshape(B, S, HEADS, HEAD_DIM)
        scale = 1.0 / np.sqrt(HEAD_DIM)
        scores = jnp.einsum('bqhd,bkd->bhqk', q, k) * scale
        min_val = jnp.finfo(scores.dtype).min
        causal = jnp.tril(jnp.ones((S, S), dtype=bool))
        scores = jnp.where(causal[None, None], scores, min_val)
        attn = jax.nn.softmax(scores, axis=-1)
        ctx = jnp.einsum('bhqk,bkd->bqhd', attn, v)
        ctx = ctx.reshape(B, S, D_MODEL)
        out = jnp.einsum('bsd,ed->bse', ctx, out_w) + out_b
        return out

    def _L0_xattn_ref(q, k, v):
        import jax, jax.numpy as jnp
        import numpy as np
        import math
        NUM_Q_HEADS = 32
        NUM_KV_HEADS = 8
        B, S, E = q.shape
        H, KV = (NUM_Q_HEADS, NUM_KV_HEADS)
        D = E // H
        G = H // KV
        scale = math.sqrt(D)
        qh = q.reshape(B, S, KV, G, D).transpose(0, 2, 3, 1, 4)
        kh = k.reshape(B, S, KV, D).transpose(0, 2, 1, 3)
        vh = v.reshape(B, S, KV, D).transpose(0, 2, 1, 3)
        scores = jnp.einsum('bkgsd,bktd->bkgst', qh, kh) / scale
        weights = jax.nn.softmax(scores, axis=-1)
        out = jnp.einsum('bkgst,bktd->bkgsd', weights, vh)
        return out.transpose(0, 3, 1, 2, 4).reshape(B, S, E)

    def _L0_ffn_ref(x, gate_w, base_gate_up, base_down, expert_gate_up, expert_down):
        import jax, jax.numpy as jnp
        import numpy as np
        H, I, E, K = (256, 512, 8, 2)
        B, S = (1, 256)

        def _silu_mul(gu):
            d = gu.shape[-1] // 2
            return jax.nn.silu(gu[..., :d]) * gu[..., d:]
        base_y = _silu_mul(x @ base_gate_up) @ base_down
        b, s, h = x.shape
        xf = x.reshape(-1, h)
        n = xf.shape[0]
        n_exp = gate_w.shape[1]
        probs = jax.nn.softmax((xf @ gate_w).astype(jnp.float32), axis=-1)
        w, idx = jax.lax.top_k(probs, K)
        w = (w / w.sum(axis=-1, keepdims=True)).astype(x.dtype)
        comb = jnp.zeros((n, n_exp), x.dtype).at[jnp.arange(n)[:, None], idx].add(w)
        out = jnp.zeros_like(xf)
        for e in range(n_exp):
            y = _silu_mul(xf @ expert_gate_up[e]) @ expert_down[e]
            out = out + comb[:, e:e + 1] * y
        return out.reshape(b, s, h) + base_y
    x = _layernorm(x + _L0_attn_ref(x, L0_attn_Wqkv_w, L0_attn_Wqkv_b, L0_attn_out_w, L0_attn_out_b), axis=-1)
    x = _layernorm(x + _L0_xattn_ref(x, ctx_512, ctx_512), axis=-1)
    x = _layernorm(x + _L0_ffn_ref(x, L0_ffn_gate_w, L0_ffn_base_gate_up, L0_ffn_base_down, L0_ffn_expert_gate_up, L0_ffn_expert_down), axis=-1)
    return x

_drawn_inputs = setup_inputs


def setup_inputs(seed=0):
    import zlib

    import numpy as np

    out = dict(_drawn_inputs(seed))
    spreads = {'L0_attn_Wqkv_b': (0.0, 0.1), 'L0_attn_out_b': (0.0, 0.1)}
    factors = {'L0_ffn_gate_w': 3.857,
     'L0_ffn_expert_gate_up': 3.334,
     'L0_ffn_expert_down': 3.332,
     'L0_ffn_base_gate_up': 2.985,
     'L0_ffn_base_down': 2.974}
    for name, (base, spread) in spreads.items():
        noise = np.random.default_rng([zlib.crc32(name.encode()), seed]).standard_normal(out[name].shape)
        drawn = base * np.exp(spread * noise) if base else spread * noise
        out[name] = jnp.asarray(drawn.astype(out[name].dtype))
    for name, factor in factors.items():
        out[name] = (out[name] * factor).astype(out[name].dtype)
    return out
```

```python
from contextlib import ExitStack

import numpy as np

import concourse.bass as bass
from concourse import mybir

F32 = mybir.dt.float32
F32R = mybir.dt.float32r
BF16 = mybir.dt.bfloat16
ALU = mybir.AluOpType
ACT = mybir.ActivationFunctionType
AX = mybir.AxisListType

B, S, D = 16, 128, 256
HEADS, HD = 16, 16
XKV, XG, XD = 8, 4, 8
INNER, EXPERTS = 512, 8
P = 128
QKV = D + 2 * HD
EPS = 1e-5
MASKED = -1e30
SCALE_S = float(HD) ** -0.5
SCALE_X = float(XD) ** -0.5
GROUP = 512
GROUPS = B * S // GROUP
TILES = GROUP // P
NETS = EXPERTS + 1

ORDER = [
    ("s_qkv", 0, 2), ("c_max", 0, 0), ("c_max", 1, 0),
    ("s_turn", 0, 2), ("c_max", 2, 0), ("c_max", 3, 0),
    ("s_max", 0, 1), ("s_max", 1, 1), ("c_shift", 0, 0),
    ("s_shift", 0, 1), ("c_main", 0, 0), ("c_main", 1, 0),
    ("s_main", 0, 1), ("c_sum", 0, 0), ("c_main", 2, 0),
    ("s_sum", 0, 1), ("s_main", 1, 1), ("c_sum", 1, 0), ("c_main", 3, 0),
    ("s_sum", 1, 1), ("s_out", 0, 1), ("c_sum", 2, 0),
    ("s_out", 1, 1), ("s_proj", 0, 1), ("c_sum", 3, 0), ("c_out", 0, 0),
    ("s_res", 0, 1), ("c_out", 1, 0), ("s_ln", 0, 1), ("c_ln", 0, 0), ("c_turn", 0, 1),
]
DELTAS = [d for _, _, d in ORDER]
FIRST_STEP, LAST_STEP = -max(DELTAS), B - 1 - min(DELTAS)
LOOP_FROM = 2
LOOP_STEPS = (B - max(DELTAS) - LOOP_FROM) // 2 * 2

SCORE_USE = {"s_max": ("s_max_read", 2), "s_main": ("s_exp", 2), "c_max": ("c_max_read", 4), "c_main": ("c_exp", 4)}
PROB_USE = {"s_main": ("s_summed", 2), "c_main": ("c_summed", 4)}
SUM_USE = {"s_sum": ("s_sum_read", 2), "c_sum": ("c_sum_read", 2)}
MISC_USE = {
    "s_qkv": [("s_qkv_read", 1, 1)],
    "s_turn": [("s_q_read", 2, 1), ("s_q_read", 2, 2), ("s_k_read", 1, 1)],
    "s_shift": [("s_shift_read", 1, 1)],
    "s_out": [("s_out_read", 2, None)],
    "s_proj": [("s_ctx_read", 1, 1)],
    "s_res": [("s_res_read", 1, 1)],
    "c_turn": [("c_q_read", 2, 1), ("c_q_read", 2, 2)],
    "c_shift": [("c_shift_read", 1, 1)],
    "c_out": [("c_out_read", 2, None)],
}


class Seq:

    def __init__(self, off, i=None):
        self.off, self.i = off, i

    def at(self, per, plus=0):
        v = per * self.off + plus
        return v if self.i is None else self.i * (2 * per) + v

    def back(self, n):
        return Seq(self.off - n, self.i)

    @property
    def odd(self):
        return self.off % 2

    @property
    def exists(self):
        return 0 <= self.off < B if self.i is None else self.off >= 0


def wait(eng, sem, seq, per=1, upto=None):
    assert seq.i is None or seq.exists
    if seq.exists:
        eng.wait_ge(sem, seq.at(per, per if upto is None else upto))


class Ring:

    def __init__(self, slots, uses):
        self.slots, self.uses = slots, uses
        assert 2 * len(uses) % slots == 0

    def _at(self, stage, unit, part):
        return next(n for n, u in enumerate(self.uses) if u[:3] == (stage, unit, part))

    def slot(self, stage, unit, seq, part=0):
        n = self._at(stage, unit, part)
        return ((seq.off - self.uses[n][3]) * len(self.uses) + n) % self.slots

    def wait_free(self, eng, sems, stage, unit, seq, part=0):
        n = self._at(stage, unit, part)
        at = (seq.off - self.uses[n][3]) * len(self.uses) + n
        while True:
            at -= self.slots
            step, m = divmod(at, len(self.uses))
            _, _, _, delta, name, per, upto = self.uses[m]
            if step + delta < -2 * len(self.uses):
                return
            before = Seq(step + delta, seq.i)
            assert seq.i is None or before.exists
            if before.exists:
                eng.wait_ge(sems[name], before.at(per, upto))
                return


def rings():
    score, prob, summed, misc = [], [], [], []
    for stage, unit, delta in ORDER:
        if stage in SCORE_USE:
            name, per = SCORE_USE[stage]
            score.append((stage, unit, 0, delta, name, per, unit + 1))
        if stage in PROB_USE:
            name, per = PROB_USE[stage]
            prob.append((stage, unit, 0, delta, name, per, unit + 1))
        if stage == "s_sum" or stage == "c_sum" and unit % 2 == 0:
            name, per = SUM_USE[stage]
            summed.append((stage, unit, 0, delta, name, per, (unit if stage == "s_sum" else unit // 2) + 1))
        for part, (name, per, upto) in enumerate(MISC_USE.get(stage, [])):
            misc.append((stage, unit, part, delta, name, per, unit + 1 if upto is None else upto))
    return Ring(2, score), Ring(4, prob), Ring(2, summed), Ring(2, misc)


def decoder_layer(nc, x, xT, ctx, ctxT, wqkvT, bqkv, woT, bo, gate_w, base_gu, base_down, exp_gu, exp_down, consts, out):
    with ExitStack() as both:
        def sb(name, shape, dt=F32, scope=both):
            return scope.enter_context(nc.sbuf_tensor(name, shape, dt))

        stream = sb("stream", [P, B, D])
        raw_gu0, raw_down0 = sb("raw_gu0", [P, 2, 2 * INNER]), sb("raw_down0", [P, INNER // P, D])
        gu_hi0, gu_lo0 = sb("gu_hi0", [P, 2, 2 * INNER], F32R), sb("gu_lo0", [P, 2, 2 * INNER], F32R)
        down_hi0, down_lo0 = sb("down_hi0", [P, INNER // P, D], F32R), sb("down_lo0", [P, INNER // P, D], F32R)
        ident = sb("ident", [P, P])
        eps = sb("eps", [P, 1])
        raw_loaded = [both.enter_context(nc.semaphore(f"raw_loaded{p}")) for p in range(2)]
        gu_split = both.enter_context(nc.semaphore("gu_split"))
        down_split = both.enter_context(nc.semaphore("down_split"))
        weights0 = (raw_gu0, raw_down0, gu_hi0, gu_lo0, down_hi0, down_lo0, raw_loaded, gu_split, down_split)
        attention(nc, x, xT, ctx, ctxT, wqkvT, bqkv, woT, bo, consts, stream, ident, eps, base_gu, base_down,
                  exp_gu, exp_down, weights0)
        experts(nc, gate_w, exp_gu, exp_down, consts, stream, ident, eps, weights0, out)


def load_net(eng, net, raw_gu, raw_down, loaded, gu, down):
    g = gu if net is None else gu[bass.ds(net, 1)].squeeze(0) if not isinstance(net, int) else gu[net]
    d = down if net is None else down[bass.ds(net, 1)].squeeze(0) if not isinstance(net, int) else down[net]
    eng.dma_start(raw_gu[:], g.rearrange("(k p) n -> p k n", p=P)).then_inc(loaded, 16)
    eng.dma_start(raw_down[:], d.rearrange("(k p) n -> p k n", p=P)).then_inc(loaded, 16)


def attention(nc, x, xT, ctx, ctxT, wqkvT, bqkv, woT, bo, consts, stream, ident, eps, base_gu, base_down,
              exp_gu, exp_down, weights0):
    raw_gu0, raw_down0, gu_hi0, gu_lo0, down_hi0, down_lo0, raw_loaded, gu_split, down_split = weights0
    score_ring, prob_ring, sum_ring, misc_ring = rings()
    with ExitStack() as scope:
        def sb(name, shape, dt=F32):
            return scope.enter_context(nc.sbuf_tensor(name, shape, dt))

        def two(name, shape, dt=F32):
            return [sb(f"{name}{p}", shape, dt) for p in range(2)]

        scores = scope.enter_context(nc.psum_tensor("scores", [P, 2, 1024], F32))
        sums = scope.enter_context(nc.psum_tensor("sums", [P, 2, 512], F32))
        misc = scope.enter_context(nc.psum_tensor("misc", [P, 2, 512], F32))

        cst = sb("cst", [P, 3 * P + 24])
        ident_r, ident_b = sb("ident_r", [P, P], F32R), sb("ident_b", [P, P], BF16)
        mask_qk, mask_kq = sb("mask_qk", [P, 4, P], BF16), sb("mask_kq", [P, 4, P], BF16)
        blk_s, blk_c = cst[:, 3 * P:3 * P + 2], cst[:, 3 * P + 2:3 * P + 6]
        neg_s, neg_c = cst[0:32, 3 * P + 6:3 * P + 14], cst[0:32, 3 * P + 14:3 * P + 22]
        raw_wqkv, raw_wo = sb("raw_wqkv", [P, 2, QKV]), sb("raw_wo", [P, 2, D])
        wqkv_hi, wqkv_lo = sb("wqkv_hi", [P, 2, QKV], F32R), sb("wqkv_lo", [P, 2, QKV], F32R)
        wo_hi, wo_lo = sb("wo_hi", [P, 2, D], F32R), sb("wo_lo", [P, 2, D], F32R)
        b_qkv, b_o = sb("b_qkv", [P, QKV]), sb("b_o", [P, D])

        xT_in, x_in = two("xT_in", [P, 2, S]), two("x_in", [P, D])
        ctxT_in, ctx_in = two("ctxT_in", [96, 2, S]), two("ctx_in", [P, XKV * XD])
        xT_hi, xT_lo = two("xT_hi", [P, 2, S], F32R), two("xT_lo", [P, 2, S], F32R)
        x_bias = two("x_bias", [P, D])

        qkv = sb("qkv", [P, QKV])
        rows_s = sb("rows_s", [P, 9, 96], F32R)
        q_s = two("q_s", [P, 8, S], F32R)
        k_s = two("k_s", [P, 2, S], F32R)
        v_s = two("v_s", [P, 2, 192], F32R)
        max_s = sb("max_s", [P, 32])
        sumT_s = sb("sumT_s", [P, 2, 512])
        rden_s = sb("rden_s", [P, 2, 8])
        raw_s = sb("raw_s", [P, 2, 8, HD])
        ctx_s = two("ctx_s", [P, D])
        ctxT_hi, ctxT_lo = sb("ctxT_hi", [P, 2, S], F32R), sb("ctxT_lo", [P, 2, S], F32R)
        pre1, x1 = two("pre1_", [P, D]), two("x1_", [P, D])

        rows_c = sb("rows_c", [P, 8, 96], F32R)
        q_c = two("q_c", [P, 8, S], F32R)
        k_split = sb("k_split", [96, 2, S], F32R)
        k_c = two("k_c", [P, 2, 4, S], F32R)
        v_c = two("v_c", [P, 2, 640], F32R)
        max_c = sb("max_c", [P, 32])
        sumT_c = sb("sumT_c", [P, 2, 512])
        rden_c = sb("rden_c", [P, 2, 16])
        raw_c = sb("raw_c", [P, 2, 4, 4, XD])
        ctx_c = sb("ctx_c", [P, D])
        pre2 = two("pre2_", [P, D])

        in_zero = sb("in_zero_t", [P, 2, S])
        prob, prob_hi, prob_lo = sb("prob", [P, 4, 1024]), sb("prob_hi", [P, 4, 1024], F32R), sb("prob_lo", [P, 4, 1024], F32R)
        norm = {k: dict(stats=sb(f"stats_{k}", [P, 6]), mv=sb(f"mv_{k}", [P, 2]), ln=sb(f"ln_{k}", [P, 1]),
                        r=sb(f"r_{k}", [P, 1]), t=sb(f"t_{k}", [P, 3])) for k in "sc"}

        names = """consts_loaded consts_set weights_loaded w_hi w_split tables tables_b
            xT_hi_set xT_split x_biased s_qkv_full s_qkv_read s_rows_hi s_rows_lo s_q_full s_q_read s_k_full s_k_read
            s_max_full s_max_read s_shift_full s_shift_read s_main_full s_exp s_prob_hi s_prob_lo s_summed s_sum_read
            s_out_full s_rden s_out_read s_ctx s_ctx_full s_ctx_hi s_ctx_read s_res_full s_res_read s_stats s_mv s_ln s_rsqrt0
            s_newton x1_set
            ctx_k_hi ctx_k_lo ctx_k_set ctx_v_hi ctx_v_set c_rows_hi c_rows_lo c_q_full c_q_read c_max_full c_max_read c_shift_full
            c_shift_read c_main_full c_exp c_prob_hi c_prob_lo c_summed c_sum_read c_out_full c_rden c_out_read c_ctx c_res
            c_stats c_mv c_ln c_rsqrt0 c_newton x2_set net0_hi in_zero""".split()
        sem = {n: scope.enter_context(nc.semaphore(n)) for n in names}
        x_loaded = [scope.enter_context(nc.semaphore(f"x_loaded{p}")) for p in range(2)]
        ctx_loaded = [scope.enter_context(nc.semaphore(f"ctx_loaded{p}")) for p in range(2)]

        def f32(ap):
            return ap.bitcast(F32)

        def run(eng, stages):
            def step(s, i=None):
                for stage, unit, delta in ORDER:
                    seq = Seq(s + delta, i)
                    if stage in stages and seq.exists:
                        stages[stage](seq, unit)
            for s in range(FIRST_STEP, LOOP_FROM):
                step(s)
            with eng.Fori(0, LOOP_STEPS // 2) as i:
                step(LOOP_FROM, i)
                step(LOOP_FROM + 1, i)
            for s in range(LOOP_FROM + LOOP_STEPS, LAST_STEP + 1):
                step(s)

        def loaded_value(seq):
            v = 32 * (seq.off // 2 + 1)
            return v if seq.i is None else seq.i * 32 + v

        block = scope.enter_context(nc.Block())

        @block.sync
        def _(sp):
            sp.dma_start(cst[:, 0:3 * P + 22], consts[:, 0:3 * P + 22]).then_inc(sem["consts_loaded"], 16)
            sp.dma_start(raw_wqkv[:], wqkvT.rearrange("(k p) n -> p k n", p=P)).then_inc(sem["weights_loaded"], 16)
            sp.dma_start(b_qkv[:], bqkv.partition_broadcast(P)).then_inc(sem["weights_loaded"], 16)
            sp.dma_start(raw_wo[:], woT.rearrange("(k p) n -> p k n", p=P)).then_inc(sem["weights_loaded"], 16)
            sp.dma_start(b_o[:], bo.partition_broadcast(P)).then_inc(sem["weights_loaded"], 16)

            def load(seq):
                p = seq.odd
                wait(sp, sem["xT_split"], seq.back(2))
                wait(sp, sem["x_biased"], seq.back(2))
                sp.dma_start(xT_in[p][:], xT.rearrange("(k p) t -> p k t", p=P)[:, :, bass.ds(seq.at(S), S)]).then_inc(x_loaded[p], 16)
                sp.dma_start(x_in[p][:], x[bass.ds(seq.at(S), S), :]).then_inc(x_loaded[p], 16)
                wait(sp, sem["ctx_k_lo"], seq.back(2))
                wait(sp, sem["ctx_v_set"], seq.back(2))
                sp.dma_start(ctxT_in[p][:], ctxT[:, :, bass.ds(seq.at(S), S)]).then_inc(ctx_loaded[p], 16)
                sp.dma_start(ctx_in[p][:], ctx[bass.ds(seq.at(S), S), :]).then_inc(ctx_loaded[p], 16)

            load(Seq(0))
            load(Seq(1))
            load_net(sp, None, raw_gu0, raw_down0, raw_loaded[0], base_gu, base_down)
            with sp.Fori(0, B // 2 - 1) as i:
                load(Seq(2, i))
                load(Seq(3, i))

        @block.gpsimd
        def _(pool):
            pool.wait_ge(sem["weights_loaded"], 64)
            pool.tensor_scalar(wqkv_hi[:], raw_wqkv[:], 1.0, None, ALU.mult).then_inc(sem["w_hi"], 1)
            pool.tensor_scalar(wo_hi[:], raw_wo[:], 1.0, None, ALU.mult).then_inc(sem["w_hi"], 1)
            pool.wait_ge(sem["w_hi"], 2)
            pool.tensor_tensor(wqkv_lo[:], raw_wqkv[:], f32(wqkv_hi[:]), ALU.subtract).then_inc(sem["w_split"], 1)
            pool.tensor_tensor(wo_lo[:], raw_wo[:], f32(wo_hi[:]), ALU.subtract).then_inc(sem["w_split"], 1)

            def s_qkv(seq, unit):
                p = seq.odd
                pool.wait_ge(x_loaded[p], loaded_value(seq))
                wait(pool, sem["s_qkv_full"], seq.back(2))
                pool.tensor_tensor(xT_hi[p][:], xT_in[p][:], in_zero[:], ALU.add).then_inc(sem["xT_hi_set"], 1)
                wait(pool, sem["xT_hi_set"], seq)
                pool.tensor_tensor(xT_lo[p][:], xT_in[p][:], f32(xT_hi[p][:]), ALU.subtract).then_inc(sem["xT_split"], 1)
                wait(pool, sem["s_res_read"], seq.back(2))
                pool.tensor_tensor(x_bias[p][:], x_in[p][:], b_o[:], ALU.add).then_inc(sem["x_biased"], 1)

            def s_main(seq, unit):
                n = prob_ring.slot("s_main", unit, seq)
                wait(pool, sem["s_prob_hi"], seq, 2, unit + 1)
                pool.tensor_tensor(prob_lo[:, n, :], prob[:, n, :], f32(prob_hi[:, n, :]), ALU.subtract).then_inc(sem["s_prob_lo"], 1)

            def c_main(seq, unit):
                n = prob_ring.slot("c_main", unit, seq)
                wait(pool, sem["c_prob_hi"], seq, 4, unit + 1)
                pool.tensor_tensor(prob_lo[:, n, :], prob[:, n, :], f32(prob_hi[:, n, :]), ALU.subtract).then_inc(sem["c_prob_lo"], 1)

            def c_turn(seq, unit):
                p = seq.odd
                pool.wait_ge(ctx_loaded[p], loaded_value(seq))
                wait(pool, sem["ctx_k_set"], seq.back(1))
                pool.tensor_tensor(k_split[:], ctxT_in[p][:], in_zero[0:96], ALU.add).then_inc(sem["ctx_k_hi"], 1)
                wait(pool, sem["ctx_k_hi"], seq)
                pool.tensor_tensor(k_split[64:96], ctxT_in[p][64:96], f32(k_split[64:96]), ALU.subtract).then_inc(sem["ctx_k_lo"], 1)
                wait(pool, sem["ctx_k_lo"], seq)
                wait(pool, sem["c_main_full"], seq.back(2), 4)
                for a in range(2):
                    ins = pool.tensor_tensor(
                        k_c[p][0:96, a], f32(k_split[:, a, :]).unsqueeze(1).broadcast_to([96, 4, S]),
                        blk_c[0:96].unsqueeze(2).broadcast_to([96, 4, S]), ALU.mult)
                ins.then_inc(sem["ctx_k_set"], 1)
                wait(pool, sem["c_summed"], seq.back(2), 4)
                place = v_c[p][:].rearrange("p a (j s) -> p a j s", j=4)
                src = ctx_in[p][:].rearrange("p (a j d) -> p a j d", a=2, j=4)
                pool.tensor_tensor(place[:, :, :, 0:XD], src, in_zero[:, 0, 0:64].rearrange("p (a j d) -> p a j d", a=2, j=4),
                                   ALU.add).then_inc(sem["ctx_v_hi"], 1)
                wait(pool, sem["ctx_v_hi"], seq)
                pool.tensor_tensor(place[:, :, :, XD + 1:2 * XD + 1], src, f32(place[:, :, :, 0:XD]), ALU.subtract)\
                    .then_inc(sem["ctx_v_set"], 1)

            pool.wait_ge(sem["in_zero"], 1)
            pool.wait_ge(sem["tables"], 3)
            run(pool, dict(s_qkv=s_qkv, s_main=s_main, c_main=c_main, c_turn=c_turn))
            pool.wait_ge(raw_loaded[0], 32)
            pool.tensor_scalar(gu_hi0[:], raw_gu0[:], 1.0, None, ALU.mult).then_inc(sem["net0_hi"], 1)
            pool.wait_ge(sem["net0_hi"], 1)
            pool.tensor_tensor(gu_lo0[:], raw_gu0[:], f32(gu_hi0[:]), ALU.subtract).then_inc(gu_split, 1)
            pool.tensor_scalar(down_hi0[:], raw_down0[:], 1.0, None, ALU.mult).then_inc(sem["net0_hi"], 1)
            pool.wait_ge(sem["net0_hi"], 2)
            pool.tensor_tensor(down_lo0[:], raw_down0[:], f32(down_hi0[:]), ALU.subtract).then_inc(down_split, 1)

        @block.scalar
        def _(act):
            def s_qkv(seq, unit):
                p = seq.odd
                wait(act, sem["s_qkv_read"], seq)
                wait(act, sem["s_k_full"], seq.back(1))
                wait(act, sem["s_summed"], seq.back(2), 2)
                q = qkv[:, 0:D].rearrange("p (n c) -> p n c", c=32)
                act.copy(rows_s[:, 0:8, 0:32], q)
                act.copy(rows_s[:, 0:8, 64:96], q)
                act.copy(rows_s[:, 8, 0:64].rearrange("p (r d) -> p r d", d=HD), qkv[:, D:D + HD].unsqueeze(1).broadcast_to([P, 4, HD]))
                act.copy(v_s[p][:, :, 0:HD], qkv[:, D + HD:QKV].unsqueeze(1).broadcast_to([P, 2, HD])).then_inc(sem["s_rows_hi"], 1)

            def s_turn(seq, unit):
                wait(act, sem["s_main_full"], seq.back(2), 2)
                for u in range(2):
                    n = misc_ring.slot("s_turn", 0, seq, u)
                    wait(act, sem["s_q_full"], seq, 2, u + 1)
                    act.copy(q_s[seq.odd][0:96, 4 * u:4 * u + 4, :], misc[0:96, n, :].rearrange("p (n t) -> p n t", n=4))\
                        .then_inc(sem["s_q_read"], 1)

            def exp_unit(stage, unit, seq, per, scale, full, exped, hi, lo):
                n, m = score_ring.slot(stage, unit, seq), prob_ring.slot(stage, unit, seq)
                wait(act, sem[full], seq, per, unit + 1)
                prob_ring.wait_free(act, sem, stage, unit, seq)
                act.activation(prob[:, m, :], scores[:, n, :], ACT.Exp, scale=scale).then_inc(sem[exped], 1)
                wait(act, sem[exped], seq, per, unit + 1)
                act.copy(prob_hi[:, m, :], prob[:, m, :]).then_inc(sem[hi], 1)

            def s_main(seq, unit):
                exp_unit("s_main", unit, seq, 2, SCALE_S, "s_main_full", "s_exp", "s_prob_hi", "s_prob_lo")

            def c_main(seq, unit):
                exp_unit("c_main", unit, seq, 4, SCALE_X, "c_main_full", "c_exp", "c_prob_hi", "c_prob_lo")

            def s_sum(seq, unit):
                n = sum_ring.slot("s_sum", unit, seq)
                wait(act, sem["s_summed"], seq, 2, unit + 1)
                wait(act, sem["s_out_full"], seq.back(1), 2, unit + 1)
                act.copy(sumT_s[:, unit, :], sums[:, n, :]).then_inc(sem["s_sum_read"], 1)

            def c_sum(seq, unit):
                if unit % 2 == 0:
                    return
                n = sum_ring.slot("c_sum", unit - 1, seq)
                wait(act, sem["c_summed"], seq, 4, unit + 1)
                wait(act, sem["c_out_full"], seq.back(1), 2, unit // 2 + 1)
                act.copy(sumT_c[:, unit // 2, :], sums[:, n, :]).then_inc(sem["c_sum_read"], 1)

            def s_proj(seq, unit):
                n = misc_ring.slot("s_proj", 0, seq)
                wait(act, sem["s_ctx_full"], seq)
                wait(act, sem["s_res_full"], seq.back(1))
                act.copy(ctxT_hi[:], misc[:, n, 0:2 * S].rearrange("p (k t) -> p k t", k=2)).then_inc(sem["s_ctx_hi"], 1)

            def rsqrt_start(seq, k):
                wait(act, sem[f"{k}_mv"], seq)
                wait(act, sem[f"{k}_newton"], seq.back(1), 4, 4)
                act.activation(norm[k]["ln"][:], norm[k]["mv"][:, 1:2], ACT.Ln, bias=eps[:]).then_inc(sem[f"{k}_ln"], 1)
                wait(act, sem[f"{k}_ln"], seq)
                act.activation(norm[k]["r"][:], norm[k]["ln"][:], ACT.Exp, scale=-0.5).then_inc(sem[f"{k}_rsqrt0"], 1)

            def s_ln(seq, unit):
                rsqrt_start(seq, "s")

            def c_ln(seq, unit):
                rsqrt_start(seq, "c")

            def c_turn(seq, unit):
                wait(act, sem["x1_set"], seq)
                wait(act, sem["c_q_full"], seq.back(1), 2)
                for part in (0, 2):
                    for a in range(2):
                        ins = act.copy(
                            rows_c[:, 4 * a:4 * a + 4, 32 * part:32 * part + 32].rearrange("p g (j d) -> p g j d", j=4),
                            x1[seq.odd][:, P * a:P * a + P].rearrange("p (j g d) -> p g j d", j=4, g=4))
                ins.then_inc(sem["c_rows_hi"], 1)
                wait(act, sem["c_main_full"], seq.back(2), 4)
                for u in range(2):
                    n = misc_ring.slot("c_turn", 0, seq, u)
                    wait(act, sem["c_q_full"], seq, 2, u + 1)
                    act.copy(q_c[seq.odd][0:96, 4 * u:4 * u + 4, :], misc[0:96, n, :].rearrange("p (n t) -> p n t", n=4))\
                        .then_inc(sem["c_q_read"], 1)

            act.preload_act_table_set("natural_log_exp_and_others")
            act.wait_ge(sem["tables"], 3)
            run(act, dict(s_qkv=s_qkv, s_turn=s_turn, s_main=s_main, c_main=c_main, s_sum=s_sum, c_sum=c_sum,
                          s_proj=s_proj, s_ln=s_ln, c_ln=c_ln, c_turn=c_turn))

        @block.vector
        def _(dve):
            dve.memset(in_zero[:], 0.0).then_inc(sem["in_zero"], 1)
            dve.memset(max_s[:], 0.0)
            for p in range(2):
                dve.memset(f32(v_s[p][:]), 0.0)
                dve.memset(f32(v_c[p][:]), 0.0)
            dve.memset(eps[:], EPS).then_inc(sem["tables"], 1)
            dve.wait_ge(sem["tables"], 1)
            for p in range(2):
                dve.memset(f32(v_s[p][:, :, HD:HD + 1]), 1.0)
                ins = dve.memset(f32(v_c[p][:].rearrange("p a (j s) -> p a j s", j=4)[:, :, :, XD:XD + 1]), 1.0)
            ins.then_inc(sem["tables"], 1)
            dve.wait_ge(sem["consts_loaded"], 16)
            dve.tensor_copy(ident[:], cst[:, 0:P])
            dve.tensor_copy(ident_r[:], cst[:, 0:P])
            dve.tensor_copy(ident_b[:], cst[:, 0:P])
            dve.tensor_copy(mask_qk[:], cst[:, P:2 * P].unsqueeze(1).broadcast_to([P, 4, P]))
            dve.tensor_copy(mask_kq[:], cst[:, 2 * P:3 * P].unsqueeze(1).broadcast_to([P, 4, P]))
            for p in range(2):
                dve.tensor_copy(k_s[p][96:128], blk_s[96:128].unsqueeze(2).broadcast_to([32, 2, S]))
                for a in range(2):
                    ins = dve.tensor_copy(k_c[p][96:128, a], blk_c[96:128].unsqueeze(2).broadcast_to([32, 4, S]))
            ins.then_inc(sem["tables"], 1)

            def s_qkv(seq, unit):
                p, n = seq.odd, misc_ring.slot("s_qkv", 0, seq)
                wait(dve, sem["s_qkv_full"], seq)
                wait(dve, sem["s_rows_lo"], seq.back(1))
                dve.tensor_tensor(qkv[:], misc[:, n, 0:QKV], b_qkv[:], ALU.add).then_inc(sem["s_qkv_read"], 1)
                wait(dve, sem["s_rows_hi"], seq)
                dve.tensor_tensor(rows_s[:, 0:8, 32:64], qkv[:, 0:D].rearrange("p (n c) -> p n c", c=32),
                                  f32(rows_s[:, 0:8, 0:32]), ALU.subtract)
                dve.tensor_tensor(rows_s[:, 8, 64:96].rearrange("p (r d) -> p r d", d=HD),
                                  qkv[:, D:D + HD].unsqueeze(1).broadcast_to([P, 2, HD]),
                                  f32(rows_s[:, 8, 0:32]).rearrange("p (r d) -> p r d", d=HD), ALU.subtract)
                dve.tensor_tensor(v_s[p][:, :, HD + 1:2 * HD + 1], qkv[:, D + HD:QKV].unsqueeze(1).broadcast_to([P, 2, HD]),
                                  f32(v_s[p][:, :, 0:HD]), ALU.subtract).then_inc(sem["s_rows_lo"], 1)

            def s_turn(seq, unit):
                n = misc_ring.slot("s_turn", 0, seq, 2)
                wait(dve, sem["s_k_full"], seq)
                wait(dve, sem["s_main_full"], seq.back(2), 2)
                dve.tensor_tensor(k_s[seq.odd][0:96], misc[0:96, n, 0:S].unsqueeze(1).broadcast_to([96, 2, S]),
                                  blk_s[0:96].unsqueeze(2).broadcast_to([96, 2, S]), ALU.mult).then_inc(sem["s_k_read"], 1)

            def row_max(stage, unit, seq, per, full, read, out_, shifted):
                n = score_ring.slot(stage, unit, seq)
                wait(dve, sem[full], seq, per, unit + 1)
                if unit == 0:
                    wait(dve, sem[shifted], seq.back(1))
                dve.tensor_reduce(out_[:, 8 * unit:8 * unit + 8], scores[:, n, :].rearrange("p (h k) -> p h k", k=S),
                                  AX.X, ALU.max).then_inc(sem[read], 1)

            def s_max(seq, unit):
                row_max("s_max", unit, seq, 2, "s_max_full", "s_max_read", max_s, "s_shift_full")

            def c_max(seq, unit):
                row_max("c_max", unit, seq, 4, "c_max_full", "c_max_read", max_c, "c_shift_full")

            def shift_rows(stage, seq, q, neg, full, read):
                n = misc_ring.slot(stage, 0, seq)
                wait(dve, sem[full], seq)
                dve.tensor_tensor(q[seq.odd][96:128], misc[0:32, n, 0:S].unsqueeze(1).broadcast_to([32, 8, S]),
                                  neg.unsqueeze(2).broadcast_to([32, 8, S]), ALU.mult).then_inc(sem[read], 1)

            def s_shift(seq, unit):
                shift_rows("s_shift", seq, q_s, neg_s, "s_shift_full", "s_shift_read")

            def c_shift(seq, unit):
                shift_rows("c_shift", seq, q_c, neg_c, "c_shift_full", "c_shift_read")

            def s_out(seq, b):
                n = misc_ring.slot("s_out", b, seq)
                part = misc[:, n, :].rearrange("p (i h s) -> p i h s", i=4, h=2)
                wait(dve, sem["s_out_full"], seq, 2, b + 1)
                wait(dve, sem["s_ctx"], seq.back(1), 2, b + 1)
                dve.reciprocal(rden_s[:, b, :].rearrange("p (h i) -> p i h", h=2), part[:, :, :, HD:HD + 1].squeeze(3)).then_inc(sem["s_rden"], 1)
                both_parts = part[:, :, :, 0:2 * (HD + 1)].rearrange("p i h (two d) -> p i h d two", two=2)[:, :, :, 0:HD, :]
                dve.tensor_reduce(raw_s[:, b].rearrange("p (h i) d -> p i h d", h=2), both_parts, AX.X, ALU.add)\
                    .then_inc(sem["s_out_read"], 1)
                wait(dve, sem["s_rden"], seq, 2, b + 1)
                wait(dve, sem["s_out_read"], seq, 2, b + 1)
                wait(dve, sem["s_ctx_full"], seq.back(2))
                dve.tensor_tensor(ctx_s[seq.odd][:].rearrange("p (n b d) -> p n b d", b=2, d=HD)[:, :, b, :], raw_s[:, b],
                                  rden_s[:, b, :].unsqueeze(2).broadcast_to([P, 8, HD]), ALU.mult).then_inc(sem["s_ctx"], 1)

            def s_proj(seq, unit):
                n = misc_ring.slot("s_proj", 0, seq)
                wait(dve, sem["s_ctx_hi"], seq)
                dve.tensor_tensor(ctxT_lo[:], misc[:, n, 0:2 * S].rearrange("p (k t) -> p k t", k=2), f32(ctxT_hi[:]),
                                  ALU.subtract).then_inc(sem["s_ctx_read"], 1)

            def s_res(seq, unit):
                n = misc_ring.slot("s_res", 0, seq)
                wait(dve, sem["s_res_full"], seq)
                wait(dve, sem["x_biased"], seq)
                wait(dve, sem["x1_set"], seq.back(2))
                dve.tensor_tensor(pre1[seq.odd][:], misc[:, n, 0:D], x_bias[seq.odd][:], ALU.add).then_inc(sem["s_res_read"], 1)
                wait(dve, sem["s_res_read"], seq)
                stats("s", seq, pre1[seq.odd])

            def stats(k, seq, pre):
                wait(dve, sem[f"{k}_mv"], seq.back(1))
                dve.bn_stats(norm[k]["stats"][:], pre[:]).then_inc(sem[f"{k}_stats"], 1)
                wait(dve, sem[f"{k}_newton"], seq.back(1), 4)
                wait(dve, sem[f"{k}_ln"], seq.back(1))
                wait(dve, sem["x1_set" if k == "s" else "x2_set"], seq.back(1))
                wait(dve, sem[f"{k}_stats"], seq)
                dve.memset(norm[k]["t"][:, 0:1], 0.0)
                dve.bn_aggr(norm[k]["mv"][:], norm[k]["stats"][:]).then_inc(sem[f"{k}_mv"], 1)

            def newton(k, seq):
                r, t, mv, s = norm[k]["r"], norm[k]["t"], norm[k]["mv"], sem[f"{k}_newton"]
                wait(dve, sem[f"{k}_rsqrt0"], seq)
                wait(dve, sem["x1_set" if k == "s" else "x2_set"], seq.back(1))
                dve.tensor_tensor(t[:, 0:1], r[:], r[:], ALU.mult).then_inc(s, 1)
                wait(dve, s, seq, 4, 1)
                dve.scalar_tensor_tensor(t[:, 1:2], mv[:, 1:2], EPS, t[:, 0:1], ALU.add, ALU.mult).then_inc(s, 1)
                wait(dve, s, seq, 4, 2)
                dve.tensor_scalar(t[:, 0:1], t[:, 1:2], -0.5, 1.5, ALU.mult, ALU.add).then_inc(s, 1)
                wait(dve, s, seq, 4, 3)
                dve.tensor_tensor(t[:, 2:3], t[:, 0:1], r[:], ALU.mult).then_inc(s, 1)
                wait(dve, s, seq, 4, 4)

            def s_ln(seq, unit):
                newton("s", seq)
                wait(dve, sem["c_rows_lo"], seq.back(2))
                wait(dve, sem["c_res"], seq.back(2))
                dve.tensor_scalar(x1[seq.odd][:], pre1[seq.odd][:], norm["s"]["mv"][:, 0:1], norm["s"]["t"][:, 2:3],
                                  ALU.subtract, ALU.mult).then_inc(sem["x1_set"], 1)

            def c_turn(seq, unit):
                wait(dve, sem["c_rows_hi"], seq)
                for a in range(2):
                    ins = dve.tensor_tensor(
                        rows_c[:, 4 * a:4 * a + 4, 32:64].rearrange("p g (j d) -> p g j d", j=4),
                        x1[seq.odd][:, P * a:P * a + P].rearrange("p (j g d) -> p g j d", j=4, g=4),
                        f32(rows_c[:, 4 * a:4 * a + 4, 0:32]).rearrange("p g (j d) -> p g j d", j=4), ALU.subtract)
                ins.then_inc(sem["c_rows_lo"], 1)

            def c_out(seq, a):
                n = misc_ring.slot("c_out", a, seq)
                part = misc[:, n, :].rearrange("p (g j s) -> p g j s", g=4, j=4)
                wait(dve, sem["c_out_full"], seq, 2, a + 1)
                wait(dve, sem["c_ctx"], seq.back(1), 2, a + 1)
                dve.reciprocal(rden_c[:, a, :].rearrange("p (g j) -> p g j", g=4), part[:, :, :, XD:XD + 1].squeeze(3)).then_inc(sem["c_rden"], 1)
                both_parts = part[:, :, :, 0:2 * (XD + 1)].rearrange("p g j (two d) -> p g j d two", two=2)[:, :, :, 0:XD, :]
                dve.tensor_reduce(raw_c[:, a], both_parts, AX.X, ALU.add).then_inc(sem["c_out_read"], 1)
                wait(dve, sem["c_rden"], seq, 2, a + 1)
                wait(dve, sem["c_out_read"], seq, 2, a + 1)
                wait(dve, sem["c_res"], seq.back(1))
                dve.tensor_tensor(ctx_c[:, P * a:P * a + P].rearrange("p (j g d) -> p g j d", j=4, g=4), raw_c[:, a],
                                  rden_c[:, a, :].rearrange("p (g j) -> p g j", g=4).unsqueeze(3).broadcast_to([P, 4, 4, XD]),
                                  ALU.mult).then_inc(sem["c_ctx"], 1)
                if a == 1:
                    wait(dve, sem["c_ctx"], seq, 2)
                    wait(dve, sem["x1_set"], seq)
                    wait(dve, sem["x2_set"], seq.back(2))
                    dve.tensor_tensor(pre2[seq.odd][:], ctx_c[:], x1[seq.odd][:], ALU.add).then_inc(sem["c_res"], 1)
                    wait(dve, sem["c_res"], seq)
                    stats("c", seq, pre2[seq.odd])

            def c_ln(seq, unit):
                newton("c", seq)
                dve.tensor_scalar(stream[:, bass.ds(seq.at(1), 1), :].squeeze(1), pre2[seq.odd][:], norm["c"]["mv"][:, 0:1],
                                  norm["c"]["t"][:, 2:3], ALU.subtract, ALU.mult).then_inc(sem["x2_set"], 1)

            dve.wait_ge(sem["tables"], 3)
            run(dve, dict(s_qkv=s_qkv, s_turn=s_turn, s_max=s_max, c_max=c_max, s_shift=s_shift, c_shift=c_shift,
                          s_out=s_out, s_proj=s_proj, s_res=s_res, s_ln=s_ln, c_turn=c_turn, c_out=c_out, c_ln=c_ln))

        @block.tensor
        def _(pe):
            def three(out_, a_hi, a_lo, w_hi, w_lo, first, last):
                pe.matmul(out_, a_hi, w_hi, start=first, stop=False)
                pe.matmul(out_, a_hi, w_lo, start=False, stop=False)
                return pe.matmul(out_, a_lo, w_hi, start=False, stop=last)

            def s_qkv(seq, unit):
                p, n = seq.odd, misc_ring.slot("s_qkv", 0, seq)
                wait(pe, sem["xT_split"], seq)
                misc_ring.wait_free(pe, sem, "s_qkv", 0, seq)
                for k in range(2):
                    mm = three(misc[:, n, 0:QKV], xT_hi[p][:, k, :], xT_lo[p][:, k, :], wqkv_hi[:, k, :], wqkv_lo[:, k, :],
                               k == 0, k == 1)
                mm.then_inc(sem["s_qkv_full"], 1)

            def s_turn(seq, unit):
                wait(pe, sem["s_rows_lo"], seq)
                for u in range(2):
                    n = misc_ring.slot("s_turn", 0, seq, u)
                    misc_ring.wait_free(pe, sem, "s_turn", 0, seq, u)
                    for j in range(4):
                        mm = pe.transpose(misc[0:96, n, S * j:S * j + S].bitcast(F32R), rows_s[:, 4 * u + j, :], ident_r[:])
                    mm.then_inc(sem["s_q_full"], 1)
                n = misc_ring.slot("s_turn", 0, seq, 2)
                misc_ring.wait_free(pe, sem, "s_turn", 0, seq, 2)
                pe.transpose(misc[0:96, n, 0:S].bitcast(F32R), rows_s[:, 8, :], ident_r[:]).then_inc(sem["s_k_full"], 1)

            def s_max(seq, unit):
                p, n = seq.odd, score_ring.slot("s_max", unit, seq)
                wait(pe, sem["s_q_read"], seq, 2, unit + 1)
                wait(pe, sem["s_k_read"], seq)
                score_ring.wait_free(pe, sem, "s_max", unit, seq)
                for bank in range(2):
                    at = 512 * bank
                    pe.matmul(scores[:, n, at:at + 512], ident_b[:], mask_qk[:], start=True, stop=False)
                    for v in range(2):
                        mm = pe.matmul(scores[:, n, at + 256 * v:at + 256 * v + 256], q_s[p][0:96, 4 * unit + 2 * bank + v, :],
                                       k_s[p][0:96], start=False, stop=(v == 1))
                mm.then_inc(sem["s_max_full"], 1)

            def shift(stage, seq, maxima, read, per, full):
                n = misc_ring.slot(stage, 0, seq)
                wait(pe, sem[read], seq, per)
                misc_ring.wait_free(pe, sem, stage, 0, seq)
                pe.transpose(misc[0:32, n, 0:S], maxima[:], ident[:]).then_inc(sem[full], 1)

            def s_shift(seq, unit):
                shift("s_shift", seq, max_s, "s_max_read", 2, "s_shift_full")

            def c_shift(seq, unit):
                shift("c_shift", seq, max_c, "c_max_read", 4, "c_shift_full")

            def s_main(seq, b):
                p, n = seq.odd, score_ring.slot("s_main", b, seq)
                wait(pe, sem["s_shift_read"], seq)
                score_ring.wait_free(pe, sem, "s_main", b, seq)
                for bank in range(2):
                    at = 512 * bank
                    pe.matmul(scores[:, n, at:at + 512], ident_b[:], mask_kq[:], start=True, stop=False)
                    mm = pe.matmul(scores[:, n, at:at + 512], k_s[p][:, b, :], q_s[p][:, 4 * bank:4 * bank + 4, :],
                                   start=False, stop=True)
                mm.then_inc(sem["s_main_full"], 1)

            def s_sum(seq, b):
                p, n, m = seq.odd, sum_ring.slot("s_sum", b, seq), prob_ring.slot("s_main", b, seq)
                wait(pe, sem["s_prob_lo"], seq, 2, b + 1)
                sum_ring.wait_free(pe, sem, "s_sum", b, seq)
                v = v_s[p][:].rearrange("p h s -> p (h s)")
                for h in range(2):
                    w = v[:, P * h:P * h + P]
                    pe.matmul(sums[:, n, :], w, prob_hi[:, m, 512 * h:512 * h + 512], start=(h == 0), stop=False)
                    mm = pe.matmul(sums[:, n, :], w, prob_lo[:, m, 512 * h:512 * h + 512], start=False, stop=(h == 1))
                mm.then_inc(sem["s_summed"], 1)

            def turn_sums(stage, seq, unit, source, read, full):
                n = misc_ring.slot(stage, unit, seq)
                wait(pe, sem[read], seq, 2, unit + 1)
                misc_ring.wait_free(pe, sem, stage, unit, seq)
                for j in range(4):
                    mm = pe.transpose(misc[:, n, S * j:S * j + S], source[:, unit, S * j:S * j + S], ident[:])
                mm.then_inc(sem[full], 1)

            def s_out(seq, b):
                turn_sums("s_out", seq, b, sumT_s, "s_sum_read", "s_out_full")

            def c_out(seq, a):
                turn_sums("c_out", seq, a, sumT_c, "c_sum_read", "c_out_full")

            def s_proj(seq, unit):
                n = misc_ring.slot("s_proj", 0, seq)
                wait(pe, sem["s_ctx"], seq, 2)
                misc_ring.wait_free(pe, sem, "s_proj", 0, seq)
                for k in range(2):
                    mm = pe.transpose(misc[:, n, S * k:S * k + S], ctx_s[seq.odd][:, P * k:P * k + P], ident[:])
                mm.then_inc(sem["s_ctx_full"], 1)

            def s_res(seq, unit):
                n = misc_ring.slot("s_res", 0, seq)
                wait(pe, sem["s_ctx_read"], seq)
                misc_ring.wait_free(pe, sem, "s_res", 0, seq)
                for k in range(2):
                    mm = three(misc[:, n, 0:D], ctxT_hi[:, k, :], ctxT_lo[:, k, :], wo_hi[:, k, :], wo_lo[:, k, :],
                               k == 0, k == 1)
                mm.then_inc(sem["s_res_full"], 1)

            def c_turn(seq, unit):
                wait(pe, sem["c_rows_lo"], seq)
                for u in range(2):
                    n = misc_ring.slot("c_turn", 0, seq, u)
                    misc_ring.wait_free(pe, sem, "c_turn", 0, seq, u)
                    for j in range(4):
                        mm = pe.transpose(misc[0:96, n, S * j:S * j + S].bitcast(F32R), rows_c[:, 4 * u + j, :], ident_r[:])
                    mm.then_inc(sem["c_q_full"], 1)

            def c_max(seq, unit):
                p, n = seq.odd, score_ring.slot("c_max", unit, seq)
                wait(pe, sem["c_q_read"], seq, 2, unit // 2 + 1)
                wait(pe, sem["ctx_k_set"], seq)
                score_ring.wait_free(pe, sem, "c_max", unit, seq)
                for v in range(2):
                    mm = pe.matmul(scores[:, n, 512 * v:512 * v + 512], q_c[p][0:96, 2 * unit + v, :],
                                   k_c[p][0:96, unit // 2], start=True, stop=True)
                mm.then_inc(sem["c_max_full"], 1)

            def c_main(seq, unit):
                p, n, a = seq.odd, score_ring.slot("c_main", unit, seq), unit // 2
                wait(pe, sem["c_shift_read"], seq)
                score_ring.wait_free(pe, sem, "c_main", unit, seq)
                for v in range(2):
                    mm = pe.matmul(scores[:, n, 512 * v:512 * v + 512], k_c[p][:, a, 2 * (unit % 2) + v, :],
                                   q_c[p][:, 4 * a:4 * a + 4, :], start=True, stop=True)
                mm.then_inc(sem["c_main_full"], 1)

            def c_sum(seq, unit):
                p, a, m = seq.odd, unit // 2, prob_ring.slot("c_main", unit, seq)
                n = sum_ring.slot("c_sum", 2 * a, seq)
                wait(pe, sem["c_prob_lo"], seq, 4, unit + 1)
                wait(pe, sem["ctx_v_set"], seq)
                if unit % 2 == 0:
                    sum_ring.wait_free(pe, sem, "c_sum", unit, seq)
                for v in range(2):
                    j = 2 * (unit % 2) + v
                    w = v_c[p][:, a, P * j:P * j + P]
                    pe.matmul(sums[:, n, :], w, prob_hi[:, m, 512 * v:512 * v + 512], start=(j == 0), stop=False)
                    mm = pe.matmul(sums[:, n, :], w, prob_lo[:, m, 512 * v:512 * v + 512], start=False, stop=(j == 3))
                mm.then_inc(sem["c_summed"], 1)

            pe.wait_ge(sem["tables"], 3)
            pe.wait_ge(sem["w_split"], 2)
            run(pe, dict(s_qkv=s_qkv, s_turn=s_turn, s_max=s_max, s_shift=s_shift, s_main=s_main, s_sum=s_sum, s_out=s_out,
                         s_proj=s_proj, s_res=s_res, c_turn=c_turn, c_max=c_max, c_shift=c_shift, c_main=c_main,
                         c_sum=c_sum, c_out=c_out))


def experts(nc, gate_w, exp_gu, exp_down, consts, stream, ident, eps, weights0, out):
    raw_gu0, raw_down0, gu_hi0, gu_lo0, down_hi0, down_lo0, raw_loaded, gu_split, down_split = weights0
    with ExitStack() as scope:
        def sb(name, shape, dt=F32):
            return scope.enter_context(nc.sbuf_tensor(name, shape, dt))

        inner = scope.enter_context(nc.psum_tensor("inner", [P, 4, 512], F32))
        y = scope.enter_context(nc.psum_tensor("y", [P, 2, 2, 512], F32))

        raw_gu = [raw_gu0, sb("raw_gu1", [P, 2, 2 * INNER])]
        raw_down = [raw_down0, sb("raw_down1", [P, INNER // P, D])]
        gu_hi = [gu_hi0, sb("gu_hi1", [P, 2, 2 * INNER], F32R)]
        gu_lo = [gu_lo0, sb("gu_lo1", [P, 2, 2 * INNER], F32R)]
        down_hi = [down_hi0, sb("down_hi1", [P, INNER // P, D], F32R)]
        down_lo = [down_lo0, sb("down_lo1", [P, INNER // P, D], F32R)]
        sT_hi, sT_lo = sb("sT_hi", [P, 2, B * S], F32R), sb("sT_lo", [P, 2, B * S], F32R)
        raw_gate = sb("raw_gate", [P, 2, EXPERTS])
        gate_hi, gate_lo = sb("gate_hi", [P, 2, EXPERTS], F32R), sb("gate_lo", [P, 2, EXPERTS], F32R)
        descending = sb("descending", [P, EXPERTS])
        logitsT = sb("logitsT", [EXPERTS, B * S])
        gates = {n: sb(f"gate_{n}", [P, B, EXPERTS]) for n in "shifted e p order first rest order2 second both w".split()}
        stat = {n: sb(f"stat_{n}", [P, B]) for n in "max sum rsum p1 o1 p2 o2 wsum rwsum".split()}
        share = sb("share", [P, B, NETS])
        silu = sb("silu", [P, 2, GROUP])
        hidden = [sb(f"hidden{p}", [P, 4, GROUP]) for p in range(2)]
        hidden_hi = [sb(f"hidden_hi{p}", [P, 4, GROUP], F32R) for p in range(2)]
        hidden_lo = [sb(f"hidden_lo{p}", [P, 4, GROUP], F32R) for p in range(2)]
        zeros = sb("zeros", [P, 1024])
        stats, mv = sb("stats", [P, B, 6]), sb("mv", [P, B, 2])
        lnv, r0, t0, t1, rstd = (sb(n, [P, B]) for n in ("lnv", "r0", "t0", "t1", "rstd"))

        names = """gate_loaded gate_hi_set gate_split sT_full sT_hi_set sT_set logits_full logits_read gates_full step exps
            shares inner_full silu_set hidden_set hidden_hi_set hidden_lo_set y_full y_read w_hi aggr ln_set rsqrt0 newton
            normed stored""".split()
        sem = {n: scope.enter_context(nc.semaphore("b_" + n)) for n in names}

        def f32(ap):
            return ap.bitcast(F32)

        def run(eng, net):
            net(Seq(0))
            with eng.Fori(0, EXPERTS // 2) as i:
                net(Seq(1, i))
                net(Seq(2, i))

        def upto(eng, s, seq, per, plus):
            if seq.i is not None or per * seq.off + plus > 0:
                eng.wait_ge(s, seq.at(per, plus))

        block = scope.enter_context(nc.Block())

        @block.sync
        def _(sp):
            sp.dma_start(raw_gate[:], gate_w.rearrange("(k p) n -> p k n", p=P)).then_inc(sem["gate_loaded"], 16)
            sp.dma_start(descending[:], consts[:, 3 * P + 22:3 * P + 22 + EXPERTS]).then_inc(sem["gate_loaded"], 16)

            def load(seq):
                sp.wait_ge(gu_split, seq.at(1, -1))
                sp.wait_ge(down_split, seq.at(1, -1))
                load_net(sp, seq.at(1, -1), raw_gu[seq.odd], raw_down[seq.odd], raw_loaded[seq.odd], exp_gu, exp_down)

            load_net(sp, 0, raw_gu[1], raw_down[1], raw_loaded[1], exp_gu, exp_down)
            load(Seq(2))
            with sp.Fori(0, (EXPERTS - 2) // 2) as i:
                load(Seq(3, i))
                load(Seq(4, i))
            tiles = out.rearrange("(t p) d -> p t d", p=P)
            for g in range(GROUPS):
                sp.wait_ge(sem["normed"], g + 1)
                sp.dma_start(tiles[:, TILES * g:TILES * g + TILES, :], stream[:, TILES * g:TILES * g + TILES, :]).then_inc(sem["stored"], 16)
            sp.wait_ge(sem["stored"], 16 * GROUPS)

        @block.gpsimd
        def _(pool):
            pool.wait_ge(sem["gate_loaded"], 32)
            pool.tensor_scalar(gate_hi[:], raw_gate[:], 1.0, None, ALU.mult).then_inc(sem["gate_hi_set"], 1)
            pool.wait_ge(sem["gate_hi_set"], 1)
            pool.tensor_tensor(gate_lo[:], raw_gate[:], f32(gate_hi[:]), ALU.subtract).then_inc(sem["gate_split"], 1)

            def split_next(seq, k):
                q = 1 - seq.odd
                if k == 0:
                    upto(pool, sem["y_full"], seq, 8, 0)
                    nxt = 32 * ((seq.off + 1) // 2 + 1)
                    pool.wait_ge(raw_loaded[q], nxt if seq.i is None else seq.i * 32 + nxt)
                hi, lo, raw = ((gu_hi[q][:, k, :], gu_lo[q][:, k, :], raw_gu[q][:, k, :]) if k < 2 else
                               (down_hi[q][:], down_lo[q][:], raw_down[q][:]))
                pool.tensor_tensor(hi, raw, zeros[:, 0:1024] if k < 2 else zeros[:, 0:1024].rearrange("p (a b) -> p a b", b=D),
                                   ALU.add).then_inc(sem["w_hi"], 1)
                upto(pool, sem["w_hi"], seq, 3, k + 1)
                ins = pool.tensor_tensor(lo, raw, f32(hi), ALU.subtract)
                if k:
                    ins.then_inc(gu_split if k == 1 else down_split, 1)

            def net(seq, last=False):
                for g in range(GROUPS):
                    for c in range(4):
                        upto(pool, sem["hidden_hi_set"], seq, 16, 4 * g + c + 1)
                        upto(pool, sem["y_full"], seq, 8, 2 * g - 2)
                        pool.tensor_tensor(hidden_lo[g % 2][:, c], hidden[g % 2][:, c], f32(hidden_hi[g % 2][:, c]),
                                           ALU.subtract).then_inc(sem["hidden_lo_set"], 1)
                    if g < 3 and not last:
                        split_next(seq, g)

            net(Seq(0))
            with pool.Fori(0, EXPERTS // 2 - 1) as i:
                net(Seq(1, i))
                net(Seq(2, i))
            net(Seq(EXPERTS - 1))
            net(Seq(EXPERTS), last=True)

        @block.scalar
        def _(act):
            for g in range(GROUPS):
                act.wait_ge(sem["sT_full"], g + 1)
                act.copy(sT_hi[:, :, GROUP * g:GROUP * g + GROUP], y[:, g % 2]).then_inc(sem["sT_hi_set"], 1)
            act.wait_ge(sem["step"], 2)
            act.activation(gates["e"][:], gates["shifted"][:], ACT.Exp).then_inc(sem["exps"], 1)

            def net(seq):
                for g in range(GROUPS):
                    for c in range(4):
                        at = 4 * g + c
                        upto(act, sem["inner_full"], seq, 16, at + 1)
                        upto(act, sem["hidden_set"], seq, 16, at - 1)
                        act.activation(silu[:, c % 2, :], inner[:, 2 * (c % 2), :], ACT.Silu).then_inc(sem["silu_set"], 1)
                        if c:
                            high(seq, g, c - 1)
                    high(seq, g, 3)

            def high(seq, g, c):
                upto(act, sem["hidden_set"], seq, 16, 4 * g + c + 1)
                upto(act, sem["y_full"], seq, 8, 2 * g - 2)
                act.copy(hidden_hi[g % 2][:, c], hidden[g % 2][:, c]).then_inc(sem["hidden_hi_set"], 1)

            run(act, net)
            act.preload_act_table_set("natural_log_exp_and_others")
            for g in range(GROUPS):
                a, b = TILES * g, TILES * g + TILES
                act.wait_ge(sem["aggr"], g + 1)
                act.activation(lnv[:, a:b], mv[:, a:b, 1:2].squeeze(2), ACT.Ln, bias=eps[:]).then_inc(sem["ln_set"], 1)
                act.wait_ge(sem["ln_set"], g + 1)
                act.activation(r0[:, a:b], lnv[:, a:b], ACT.Exp, scale=-0.5).then_inc(sem["rsqrt0"], 1)

        @block.vector
        def _(dve):
            dve.memset(share[:, :, 0:1], 1.0)
            dve.memset(zeros[:], 0.0)
            for g in range(GROUPS):
                dve.wait_ge(sem["sT_hi_set"], g + 1)
                cols = slice(GROUP * g, GROUP * g + GROUP)
                dve.tensor_tensor(sT_lo[:, :, cols], y[:, g % 2], f32(sT_hi[:, :, cols]), ALU.subtract).then_inc(sem["sT_set"], 1)
                dve.wait_ge(sem["logits_full"], g + 1)
                dve.tensor_copy(logitsT[:, cols], inner[0:EXPERTS, g, :]).then_inc(sem["logits_read"], 1)

            done = [0]

            def then(ins):
                done[0] += 1
                ins.then_inc(sem["step"], 1)
                dve.wait_ge(sem["step"], done[0])

            def all8(t):
                return t[:].unsqueeze(2).broadcast_to([P, B, EXPERTS])

            order = descending[:].unsqueeze(1).broadcast_to([P, B, EXPERTS])
            logits = y[:, 0, 0, 0:B * EXPERTS].rearrange("p (t n) -> p t n", n=EXPERTS)
            dve.wait_ge(sem["gates_full"], 1)
            dve.wait_ge(sem["gate_loaded"], 32)
            then(dve.tensor_reduce(stat["max"][:], logits, AX.X, ALU.max))
            then(dve.tensor_tensor(gates["shifted"][:], logits, all8(stat["max"]), ALU.subtract))
            dve.wait_ge(sem["exps"], 1)
            then(dve.tensor_reduce(stat["sum"][:], gates["e"][:], AX.X, ALU.add))
            then(dve.reciprocal(stat["rsum"][:], stat["sum"][:]))
            then(dve.tensor_tensor(gates["p"][:], gates["e"][:], all8(stat["rsum"]), ALU.mult))
            then(dve.tensor_reduce(stat["p1"][:], gates["p"][:], AX.X, ALU.max))
            then(dve.tensor_tensor(gates["order"][:], gates["p"][:], all8(stat["p1"]), ALU.is_equal))
            then(dve.tensor_tensor(gates["order"][:], gates["order"][:], order, ALU.mult))
            then(dve.tensor_reduce(stat["o1"][:], gates["order"][:], AX.X, ALU.max))
            then(dve.tensor_tensor(gates["first"][:], gates["order"][:], all8(stat["o1"]), ALU.is_equal))
            then(dve.scalar_tensor_tensor(gates["rest"][:], gates["first"][:], -2.0, gates["p"][:], ALU.mult, ALU.add))
            then(dve.tensor_reduce(stat["p2"][:], gates["rest"][:], AX.X, ALU.max))
            then(dve.tensor_tensor(gates["order2"][:], gates["rest"][:], all8(stat["p2"]), ALU.is_equal))
            then(dve.tensor_tensor(gates["order2"][:], gates["order2"][:], order, ALU.mult))
            then(dve.tensor_reduce(stat["o2"][:], gates["order2"][:], AX.X, ALU.max))
            then(dve.tensor_tensor(gates["second"][:], gates["order2"][:], all8(stat["o2"]), ALU.is_equal))
            then(dve.tensor_tensor(gates["both"][:], gates["first"][:], gates["second"][:], ALU.add))
            then(dve.tensor_tensor(gates["w"][:], gates["p"][:], gates["both"][:], ALU.mult))
            then(dve.tensor_reduce(stat["wsum"][:], gates["w"][:], AX.X, ALU.add))
            then(dve.reciprocal(stat["rwsum"][:], stat["wsum"][:]))
            then(dve.tensor_tensor(share[:, :, 1:NETS], gates["w"][:], all8(stat["rwsum"]), ALU.mult))

            def add_outputs(seq, g):
                for bank in range(2):
                    upto(dve, sem["y_full"], seq, 8, 2 * g + bank + 1)
                    upto(dve, sem["y_read"], seq, 8, 2 * g)
                    for v in range(2):
                        t = TILES * g + 2 * bank + v
                        ins = dve.scalar_tensor_tensor(stream[:, t, :], y[:, g % 2, bank, D * v:D * v + D],
                                                       share[:, t, bass.ds(seq.at(1), 1)], stream[:, t, :], ALU.mult, ALU.add)
                    ins.then_inc(sem["y_read"], 1)

            def net(seq):
                for g in range(GROUPS):
                    for c in range(4):
                        at = 4 * g + c
                        upto(dve, sem["silu_set"], seq, 16, at + 1)
                        upto(dve, sem["hidden_lo_set"], seq, 16, at - 7)
                        dve.tensor_tensor(hidden[g % 2][:, c], silu[:, c % 2, :], inner[:, 2 * (c % 2) + 1, :], ALU.mult)\
                            .then_inc(sem["hidden_set"], 1)
                    if g:
                        add_outputs(seq, g - 1)
                    elif seq.off or seq.i is not None:
                        add_outputs(seq.back(1), GROUPS - 1)

            run(dve, net)
            chain = [0]

            def link(ins):
                chain[0] += 1
                ins.then_inc(sem["newton"], 1)
                dve.wait_ge(sem["newton"], chain[0])

            for g in range(GROUPS):
                if g == GROUPS - 1:
                    add_outputs(Seq(NETS - 1), GROUPS - 1)
                a, b = TILES * g, TILES * g + TILES
                dve.wait_ge(sem["y_read"], 8 * (NETS - 1) + 2 * g + 2)
                for t in range(a, b):
                    ins = dve.bn_stats(stats[:, t, :], stream[:, t, :])
                link(ins)
                for t in range(a, b):
                    ins = dve.bn_aggr(mv[:, t, :], stats[:, t, :])
                ins.then_inc(sem["aggr"], 1)
                dve.wait_ge(sem["rsqrt0"], g + 1)
                link(dve.tensor_tensor(t0[:, a:b], r0[:, a:b], r0[:, a:b], ALU.mult))
                link(dve.scalar_tensor_tensor(t1[:, a:b], mv[:, a:b, 1:2].squeeze(2), EPS, t0[:, a:b], ALU.add, ALU.mult))
                link(dve.tensor_scalar(t0[:, a:b], t1[:, a:b], -0.5, 1.5, ALU.mult, ALU.add))
                link(dve.tensor_tensor(rstd[:, a:b], t0[:, a:b], r0[:, a:b], ALU.mult))
                for t in range(a, b):
                    ins = dve.tensor_scalar(stream[:, t, :], stream[:, t, :], mv[:, t, 0:1], rstd[:, t:t + 1],
                                            ALU.subtract, ALU.mult)
                ins.then_inc(sem["normed"], 1)

        @block.tensor
        def _(pe):
            def turn_stream(g):
                if g >= 2:
                    pe.wait_ge(sem["sT_set"], g - 1)
                for k in range(2):
                    for t in range(TILES):
                        mm = pe.transpose(y[:, g % 2, k, P * t:P * t + P], stream[:, TILES * g + t, P * k:P * k + P], ident[:])
                mm.then_inc(sem["sT_full"], 1)

            turn_stream(0)
            pe.wait_ge(sem["gate_split"], 1)
            for g in range(GROUPS):
                if g + 1 < GROUPS:
                    turn_stream(g + 1)
                pe.wait_ge(sem["sT_set"], g + 1)
                cols = slice(GROUP * g, GROUP * g + GROUP)
                for k in range(2):
                    pe.matmul(inner[0:EXPERTS, g, :], gate_hi[:, k, :], sT_hi[:, k, cols], start=(k == 0), stop=False)
                    pe.matmul(inner[0:EXPERTS, g, :], gate_lo[:, k, :], sT_hi[:, k, cols], start=False, stop=False)
                    mm = pe.matmul(inner[0:EXPERTS, g, :], gate_hi[:, k, :], sT_lo[:, k, cols], start=False, stop=(k == 1))
                mm.then_inc(sem["logits_full"], 1)
            pe.wait_ge(sem["logits_read"], GROUPS)
            for t in range(B):
                mm = pe.transpose(y[:, 0, 0, EXPERTS * t:EXPERTS * t + EXPERTS], logitsT[:, P * t:P * t + P],
                                  ident[0:EXPERTS, 0:EXPERTS])
            mm.then_inc(sem["gates_full"], 1)

            def inner_products(seq, g):
                p = seq.odd
                cols = slice(GROUP * g, GROUP * g + GROUP)
                if g == 0:
                    upto(pe, gu_split, seq, 1, 1)
                for c in range(4):
                    upto(pe, sem["hidden_set"], seq, 16, 4 * g + c - 1)
                    for half in range(2):
                        bank = 2 * (c % 2) + half
                        at = slice(INNER * half + P * c, INNER * half + P * c + P)
                        for k in range(2):
                            pe.matmul(inner[:, bank, :], gu_hi[p][:, k, at], sT_hi[:, k, cols], start=(k == 0), stop=False)
                            pe.matmul(inner[:, bank, :], gu_hi[p][:, k, at], sT_lo[:, k, cols], start=False, stop=False)
                            mm = pe.matmul(inner[:, bank, :], gu_lo[p][:, k, at], sT_hi[:, k, cols], start=False, stop=(k == 1))
                    mm.then_inc(sem["inner_full"], 1)

            def outer_products(seq, g):
                p = seq.odd
                upto(pe, sem["hidden_lo_set"], seq, 16, 4 * g + 4)
                if g == 0:
                    upto(pe, down_split, seq, 1, 1)
                for bank in range(2):
                    upto(pe, sem["y_read"], seq, 8, 2 * (g - 2) + bank + 1)
                    for v in range(2):
                        t = 2 * bank + v
                        for c in range(4):
                            h_hi = hidden_hi[g % 2][:, c, P * t:P * t + P]
                            h_lo = hidden_lo[g % 2][:, c, P * t:P * t + P]
                            o = y[:, g % 2, bank, D * v:D * v + D]
                            pe.matmul(o, h_hi, down_hi[p][:, c, :], start=(c == 0), stop=False)
                            pe.matmul(o, h_hi, down_lo[p][:, c, :], start=False, stop=False)
                            mm = pe.matmul(o, h_lo, down_hi[p][:, c, :], start=False, stop=(c == 3))
                    mm.then_inc(sem["y_full"], 1)

            def net(seq):
                for g in range(GROUPS):
                    inner_products(seq, g)
                    if g:
                        outer_products(seq, g - 1)
                    elif seq.off or seq.i is not None:
                        outer_products(seq.back(1), GROUPS - 1)

            pe.wait_ge(sem["step"], 2)
            run(pe, net)
            outer_products(Seq(NETS - 1), GROUPS - 1)


def constants():
    c = np.zeros((P, 3 * P + 22 + EXPERTS), np.float32)
    q, r = np.arange(P), np.arange(P)
    c[:, 0:P] = np.eye(P)
    c[:, P:2 * P] = np.where(q[None, :] <= q[:, None], 0.0, MASKED)
    c[:, 2 * P:3 * P] = c[:, P:2 * P].T
    at = 3 * P
    for b in range(2):
        c[:, at + b] = np.where(r < 96, r % 32 // HD == b, (r < 96 + HEADS) & (r % 2 == b))
    for j in range(4):
        c[:, at + 2 + j] = np.where(r < 96, r % 32 // XD == j, r % 4 == j)
    for n in range(8):
        c[0:32, at + 6 + n] = -1.0 * ((r[:32] < HEADS) & (r[:32] // 2 == n))
        c[0:32, at + 14 + n] = -1.0 * (r[:32] // 4 == n)
    c[:, at + 22:] = np.arange(EXPERTS, 0, -1)
    return c


def kernel(x, ctx_512, L0_attn_Wqkv_w, L0_attn_Wqkv_b, L0_attn_out_w, L0_attn_out_b, L0_ffn_gate_w,
           L0_ffn_base_gate_up, L0_ffn_base_down, L0_ffn_expert_gate_up, L0_ffn_expert_down):
    import concourse.bacc as bacc
    from concourse.bass_utils import run_bass_kernel_spmd

    x = np.asarray(x).reshape(B * S, D)
    ctx = np.asarray(ctx_512).reshape(B * S, XKV * XD)
    ctxT = np.tile(ctx.reshape(B * S, 2, 32).transpose(2, 1, 0), (3, 1, 1))
    arrays = dict(
        x=x, xT=x.T, ctx=ctx, ctxT=ctxT, wqkvT=np.asarray(L0_attn_Wqkv_w).T, bqkv=L0_attn_Wqkv_b,
        woT=np.asarray(L0_attn_out_w).T, bo=L0_attn_out_b, gate_w=L0_ffn_gate_w, base_gu=L0_ffn_base_gate_up,
        base_down=L0_ffn_base_down, exp_gu=L0_ffn_expert_gate_up, exp_down=L0_ffn_expert_down, consts=constants())
    arrays = {f"in_{n}": np.ascontiguousarray(a) for n, a in arrays.items()}
    nc = bacc.Bacc("TRN2", target_bir_lowering=False, num_devices=1)
    args = [nc.dram_tensor(n, a.shape, mybir.dt.from_np(a.dtype), kind="ExternalInput").ap() for n, a in arrays.items()]
    args.append(nc.dram_tensor("out", (B * S, D), F32, kind="ExternalOutput").ap())
    decoder_layer(nc, *args)
    r = run_bass_kernel_spmd(nc, [arrays], core_ids=[0])
    return r.results[0]["out"].reshape(B, S, D)
```

```python
from contextlib import ExitStack

import numpy as np

import concourse.bass as bass
from concourse import mybir

F32 = mybir.dt.float32
F32R = mybir.dt.float32r
BF16 = mybir.dt.bfloat16
ALU = mybir.AluOpType
ACT = mybir.ActivationFunctionType
AX = mybir.AxisListType

B, S, D = 16, 128, 256
HEADS, HD = 16, 16
XKV, XG, XD = 8, 4, 8
INNER, EXPERTS = 512, 8
P = 128
QKV = D + 2 * HD
EPS = 1e-5
MASKED = -1e30
SCALE_S = float(HD) ** -0.5
SCALE_X = float(XD) ** -0.5
GROUP = 512
GROUPS = B * S // GROUP
TILES = GROUP // P
NETS = EXPERTS + 1

PE_ORDER = [
    ("c_main", 3, -1), ("s_shift", 0, 2), ("s_out", 1, 1), ("c_max", 1, 0), ("c_max", 2, 0), ("c_sum", 0, -1),
    ("c_sum", 1, -1), ("s_proj", 0, 1), ("s_main", 0, 2), ("c_max", 3, 0), ("s_turn", 0, 3), ("s_main", 1, 2),
    ("s_res", 0, 1), ("c_shift", 0, 0), ("s_max", 0, 3), ("c_sum", 2, -1), ("c_sum", 3, -1), ("c_main", 0, 0),
    ("c_out", 0, -1), ("c_out", 1, -1), ("s_sum", 0, 2), ("c_main", 1, 0), ("s_max", 1, 3), ("c_turn", 0, 1),
    ("c_main", 2, 0), ("s_out", 0, 2), ("c_max", 0, 1), ("s_qkv", 0, 4), ("s_sum", 1, 2),
]
ACT_ORDER = [
    ("s_exp", 0, 2), ("s_turn", 0, 3), ("s_high", 0, 2), ("s_exp", 1, 2), ("c_values", 0, 0), ("s_high", 1, 2),
    ("s_ln", 0, 1), ("c_read", 0, -1), ("s_split", 0, 4), ("c_read", 1, -1), ("c_exp", 0, 0), ("c_rows", 0, 1),
    ("c_high", 0, 0), ("c_exp", 1, 0), ("s_read", 0, 2), ("c_turn", 0, 1), ("c_exp", 2, 0), ("c_high", 1, 0),
    ("s_read", 1, 2), ("c_exp", 3, 0), ("c_keys", 0, 2), ("c_high", 2, 0), ("c_high", 3, 0), ("s_rows", 0, 4),
    ("s_proj", 0, 2), ("c_ln", 0, -1),
]
DVE_ORDER = [
    ("s_out", 1, 1), ("c_max", 1, 0), ("c_max", 2, 0), ("s_rows", 0, 3), ("s_proj", 0, 1), ("c_keys", 0, 1),
    ("c_ln", 0, -2), ("c_max", 3, 0), ("s_turn", 0, 3), ("s_res", 0, 1), ("c_shift", 0, 0), ("s_ln", 0, 1),
    ("s_max", 0, 3), ("c_out", 0, -1), ("c_rows", 0, 1), ("c_out", 1, -1), ("s_max", 1, 3), ("c_res", 0, -1),
    ("s_out", 0, 2), ("c_max", 0, 1), ("s_bias", 0, 4), ("s_shift", 0, 3),
]
POOL_ORDER = [
    ("c_low", 1, -1), ("c_low", 2, -1), ("x_bias", 0, 1), ("c_low", 3, -1), ("s_low", 0, 2), ("c_values", 0, 0),
    ("s_split", 0, 4), ("c_keys", 0, 1), ("s_low", 1, 2), ("c_low", 0, 0),
]
SP_ORDER = [
    ("load_xT", 0, 4), ("load_ctx", 0, 2), ("load_x", 0, 2),
]
DELTAS = [d for order in (PE_ORDER, ACT_ORDER, DVE_ORDER, POOL_ORDER, SP_ORDER) for _, _, d in order]
FIRST_STEP, LAST_STEP = -max(DELTAS), B - 1 - min(DELTAS)
UNROLL = 4
LOOP_FROM = 2 - min(DELTAS)
LOOP_STEPS = (B - max(DELTAS) - LOOP_FROM) // UNROLL * UNROLL

SCORE_USE = {"s_max": ("s_max_read", 2), "s_main": ("s_exp", 2), "c_max": ("c_max_read", 4), "c_main": ("c_exp", 4)}
PROB_USE = {"s_exp": ("s_summed", 2), "c_exp": ("c_summed", 4)}
SUM_USE = {"s_sum": ("s_sum_read", 2), "c_sum": ("c_sum_read", 2)}
MISC_USE = {
    "s_qkv": [("s_qkv_read", 1, 1)],
    "s_turn": [("s_q_read", 2, 1), ("s_q_read", 2, 2), ("s_k_read", 1, 1)],
    "s_shift": [("s_shift_read", 1, 1)],
    "s_out": [("s_out_read", 2, None)],
    "s_proj": [("s_ctx_read", 1, 1)],
    "s_res": [("s_res_read", 1, 1)],
    "c_turn": [("c_q_read", 2, 1), ("c_q_read", 2, 2)],
    "c_shift": [("c_shift_read", 1, 1)],
    "c_out": [("c_out_read", 2, None)],
}


class Seq:

    def __init__(self, off, i=None, stride=2):
        self.off, self.i, self.stride = off, i, stride

    def at(self, per, plus=0):
        v = per * self.off + plus
        return v if self.i is None else self.i * (self.stride * per) + v

    def back(self, n):
        return Seq(self.off - n, self.i, self.stride)

    @property
    def odd(self):
        return self.off % 2

    @property
    def exists(self):
        return 0 <= self.off < B if self.i is None else self.off >= 0


def wait(eng, sem, seq, per=1, upto=None):
    assert seq.i is None or seq.exists
    if seq.exists:
        eng.wait_ge(sem, seq.at(per, per if upto is None else upto))


class Ring:

    def __init__(self, slots, uses):
        self.slots, self.uses = slots, uses
        assert 2 * len(uses) % slots == 0

    def _at(self, stage, unit, part):
        return next(n for n, u in enumerate(self.uses) if u[:3] == (stage, unit, part))

    def slot(self, stage, unit, seq, part=0):
        n = self._at(stage, unit, part)
        return ((seq.off - self.uses[n][3]) * len(self.uses) + n) % self.slots

    def wait_free(self, eng, sems, stage, unit, seq, part=0):
        n = self._at(stage, unit, part)
        at = (seq.off - self.uses[n][3]) * len(self.uses) + n
        while True:
            at -= self.slots
            step, m = divmod(at, len(self.uses))
            _, _, _, delta, name, per, upto = self.uses[m]
            if step + delta < -2 * len(self.uses):
                return
            before = Seq(step + delta, seq.i, seq.stride)
            assert seq.i is None or before.exists
            if before.exists:
                eng.wait_ge(sems[name], before.at(per, upto))
                return


def rings():
    score, prob, summed, misc = [], [], [], []
    for stage, unit, delta in ACT_ORDER:
        if stage in PROB_USE:
            name, per = PROB_USE[stage]
            prob.append((stage, unit, 0, delta, name, per, unit + 1))
    for stage, unit, delta in PE_ORDER:
        if stage in SCORE_USE:
            name, per = SCORE_USE[stage]
            score.append((stage, unit, 0, delta, name, per, unit + 1))
        if stage == "s_sum" or stage == "c_sum" and unit % 2 == 0:
            name, per = SUM_USE[stage]
            summed.append((stage, unit, 0, delta, name, per, (unit if stage == "s_sum" else unit // 2) + 1))
        for part, (name, per, upto) in enumerate(MISC_USE.get(stage, [])):
            misc.append((stage, unit, part, delta, name, per, unit + 1 if upto is None else upto))
    return Ring(2, score), Ring(4, prob), Ring(2, summed), Ring(2, misc)


def decoder_layer(nc, x, xT, ctx, ctxT, wqkvT, bqkv, woT, bo, gate_w, base_gu, base_down, exp_gu, exp_down, consts, out):
    with ExitStack() as both:
        def sb(name, shape, dt=F32, scope=both):
            return scope.enter_context(nc.sbuf_tensor(name, shape, dt))

        stream = sb("stream", [P, B, D])
        raw_gu0, raw_down0 = sb("raw_gu0", [P, 2, 2 * INNER]), sb("raw_down0", [P, INNER // P, D])
        gu_hi0, gu_lo0 = sb("gu_hi0", [P, 2, 2 * INNER], F32R), sb("gu_lo0", [P, 2, 2 * INNER], F32R)
        down_hi0, down_lo0 = sb("down_hi0", [P, INNER // P, D], F32R), sb("down_lo0", [P, INNER // P, D], F32R)
        ident = sb("ident", [P, P])
        eps = sb("eps", [P, 1])
        raw_loaded = [both.enter_context(nc.semaphore(f"raw_loaded{p}")) for p in range(2)]
        gu_split = both.enter_context(nc.semaphore("gu_split"))
        down_split = both.enter_context(nc.semaphore("down_split"))
        weights0 = (raw_gu0, raw_down0, gu_hi0, gu_lo0, down_hi0, down_lo0, raw_loaded, gu_split, down_split)
        attention(nc, x, xT, ctx, ctxT, wqkvT, bqkv, woT, bo, consts, stream, ident, eps, base_gu, base_down,
                  exp_gu, exp_down, weights0)
        experts(nc, gate_w, exp_gu, exp_down, consts, stream, ident, eps, weights0, out)


def load_net(eng, net, raw_gu, raw_down, loaded, gu, down):
    g = gu if net is None else gu[bass.ds(net, 1)].squeeze(0) if not isinstance(net, int) else gu[net]
    d = down if net is None else down[bass.ds(net, 1)].squeeze(0) if not isinstance(net, int) else down[net]
    eng.dma_start(raw_gu[:], g.rearrange("(k p) n -> p k n", p=P)).then_inc(loaded, 16)
    eng.dma_start(raw_down[:], d.rearrange("(k p) n -> p k n", p=P)).then_inc(loaded, 16)


def attention(nc, x, xT, ctx, ctxT, wqkvT, bqkv, woT, bo, consts, stream, ident, eps, base_gu, base_down,
              exp_gu, exp_down, weights0):
    raw_gu0, raw_down0, gu_hi0, gu_lo0, down_hi0, down_lo0, raw_loaded, gu_split, down_split = weights0
    score_ring, prob_ring, sum_ring, misc_ring = rings()
    with ExitStack() as scope:
        def sb(name, shape, dt=F32):
            return scope.enter_context(nc.sbuf_tensor(name, shape, dt))

        def two(name, shape, dt=F32):
            return [sb(f"{name}{p}", shape, dt) for p in range(2)]

        scores = scope.enter_context(nc.psum_tensor("scores", [P, 2, 1024], F32))
        sums = scope.enter_context(nc.psum_tensor("sums", [P, 2, 512], F32))
        misc = scope.enter_context(nc.psum_tensor("misc", [P, 2, 512], F32))

        cst = sb("cst", [P, 3 * P + 24])
        ident_r, ident_b = sb("ident_r", [P, P], F32R), sb("ident_b", [P, P], BF16)
        mask_qk, mask_kq = sb("mask_qk", [P, 4, P], BF16), sb("mask_kq", [P, 4, P], BF16)
        blk_s, blk_c = cst[:, 3 * P:3 * P + 2], cst[:, 3 * P + 2:3 * P + 6]
        neg_s, neg_c = cst[0:32, 3 * P + 6:3 * P + 14], cst[0:32, 3 * P + 14:3 * P + 22]
        raw_wqkv, raw_wo = sb("raw_wqkv", [P, 2, QKV]), sb("raw_wo", [P, 2, D])
        wqkv_hi, wqkv_lo = sb("wqkv_hi", [P, 2, QKV], F32R), sb("wqkv_lo", [P, 2, QKV], F32R)
        wo_hi, wo_lo = sb("wo_hi", [P, 2, D], F32R), sb("wo_lo", [P, 2, D], F32R)
        b_qkv, b_o = sb("b_qkv", [P, QKV]), sb("b_o", [P, D])

        xT_in, x_in = two("xT_in", [P, 2, S]), two("x_in", [P, D])
        ctxT_in, ctx_in = two("ctxT_in", [96, 2, S]), two("ctx_in", [P, XKV * XD])
        xT_hi, xT_lo = two("xT_hi", [P, 2, S], F32R), two("xT_lo", [P, 2, S], F32R)
        x_bias = two("x_bias", [P, D])

        qkv = sb("qkv", [P, QKV])
        rows_s = sb("rows_s", [P, 9, 96], F32R)
        q_s = two("q_s", [P, 8, S], F32R)
        k_s = two("k_s", [P, 2, S], F32R)
        v_s = two("v_s", [P, 2, 192], F32R)
        max_s = sb("max_s", [P, 32])
        sumT_s = sb("sumT_s", [P, 2, 512])
        rden_s = sb("rden_s", [P, 2, 8])
        raw_s = sb("raw_s", [P, 2, 8, HD])
        ctx_s = two("ctx_s", [P, D])
        ctxT_hi, ctxT_lo = sb("ctxT_hi", [P, 2, S], F32R), sb("ctxT_lo", [P, 2, S], F32R)
        pre1, x1 = two("pre1_", [P, D]), [sb(f"x1_{p}", [P, D]) for p in range(UNROLL)]

        rows_c = sb("rows_c", [P, 8, 96], F32R)
        q_c = two("q_c", [P, 8, S], F32R)
        k_split = sb("k_split", [96, 2, S], F32R)
        k_c = two("k_c", [P, 2, 4, S], F32R)
        v_c = two("v_c", [P, 2, 640], F32R)
        max_c = sb("max_c", [P, 32])
        sumT_c = sb("sumT_c", [P, 2, 512])
        rden_c = sb("rden_c", [P, 2, 16])
        raw_c = sb("raw_c", [P, 2, 4, 4, XD])
        ctx_c = sb("ctx_c", [P, D])
        pre2 = two("pre2_", [P, D])

        prob, prob_hi, prob_lo = sb("prob", [P, 4, 1024]), sb("prob_hi", [P, 4, 1024], F32R), sb("prob_lo", [P, 4, 1024], F32R)
        norm = {k: dict(stats=sb(f"stats_{k}", [P, 6]), mv=sb(f"mv_{k}", [P, 2]), ln=sb(f"ln_{k}", [P, 1]),
                        r=sb(f"r_{k}", [P, 1]), t=sb(f"t_{k}", [P, 3])) for k in "sc"}

        names = """consts_loaded consts_set weights_loaded w_hi w_split tables tables_b
            xT_hi_set xT_split x_biased s_qkv_full s_qkv_read s_rows_hi s_rows_lo s_q_full s_q_read s_k_full s_k_read
            s_max_full s_max_read s_shift_full s_shift_read s_main_full s_exp s_prob_hi s_prob_lo s_summed s_sum_read
            s_out_full s_rden s_out_read s_ctx s_ctx_full s_ctx_hi s_ctx_read s_res_full s_res_read s_stats s_mv s_ln s_rsqrt0
            s_newton x1_set
            ctx_k_hi ctx_k_lo ctx_k_set ctx_v_hi ctx_v_set c_rows_hi c_rows_lo c_q_full c_q_read c_max_full c_max_read c_shift_full
            c_shift_read c_main_full c_exp c_prob_hi c_prob_lo c_summed c_sum_read c_out_full c_rden c_out_read c_ctx c_res
            c_stats c_mv c_ln c_rsqrt0 c_newton x2_set net0_hi""".split()
        sem = {n: scope.enter_context(nc.semaphore(n)) for n in names}
        xT_loaded = [scope.enter_context(nc.semaphore(f"xT_loaded{p}")) for p in range(2)]
        x_loaded = [scope.enter_context(nc.semaphore(f"x_loaded{p}")) for p in range(2)]
        ctx_loaded = [scope.enter_context(nc.semaphore(f"ctx_loaded{p}")) for p in range(2)]

        def f32(ap):
            return ap.bitcast(F32)

        def run(eng, order, stages):
            def step(s, i=None):
                for stage, unit, delta in order:
                    seq = Seq(s + delta, i, UNROLL)
                    if seq.exists:
                        stages[stage](seq, unit)
            for s in range(FIRST_STEP, LOOP_FROM):
                step(s)
            with eng.Fori(0, LOOP_STEPS // UNROLL) as i:
                for u in range(UNROLL):
                    step(LOOP_FROM + u, i)
            for s in range(LOOP_FROM + LOOP_STEPS, LAST_STEP + 1):
                step(s)

        def wait_loaded(eng, sems, seq, loads=1):
            v = 16 * loads * (seq.off // 2 + 1)
            eng.wait_ge(sems[seq.odd], v if seq.i is None else seq.i * (8 * loads * seq.stride) + v)

        block = scope.enter_context(nc.Block())

        @block.sync
        def _(sp):
            sp.dma_start(cst[:, 0:3 * P + 22], consts[:, 0:3 * P + 22]).then_inc(sem["consts_loaded"], 16)
            sp.dma_start(raw_wqkv[:], wqkvT.rearrange("(k p) n -> p k n", p=P)).then_inc(sem["weights_loaded"], 16)
            sp.dma_start(b_qkv[:], bqkv.partition_broadcast(P)).then_inc(sem["weights_loaded"], 16)
            sp.dma_start(raw_wo[:], woT.rearrange("(k p) n -> p k n", p=P)).then_inc(sem["weights_loaded"], 16)
            sp.dma_start(b_o[:], bo.partition_broadcast(P)).then_inc(sem["weights_loaded"], 16)

            def load_xT(seq, unit):
                tokens = bass.ds(seq.at(S), S)
                wait(sp, sem["xT_split"], seq.back(2))
                sp.dma_start(xT_in[seq.odd][:], xT.rearrange("(k p) t -> p k t", p=P)[:, :, tokens])\
                    .then_inc(xT_loaded[seq.odd], 16)

            def load_x(seq, unit):
                tokens = bass.ds(seq.at(S), S)
                wait(sp, sem["x_biased"], seq.back(2))
                sp.dma_start(x_in[seq.odd][:], x[tokens, :]).then_inc(x_loaded[seq.odd], 16)

            def load_ctx(seq, unit):
                tokens = bass.ds(seq.at(S), S)
                wait(sp, sem["ctx_k_lo"], seq.back(2))
                wait(sp, sem["ctx_v_set"], seq.back(2))
                sp.dma_start(ctxT_in[seq.odd][:], ctxT[:, :, tokens]).then_inc(ctx_loaded[seq.odd], 16)
                sp.dma_start(ctx_in[seq.odd][:], ctx[tokens, :]).then_inc(ctx_loaded[seq.odd], 16)

            run(sp, SP_ORDER, dict(load_xT=load_xT, load_x=load_x, load_ctx=load_ctx))
            load_net(sp, None, raw_gu0, raw_down0, raw_loaded[0], base_gu, base_down)

        @block.gpsimd
        def _(pool):
            pool.wait_ge(sem["weights_loaded"], 64)
            pool.tensor_scalar(wqkv_hi[:], raw_wqkv[:], 1.0, None, ALU.mult).then_inc(sem["w_hi"], 1)
            pool.tensor_scalar(wo_hi[:], raw_wo[:], 1.0, None, ALU.mult).then_inc(sem["w_hi"], 1)
            pool.wait_ge(sem["w_hi"], 2)
            pool.tensor_tensor(wqkv_lo[:], raw_wqkv[:], f32(wqkv_hi[:]), ALU.subtract).then_inc(sem["w_split"], 1)
            pool.tensor_tensor(wo_lo[:], raw_wo[:], f32(wo_hi[:]), ALU.subtract).then_inc(sem["w_split"], 1)

            def s_split(seq, unit):
                p = seq.odd
                wait(pool, sem["xT_hi_set"], seq)
                pool.tensor_tensor(xT_lo[p][:], xT_in[p][:], f32(xT_hi[p][:]), ALU.subtract).then_inc(sem["xT_split"], 1)

            def s_low(seq, unit):
                n = prob_ring.slot("s_exp", unit, seq)
                wait(pool, sem["s_prob_hi"], seq, 2, unit + 1)
                pool.tensor_tensor(prob_lo[:, n, :], prob[:, n, :], f32(prob_hi[:, n, :]), ALU.subtract).then_inc(sem["s_prob_lo"], 1)

            def bias(seq, unit):
                p = seq.odd
                wait_loaded(pool, x_loaded, seq)
                wait(pool, sem["s_res_read"], seq.back(2))
                pool.tensor_tensor(x_bias[p][:], x_in[p][:], b_o[:], ALU.add).then_inc(sem["x_biased"], 1)

            def c_low(seq, unit):
                n = prob_ring.slot("c_exp", unit, seq)
                wait(pool, sem["c_prob_hi"], seq, 4, unit + 1)
                pool.tensor_tensor(prob_lo[:, n, :], prob[:, n, :], f32(prob_hi[:, n, :]), ALU.subtract).then_inc(sem["c_prob_lo"], 1)

            def c_keys(seq, unit):
                p = seq.odd
                wait(pool, sem["ctx_k_lo"], seq)
                wait(pool, sem["c_main_full"], seq.back(2), 4)
                for a in range(2):
                    ins = pool.tensor_tensor(
                        k_c[p][0:96, a], f32(k_split[:, a, :]).unsqueeze(1).broadcast_to([96, 4, S]),
                        blk_c[0:96].unsqueeze(2).broadcast_to([96, 4, S]), ALU.mult)
                ins.then_inc(sem["ctx_k_set"], 1)

            def c_values(seq, unit):
                p = seq.odd
                place = v_c[p][:].rearrange("p a (j s) -> p a j s", j=4)
                wait(pool, sem["ctx_v_hi"], seq)
                pool.tensor_tensor(place[:, :, :, XD + 1:2 * XD + 1], ctx_in[p][:].rearrange("p (a j d) -> p a j d", a=2, j=4),
                                   f32(place[:, :, :, 0:XD]), ALU.subtract).then_inc(sem["ctx_v_set"], 1)

            pool.wait_ge(sem["tables"], 3)
            run(pool, POOL_ORDER, dict(s_split=s_split, x_bias=bias, s_low=s_low, c_low=c_low, c_keys=c_keys, c_values=c_values))
            pool.wait_ge(raw_loaded[0], 32)
            pool.tensor_scalar(gu_hi0[:], raw_gu0[:], 1.0, None, ALU.mult).then_inc(sem["net0_hi"], 1)
            pool.wait_ge(sem["net0_hi"], 1)
            pool.tensor_tensor(gu_lo0[:], raw_gu0[:], f32(gu_hi0[:]), ALU.subtract).then_inc(gu_split, 1)
            pool.tensor_scalar(down_hi0[:], raw_down0[:], 1.0, None, ALU.mult).then_inc(sem["net0_hi"], 1)
            pool.wait_ge(sem["net0_hi"], 2)
            pool.tensor_tensor(down_lo0[:], raw_down0[:], f32(down_hi0[:]), ALU.subtract).then_inc(down_split, 1)

        @block.scalar
        def _(act):
            def c_keys(seq, unit):
                p = seq.odd
                wait_loaded(act, ctx_loaded, seq, 2)
                wait(act, sem["ctx_k_set"], seq.back(1))
                act.copy(k_split[:], ctxT_in[p][:]).then_inc(sem["ctx_k_hi"], 1)

            def c_values(seq, unit):
                p = seq.odd
                wait_loaded(act, ctx_loaded, seq, 2)
                wait(act, sem["c_summed"], seq.back(2), 4)
                act.copy(v_c[p][:].rearrange("p a (j s) -> p a j s", j=4)[:, :, :, 0:XD],
                         ctx_in[p][:].rearrange("p (a j d) -> p a j d", a=2, j=4)).then_inc(sem["ctx_v_hi"], 1)

            def s_split(seq, unit):
                p = seq.odd
                wait_loaded(act, xT_loaded, seq)
                wait(act, sem["s_qkv_full"], seq.back(2))
                act.copy(xT_hi[p][:], xT_in[p][:]).then_inc(sem["xT_hi_set"], 1)

            def s_rows(seq, unit):
                p = seq.odd
                wait(act, sem["s_qkv_read"], seq)
                wait(act, sem["s_k_full"], seq.back(1))
                wait(act, sem["s_summed"], seq.back(2), 2)
                q = qkv[:, 0:D].rearrange("p (n c) -> p n c", c=32)
                act.copy(rows_s[:, 0:8, 0:32], q)
                act.copy(rows_s[:, 0:8, 64:96], q)
                act.copy(rows_s[:, 8, 0:64].rearrange("p (r d) -> p r d", d=HD), qkv[:, D:D + HD].unsqueeze(1).broadcast_to([P, 4, HD]))
                act.copy(v_s[p][:, :, 0:HD], qkv[:, D + HD:QKV].unsqueeze(1).broadcast_to([P, 2, HD])).then_inc(sem["s_rows_hi"], 1)

            def s_turn(seq, unit):
                wait(act, sem["s_main_full"], seq.back(2), 2)
                for u in range(2):
                    n = misc_ring.slot("s_turn", 0, seq, u)
                    wait(act, sem["s_q_full"], seq, 2, u + 1)
                    act.copy(q_s[seq.odd][0:96, 4 * u:4 * u + 4, :], misc[0:96, n, :].rearrange("p (n t) -> p n t", n=4))\
                        .then_inc(sem["s_q_read"], 1)

            def exp_unit(stage, scores_stage, unit, seq, per, scale, full, exped):
                n, m = score_ring.slot(scores_stage, unit, seq), prob_ring.slot(stage, unit, seq)
                wait(act, sem[full], seq, per, unit + 1)
                prob_ring.wait_free(act, sem, stage, unit, seq)
                act.activation(prob[:, m, :], scores[:, n, :], ACT.Exp, scale=scale).then_inc(sem[exped], 1)

            def s_exp(seq, unit):
                exp_unit("s_exp", "s_main", unit, seq, 2, SCALE_S, "s_main_full", "s_exp")

            def c_exp(seq, unit):
                exp_unit("c_exp", "c_main", unit, seq, 4, SCALE_X, "c_main_full", "c_exp")

            def s_high(seq, unit):
                m = prob_ring.slot("s_exp", unit, seq)
                wait(act, sem["s_exp"], seq, 2, unit + 1)
                act.copy(prob_hi[:, m, :], prob[:, m, :]).then_inc(sem["s_prob_hi"], 1)

            def c_high(seq, unit):
                m = prob_ring.slot("c_exp", unit, seq)
                wait(act, sem["c_exp"], seq, 4, unit + 1)
                act.copy(prob_hi[:, m, :], prob[:, m, :]).then_inc(sem["c_prob_hi"], 1)

            def s_read(seq, unit):
                n = sum_ring.slot("s_sum", unit, seq)
                wait(act, sem["s_summed"], seq, 2, unit + 1)
                wait(act, sem["s_out_full"], seq.back(1), 2, unit + 1)
                act.copy(sumT_s[:, unit, :], sums[:, n, :]).then_inc(sem["s_sum_read"], 1)

            def c_read(seq, a):
                n = sum_ring.slot("c_sum", 2 * a, seq)
                wait(act, sem["c_summed"], seq, 4, 2 * a + 2)
                wait(act, sem["c_out_full"], seq.back(1), 2, a + 1)
                act.copy(sumT_c[:, a, :], sums[:, n, :]).then_inc(sem["c_sum_read"], 1)

            def s_proj(seq, unit):
                n = misc_ring.slot("s_proj", 0, seq)
                wait(act, sem["s_ctx_full"], seq)
                wait(act, sem["s_res_full"], seq.back(1))
                act.copy(ctxT_hi[:], misc[:, n, 0:2 * S].rearrange("p (k t) -> p k t", k=2)).then_inc(sem["s_ctx_hi"], 1)

            def rsqrt_start(seq, k):
                wait(act, sem[f"{k}_mv"], seq)
                wait(act, sem[f"{k}_newton"], seq.back(1), 4, 4)
                act.activation(norm[k]["ln"][:], norm[k]["mv"][:, 1:2], ACT.Ln, bias=eps[:]).then_inc(sem[f"{k}_ln"], 1)
                wait(act, sem[f"{k}_ln"], seq)
                act.activation(norm[k]["r"][:], norm[k]["ln"][:], ACT.Exp, scale=-0.5).then_inc(sem[f"{k}_rsqrt0"], 1)

            def s_ln(seq, unit):
                rsqrt_start(seq, "s")

            def c_ln(seq, unit):
                rsqrt_start(seq, "c")

            def c_rows(seq, unit):
                wait(act, sem["x1_set"], seq)
                wait(act, sem["c_q_full"], seq.back(1), 2)
                for part in (0, 2):
                    for a in range(2):
                        ins = act.copy(
                            rows_c[:, 4 * a:4 * a + 4, 32 * part:32 * part + 32].rearrange("p g (j d) -> p g j d", j=4),
                            x1[seq.off % UNROLL][:, P * a:P * a + P].rearrange("p (j g d) -> p g j d", j=4, g=4))
                ins.then_inc(sem["c_rows_hi"], 1)

            def c_turn(seq, unit):
                wait(act, sem["c_main_full"], seq.back(2), 4)
                for u in range(2):
                    n = misc_ring.slot("c_turn", 0, seq, u)
                    wait(act, sem["c_q_full"], seq, 2, u + 1)
                    act.copy(q_c[seq.odd][0:96, 4 * u:4 * u + 4, :], misc[0:96, n, :].rearrange("p (n t) -> p n t", n=4))\
                        .then_inc(sem["c_q_read"], 1)

            act.preload_act_table_set("natural_log_exp_and_others")
            act.wait_ge(sem["tables"], 3)
            run(act, ACT_ORDER, dict(s_split=s_split, s_rows=s_rows, s_turn=s_turn, s_exp=s_exp, s_high=s_high, s_read=s_read,
                                     s_proj=s_proj, s_ln=s_ln, c_keys=c_keys, c_values=c_values, c_rows=c_rows,
                                     c_turn=c_turn, c_exp=c_exp, c_high=c_high, c_read=c_read, c_ln=c_ln))

        @block.vector
        def _(dve):
            dve.memset(max_s[:], 0.0)
            for p in range(2):
                dve.memset(f32(v_s[p][:]), 0.0)
                dve.memset(f32(v_c[p][:]), 0.0)
            dve.memset(eps[:], EPS).then_inc(sem["tables"], 1)
            dve.wait_ge(sem["tables"], 1)
            for p in range(2):
                dve.memset(f32(v_s[p][:, :, HD:HD + 1]), 1.0)
                ins = dve.memset(f32(v_c[p][:].rearrange("p a (j s) -> p a j s", j=4)[:, :, :, XD:XD + 1]), 1.0)
            ins.then_inc(sem["tables"], 1)
            dve.wait_ge(sem["consts_loaded"], 16)
            dve.tensor_copy(ident[:], cst[:, 0:P])
            dve.tensor_copy(ident_r[:], cst[:, 0:P])
            dve.tensor_copy(ident_b[:], cst[:, 0:P])
            dve.tensor_copy(mask_qk[:], cst[:, P:2 * P].unsqueeze(1).broadcast_to([P, 4, P]))
            dve.tensor_copy(mask_kq[:], cst[:, 2 * P:3 * P].unsqueeze(1).broadcast_to([P, 4, P]))
            for p in range(2):
                dve.tensor_copy(k_s[p][96:128], blk_s[96:128].unsqueeze(2).broadcast_to([32, 2, S]))
                for a in range(2):
                    ins = dve.tensor_copy(k_c[p][96:128, a], blk_c[96:128].unsqueeze(2).broadcast_to([32, 4, S]))
            ins.then_inc(sem["tables"], 1)

            def s_bias(seq, unit):
                n = misc_ring.slot("s_qkv", 0, seq)
                wait(dve, sem["s_qkv_full"], seq)
                wait(dve, sem["s_rows_lo"], seq.back(1))
                dve.tensor_tensor(qkv[:], misc[:, n, 0:QKV], b_qkv[:], ALU.add).then_inc(sem["s_qkv_read"], 1)

            def s_rows(seq, unit):
                p = seq.odd
                wait(dve, sem["s_rows_hi"], seq)
                dve.tensor_tensor(rows_s[:, 0:8, 32:64], qkv[:, 0:D].rearrange("p (n c) -> p n c", c=32),
                                  f32(rows_s[:, 0:8, 0:32]), ALU.subtract)
                dve.tensor_tensor(rows_s[:, 8, 64:96].rearrange("p (r d) -> p r d", d=HD),
                                  qkv[:, D:D + HD].unsqueeze(1).broadcast_to([P, 2, HD]),
                                  f32(rows_s[:, 8, 0:32]).rearrange("p (r d) -> p r d", d=HD), ALU.subtract)
                dve.tensor_tensor(v_s[p][:, :, HD + 1:2 * HD + 1], qkv[:, D + HD:QKV].unsqueeze(1).broadcast_to([P, 2, HD]),
                                  f32(v_s[p][:, :, 0:HD]), ALU.subtract).then_inc(sem["s_rows_lo"], 1)

            def s_turn(seq, unit):
                n = misc_ring.slot("s_turn", 0, seq, 2)
                wait(dve, sem["s_k_full"], seq)
                wait(dve, sem["s_main_full"], seq.back(2), 2)
                dve.tensor_tensor(k_s[seq.odd][0:96], misc[0:96, n, 0:S].unsqueeze(1).broadcast_to([96, 2, S]),
                                  blk_s[0:96].unsqueeze(2).broadcast_to([96, 2, S]), ALU.mult).then_inc(sem["s_k_read"], 1)

            def row_max(stage, unit, seq, per, full, read, out_, shifted):
                n = score_ring.slot(stage, unit, seq)
                wait(dve, sem[full], seq, per, unit + 1)
                if unit == 0:
                    wait(dve, sem[shifted], seq.back(1))
                dve.tensor_reduce(out_[:, 8 * unit:8 * unit + 8], scores[:, n, :].rearrange("p (h k) -> p h k", k=S),
                                  AX.X, ALU.max).then_inc(sem[read], 1)

            def s_max(seq, unit):
                row_max("s_max", unit, seq, 2, "s_max_full", "s_max_read", max_s, "s_shift_full")

            def c_max(seq, unit):
                row_max("c_max", unit, seq, 4, "c_max_full", "c_max_read", max_c, "c_shift_full")

            def shift_rows(stage, seq, q, neg, full, read):
                n = misc_ring.slot(stage, 0, seq)
                wait(dve, sem[full], seq)
                dve.tensor_tensor(q[seq.odd][96:128], misc[0:32, n, 0:S].unsqueeze(1).broadcast_to([32, 8, S]),
                                  neg.unsqueeze(2).broadcast_to([32, 8, S]), ALU.mult).then_inc(sem[read], 1)

            def s_shift(seq, unit):
                shift_rows("s_shift", seq, q_s, neg_s, "s_shift_full", "s_shift_read")

            def c_shift(seq, unit):
                shift_rows("c_shift", seq, q_c, neg_c, "c_shift_full", "c_shift_read")

            def s_out(seq, b):
                n = misc_ring.slot("s_out", b, seq)
                part = misc[:, n, :].rearrange("p (i h s) -> p i h s", i=4, h=2)
                wait(dve, sem["s_out_full"], seq, 2, b + 1)
                wait(dve, sem["s_ctx"], seq.back(1), 2, b + 1)
                dve.reciprocal(rden_s[:, b, :].rearrange("p (h i) -> p i h", h=2), part[:, :, :, HD:HD + 1].squeeze(3)).then_inc(sem["s_rden"], 1)
                both_parts = part[:, :, :, 0:2 * (HD + 1)].rearrange("p i h (two d) -> p i h d two", two=2)[:, :, :, 0:HD, :]
                dve.tensor_reduce(raw_s[:, b].rearrange("p (h i) d -> p i h d", h=2), both_parts, AX.X, ALU.add)\
                    .then_inc(sem["s_out_read"], 1)
                wait(dve, sem["s_rden"], seq, 2, b + 1)
                wait(dve, sem["s_out_read"], seq, 2, b + 1)
                wait(dve, sem["s_ctx_full"], seq.back(2))
                dve.tensor_tensor(ctx_s[seq.odd][:].rearrange("p (n b d) -> p n b d", b=2, d=HD)[:, :, b, :], raw_s[:, b],
                                  rden_s[:, b, :].unsqueeze(2).broadcast_to([P, 8, HD]), ALU.mult).then_inc(sem["s_ctx"], 1)

            def s_proj(seq, unit):
                n = misc_ring.slot("s_proj", 0, seq)
                wait(dve, sem["s_ctx_hi"], seq)
                dve.tensor_tensor(ctxT_lo[:], misc[:, n, 0:2 * S].rearrange("p (k t) -> p k t", k=2), f32(ctxT_hi[:]),
                                  ALU.subtract).then_inc(sem["s_ctx_read"], 1)

            def s_res(seq, unit):
                n = misc_ring.slot("s_res", 0, seq)
                wait(dve, sem["s_res_full"], seq)
                wait(dve, sem["x_biased"], seq)
                wait(dve, sem["x1_set"], seq.back(2))
                dve.tensor_tensor(pre1[seq.odd][:], misc[:, n, 0:D], x_bias[seq.odd][:], ALU.add).then_inc(sem["s_res_read"], 1)
                wait(dve, sem["s_res_read"], seq)
                stats("s", seq, pre1[seq.odd])

            def stats(k, seq, pre):
                wait(dve, sem[f"{k}_mv"], seq.back(1))
                dve.bn_stats(norm[k]["stats"][:], pre[:]).then_inc(sem[f"{k}_stats"], 1)
                wait(dve, sem[f"{k}_newton"], seq.back(1), 4)
                wait(dve, sem[f"{k}_ln"], seq.back(1))
                wait(dve, sem["x1_set" if k == "s" else "x2_set"], seq.back(1))
                wait(dve, sem[f"{k}_stats"], seq)
                dve.memset(norm[k]["t"][:, 0:1], 0.0)
                dve.bn_aggr(norm[k]["mv"][:], norm[k]["stats"][:]).then_inc(sem[f"{k}_mv"], 1)

            def newton(k, seq):
                r, t, mv, s = norm[k]["r"], norm[k]["t"], norm[k]["mv"], sem[f"{k}_newton"]
                wait(dve, sem[f"{k}_rsqrt0"], seq)
                wait(dve, sem["x1_set" if k == "s" else "x2_set"], seq.back(1))
                dve.tensor_tensor(t[:, 0:1], r[:], r[:], ALU.mult).then_inc(s, 1)
                wait(dve, s, seq, 4, 1)
                dve.scalar_tensor_tensor(t[:, 1:2], mv[:, 1:2], EPS, t[:, 0:1], ALU.add, ALU.mult).then_inc(s, 1)
                wait(dve, s, seq, 4, 2)
                dve.tensor_scalar(t[:, 0:1], t[:, 1:2], -0.5, 1.5, ALU.mult, ALU.add).then_inc(s, 1)
                wait(dve, s, seq, 4, 3)
                dve.tensor_tensor(t[:, 2:3], t[:, 0:1], r[:], ALU.mult).then_inc(s, 1)
                wait(dve, s, seq, 4, 4)

            def s_ln(seq, unit):
                newton("s", seq)
                if seq.i is not None or seq.off >= UNROLL:
                    wait(dve, sem["c_res"], seq.back(UNROLL))
                dve.tensor_scalar(x1[seq.off % UNROLL][:], pre1[seq.odd][:], norm["s"]["mv"][:, 0:1], norm["s"]["t"][:, 2:3],
                                  ALU.subtract, ALU.mult).then_inc(sem["x1_set"], 1)

            def c_keys(seq, unit):
                p = seq.odd
                wait(dve, sem["ctx_k_hi"], seq)
                dve.tensor_tensor(k_split[64:96], ctxT_in[p][64:96], f32(k_split[64:96]), ALU.subtract).then_inc(sem["ctx_k_lo"], 1)

            def c_rows(seq, unit):
                wait(dve, sem["c_rows_hi"], seq)
                for a in range(2):
                    ins = dve.tensor_tensor(
                        rows_c[:, 4 * a:4 * a + 4, 32:64].rearrange("p g (j d) -> p g j d", j=4),
                        x1[seq.off % UNROLL][:, P * a:P * a + P].rearrange("p (j g d) -> p g j d", j=4, g=4),
                        f32(rows_c[:, 4 * a:4 * a + 4, 0:32]).rearrange("p g (j d) -> p g j d", j=4), ALU.subtract)
                ins.then_inc(sem["c_rows_lo"], 1)

            def c_out(seq, a):
                n = misc_ring.slot("c_out", a, seq)
                part = misc[:, n, :].rearrange("p (g j s) -> p g j s", g=4, j=4)
                wait(dve, sem["c_out_full"], seq, 2, a + 1)
                wait(dve, sem["c_ctx"], seq.back(1), 2, a + 1)
                dve.reciprocal(rden_c[:, a, :].rearrange("p (g j) -> p g j", g=4), part[:, :, :, XD:XD + 1].squeeze(3)).then_inc(sem["c_rden"], 1)
                both_parts = part[:, :, :, 0:2 * (XD + 1)].rearrange("p g j (two d) -> p g j d two", two=2)[:, :, :, 0:XD, :]
                dve.tensor_reduce(raw_c[:, a], both_parts, AX.X, ALU.add).then_inc(sem["c_out_read"], 1)
                wait(dve, sem["c_rden"], seq, 2, a + 1)
                wait(dve, sem["c_out_read"], seq, 2, a + 1)
                wait(dve, sem["c_res"], seq.back(1))
                dve.tensor_tensor(ctx_c[:, P * a:P * a + P].rearrange("p (j g d) -> p g j d", j=4, g=4), raw_c[:, a],
                                  rden_c[:, a, :].rearrange("p (g j) -> p g j", g=4).unsqueeze(3).broadcast_to([P, 4, 4, XD]),
                                  ALU.mult).then_inc(sem["c_ctx"], 1)

            def c_res(seq, unit):
                wait(dve, sem["c_ctx"], seq, 2)
                wait(dve, sem["x1_set"], seq)
                wait(dve, sem["x2_set"], seq.back(2))
                dve.tensor_tensor(pre2[seq.odd][:], ctx_c[:], x1[seq.off % UNROLL][:], ALU.add).then_inc(sem["c_res"], 1)
                wait(dve, sem["c_res"], seq)
                stats("c", seq, pre2[seq.odd])

            def c_ln(seq, unit):
                newton("c", seq)
                dve.tensor_scalar(stream[:, bass.ds(seq.at(1), 1), :].squeeze(1), pre2[seq.odd][:], norm["c"]["mv"][:, 0:1],
                                  norm["c"]["t"][:, 2:3], ALU.subtract, ALU.mult).then_inc(sem["x2_set"], 1)

            dve.wait_ge(sem["tables"], 3)
            run(dve, DVE_ORDER, dict(s_bias=s_bias, s_rows=s_rows, s_turn=s_turn, s_max=s_max, s_shift=s_shift, s_out=s_out,
                                     s_proj=s_proj, s_res=s_res, s_ln=s_ln, c_keys=c_keys, c_rows=c_rows, c_max=c_max,
                                     c_shift=c_shift, c_out=c_out, c_res=c_res, c_ln=c_ln))

        @block.tensor
        def _(pe):
            def three(out_, a_hi, a_lo, w_hi, w_lo, first, last):
                pe.matmul(out_, a_hi, w_hi, start=first, stop=False)
                pe.matmul(out_, a_hi, w_lo, start=False, stop=False)
                return pe.matmul(out_, a_lo, w_hi, start=False, stop=last)

            def s_qkv(seq, unit):
                p, n = seq.odd, misc_ring.slot("s_qkv", 0, seq)
                wait(pe, sem["xT_split"], seq)
                misc_ring.wait_free(pe, sem, "s_qkv", 0, seq)
                for k in range(2):
                    mm = three(misc[:, n, 0:QKV], xT_hi[p][:, k, :], xT_lo[p][:, k, :], wqkv_hi[:, k, :], wqkv_lo[:, k, :],
                               k == 0, k == 1)
                mm.then_inc(sem["s_qkv_full"], 1)

            def s_turn(seq, unit):
                wait(pe, sem["s_rows_lo"], seq)
                for u in range(2):
                    n = misc_ring.slot("s_turn", 0, seq, u)
                    misc_ring.wait_free(pe, sem, "s_turn", 0, seq, u)
                    for j in range(4):
                        mm = pe.transpose(misc[0:96, n, S * j:S * j + S].bitcast(F32R), rows_s[:, 4 * u + j, :], ident_r[:])
                    mm.then_inc(sem["s_q_full"], 1)
                n = misc_ring.slot("s_turn", 0, seq, 2)
                misc_ring.wait_free(pe, sem, "s_turn", 0, seq, 2)
                pe.transpose(misc[0:96, n, 0:S].bitcast(F32R), rows_s[:, 8, :], ident_r[:]).then_inc(sem["s_k_full"], 1)

            def s_max(seq, unit):
                p, n = seq.odd, score_ring.slot("s_max", unit, seq)
                wait(pe, sem["s_q_read"], seq, 2, unit + 1)
                wait(pe, sem["s_k_read"], seq)
                score_ring.wait_free(pe, sem, "s_max", unit, seq)
                for bank in range(2):
                    at = 512 * bank
                    pe.matmul(scores[:, n, at:at + 512], ident_b[:], mask_qk[:], start=True, stop=False)
                    for v in range(2):
                        mm = pe.matmul(scores[:, n, at + 256 * v:at + 256 * v + 256], q_s[p][0:96, 4 * unit + 2 * bank + v, :],
                                       k_s[p][0:96], start=False, stop=(v == 1))
                mm.then_inc(sem["s_max_full"], 1)

            def shift(stage, seq, maxima, read, per, full):
                n = misc_ring.slot(stage, 0, seq)
                wait(pe, sem[read], seq, per)
                misc_ring.wait_free(pe, sem, stage, 0, seq)
                pe.transpose(misc[0:32, n, 0:S], maxima[:], ident[:]).then_inc(sem[full], 1)

            def s_shift(seq, unit):
                shift("s_shift", seq, max_s, "s_max_read", 2, "s_shift_full")

            def c_shift(seq, unit):
                shift("c_shift", seq, max_c, "c_max_read", 4, "c_shift_full")

            def s_main(seq, b):
                p, n = seq.odd, score_ring.slot("s_main", b, seq)
                wait(pe, sem["s_shift_read"], seq)
                score_ring.wait_free(pe, sem, "s_main", b, seq)
                for bank in range(2):
                    at = 512 * bank
                    pe.matmul(scores[:, n, at:at + 512], ident_b[:], mask_kq[:], start=True, stop=False)
                    mm = pe.matmul(scores[:, n, at:at + 512], k_s[p][:, b, :], q_s[p][:, 4 * bank:4 * bank + 4, :],
                                   start=False, stop=True)
                mm.then_inc(sem["s_main_full"], 1)

            def s_sum(seq, b):
                p, n, m = seq.odd, sum_ring.slot("s_sum", b, seq), prob_ring.slot("s_exp", b, seq)
                wait(pe, sem["s_prob_lo"], seq, 2, b + 1)
                sum_ring.wait_free(pe, sem, "s_sum", b, seq)
                v = v_s[p][:].rearrange("p h s -> p (h s)")
                for h in range(2):
                    w = v[:, P * h:P * h + P]
                    pe.matmul(sums[:, n, :], w, prob_hi[:, m, 512 * h:512 * h + 512], start=(h == 0), stop=False)
                    mm = pe.matmul(sums[:, n, :], w, prob_lo[:, m, 512 * h:512 * h + 512], start=False, stop=(h == 1))
                mm.then_inc(sem["s_summed"], 1)

            def turn_sums(stage, seq, unit, source, read, full):
                n = misc_ring.slot(stage, unit, seq)
                wait(pe, sem[read], seq, 2, unit + 1)
                misc_ring.wait_free(pe, sem, stage, unit, seq)
                for j in range(4):
                    mm = pe.transpose(misc[:, n, S * j:S * j + S], source[:, unit, S * j:S * j + S], ident[:])
                mm.then_inc(sem[full], 1)

            def s_out(seq, b):
                turn_sums("s_out", seq, b, sumT_s, "s_sum_read", "s_out_full")

            def c_out(seq, a):
                turn_sums("c_out", seq, a, sumT_c, "c_sum_read", "c_out_full")

            def s_proj(seq, unit):
                n = misc_ring.slot("s_proj", 0, seq)
                wait(pe, sem["s_ctx"], seq, 2)
                misc_ring.wait_free(pe, sem, "s_proj", 0, seq)
                for k in range(2):
                    mm = pe.transpose(misc[:, n, S * k:S * k + S], ctx_s[seq.odd][:, P * k:P * k + P], ident[:])
                mm.then_inc(sem["s_ctx_full"], 1)

            def s_res(seq, unit):
                n = misc_ring.slot("s_res", 0, seq)
                wait(pe, sem["s_ctx_read"], seq)
                misc_ring.wait_free(pe, sem, "s_res", 0, seq)
                for k in range(2):
                    mm = three(misc[:, n, 0:D], ctxT_hi[:, k, :], ctxT_lo[:, k, :], wo_hi[:, k, :], wo_lo[:, k, :],
                               k == 0, k == 1)
                mm.then_inc(sem["s_res_full"], 1)

            def c_turn(seq, unit):
                wait(pe, sem["c_rows_lo"], seq)
                for u in range(2):
                    n = misc_ring.slot("c_turn", 0, seq, u)
                    misc_ring.wait_free(pe, sem, "c_turn", 0, seq, u)
                    for j in range(4):
                        mm = pe.transpose(misc[0:96, n, S * j:S * j + S].bitcast(F32R), rows_c[:, 4 * u + j, :], ident_r[:])
                    mm.then_inc(sem["c_q_full"], 1)

            def c_max(seq, unit):
                p, n = seq.odd, score_ring.slot("c_max", unit, seq)
                wait(pe, sem["c_q_read"], seq, 2, unit // 2 + 1)
                wait(pe, sem["ctx_k_set"], seq)
                score_ring.wait_free(pe, sem, "c_max", unit, seq)
                for v in range(2):
                    mm = pe.matmul(scores[:, n, 512 * v:512 * v + 512], q_c[p][0:96, 2 * unit + v, :],
                                   k_c[p][0:96, unit // 2], start=True, stop=True)
                mm.then_inc(sem["c_max_full"], 1)

            def c_main(seq, unit):
                p, n, a = seq.odd, score_ring.slot("c_main", unit, seq), unit // 2
                wait(pe, sem["c_shift_read"], seq)
                score_ring.wait_free(pe, sem, "c_main", unit, seq)
                for v in range(2):
                    mm = pe.matmul(scores[:, n, 512 * v:512 * v + 512], k_c[p][:, a, 2 * (unit % 2) + v, :],
                                   q_c[p][:, 4 * a:4 * a + 4, :], start=True, stop=True)
                mm.then_inc(sem["c_main_full"], 1)

            def c_sum(seq, unit):
                p, a, m = seq.odd, unit // 2, prob_ring.slot("c_exp", unit, seq)
                n = sum_ring.slot("c_sum", 2 * a, seq)
                wait(pe, sem["c_prob_lo"], seq, 4, unit + 1)
                wait(pe, sem["ctx_v_set"], seq)
                if unit % 2 == 0:
                    sum_ring.wait_free(pe, sem, "c_sum", unit, seq)
                for v in range(2):
                    j = 2 * (unit % 2) + v
                    w = v_c[p][:, a, P * j:P * j + P]
                    pe.matmul(sums[:, n, :], w, prob_hi[:, m, 512 * v:512 * v + 512], start=(j == 0), stop=False)
                    mm = pe.matmul(sums[:, n, :], w, prob_lo[:, m, 512 * v:512 * v + 512], start=False, stop=(j == 3))
                mm.then_inc(sem["c_summed"], 1)

            pe.wait_ge(sem["tables"], 3)
            pe.wait_ge(sem["w_split"], 2)
            run(pe, PE_ORDER, dict(s_qkv=s_qkv, s_turn=s_turn, s_max=s_max, s_shift=s_shift, s_main=s_main, s_sum=s_sum, s_out=s_out,
                         s_proj=s_proj, s_res=s_res, c_turn=c_turn, c_max=c_max, c_shift=c_shift, c_main=c_main,
                         c_sum=c_sum, c_out=c_out))


def experts(nc, gate_w, exp_gu, exp_down, consts, stream, ident, eps, weights0, out):
    raw_gu0, raw_down0, gu_hi0, gu_lo0, down_hi0, down_lo0, raw_loaded, gu_split, down_split = weights0
    with ExitStack() as scope:
        def sb(name, shape, dt=F32):
            return scope.enter_context(nc.sbuf_tensor(name, shape, dt))

        inner = scope.enter_context(nc.psum_tensor("inner", [P, 4, 512], F32))
        y = scope.enter_context(nc.psum_tensor("y", [P, 2, 2, 512], F32))

        raw_gu = [raw_gu0, sb("raw_gu1", [P, 2, 2 * INNER])]
        raw_down = [raw_down0, sb("raw_down1", [P, INNER // P, D])]
        gu_hi = [gu_hi0, sb("gu_hi1", [P, 2, 2 * INNER], F32R)]
        gu_lo = [gu_lo0, sb("gu_lo1", [P, 2, 2 * INNER], F32R)]
        down_hi = [down_hi0, sb("down_hi1", [P, INNER // P, D], F32R)]
        down_lo = [down_lo0, sb("down_lo1", [P, INNER // P, D], F32R)]
        sT_hi, sT_lo = sb("sT_hi", [P, 2, B * S], F32R), sb("sT_lo", [P, 2, B * S], F32R)
        raw_gate = sb("raw_gate", [P, 2, EXPERTS])
        gate_hi, gate_lo = sb("gate_hi", [P, 2, EXPERTS], F32R), sb("gate_lo", [P, 2, EXPERTS], F32R)
        descending = sb("descending", [P, EXPERTS])
        logitsT = sb("logitsT", [EXPERTS, B * S])
        gates = {n: sb(f"gate_{n}", [P, B, EXPERTS]) for n in "shifted e p order first rest order2 second both w".split()}
        stat = {n: sb(f"stat_{n}", [P, B]) for n in "max sum rsum p1 o1 p2 o2 wsum rwsum".split()}
        share = sb("share", [P, B, NETS])
        silu = sb("silu", [P, 2, GROUP])
        hidden = [sb(f"hidden{p}", [P, 4, GROUP]) for p in range(2)]
        hidden_hi = [sb(f"hidden_hi{p}", [P, 4, GROUP], F32R) for p in range(2)]
        hidden_lo = [sb(f"hidden_lo{p}", [P, 4, GROUP], F32R) for p in range(2)]
        zeros = sb("zeros", [P, 1024])
        stats, mv = sb("stats", [P, B, 6]), sb("mv", [P, B, 2])
        lnv, r0, t0, t1, rstd = (sb(n, [P, B]) for n in ("lnv", "r0", "t0", "t1", "rstd"))

        names = """gate_loaded gate_hi_set gate_split sT_full sT_hi_set sT_set logits_full logits_read gates_full step exps
            shares inner_full silu_set hidden_set hidden_hi_set hidden_lo_set y_full y_read w_hi aggr ln_set rsqrt0 newton
            normed stored""".split()
        sem = {n: scope.enter_context(nc.semaphore("b_" + n)) for n in names}

        def f32(ap):
            return ap.bitcast(F32)

        def run(eng, net):
            net(Seq(0))
            with eng.Fori(0, EXPERTS // 2) as i:
                net(Seq(1, i))
                net(Seq(2, i))

        def upto(eng, s, seq, per, plus):
            if seq.i is not None or per * seq.off + plus > 0:
                eng.wait_ge(s, seq.at(per, plus))

        block = scope.enter_context(nc.Block())

        @block.sync
        def _(sp):
            sp.dma_start(raw_gate[:], gate_w.rearrange("(k p) n -> p k n", p=P)).then_inc(sem["gate_loaded"], 16)
            sp.dma_start(descending[:], consts[:, 3 * P + 22:3 * P + 22 + EXPERTS]).then_inc(sem["gate_loaded"], 16)

            def load(seq):
                sp.wait_ge(gu_split, seq.at(1, -1))
                sp.wait_ge(down_split, seq.at(1, -1))
                load_net(sp, seq.at(1, -1), raw_gu[seq.odd], raw_down[seq.odd], raw_loaded[seq.odd], exp_gu, exp_down)

            load_net(sp, 0, raw_gu[1], raw_down[1], raw_loaded[1], exp_gu, exp_down)
            load(Seq(2))
            with sp.Fori(0, (EXPERTS - 2) // 2) as i:
                load(Seq(3, i))
                load(Seq(4, i))
            tiles = out.rearrange("(t p) d -> p t d", p=P)
            for g in range(GROUPS):
                sp.wait_ge(sem["normed"], g + 1)
                sp.dma_start(tiles[:, TILES * g:TILES * g + TILES, :], stream[:, TILES * g:TILES * g + TILES, :]).then_inc(sem["stored"], 16)
            sp.wait_ge(sem["stored"], 16 * GROUPS)

        @block.gpsimd
        def _(pool):
            pool.wait_ge(sem["gate_loaded"], 32)
            pool.tensor_scalar(gate_hi[:], raw_gate[:], 1.0, None, ALU.mult).then_inc(sem["gate_hi_set"], 1)
            pool.wait_ge(sem["gate_hi_set"], 1)
            pool.tensor_tensor(gate_lo[:], raw_gate[:], f32(gate_hi[:]), ALU.subtract).then_inc(sem["gate_split"], 1)

            def split_next(seq, k):
                q = 1 - seq.odd
                if k == 0:
                    upto(pool, sem["y_full"], seq, 8, 0)
                    nxt = 32 * ((seq.off + 1) // 2 + 1)
                    pool.wait_ge(raw_loaded[q], nxt if seq.i is None else seq.i * 32 + nxt)
                hi, lo, raw = ((gu_hi[q][:, k, :], gu_lo[q][:, k, :], raw_gu[q][:, k, :]) if k < 2 else
                               (down_hi[q][:], down_lo[q][:], raw_down[q][:]))
                pool.tensor_tensor(hi, raw, zeros[:, 0:1024] if k < 2 else zeros[:, 0:1024].rearrange("p (a b) -> p a b", b=D),
                                   ALU.add).then_inc(sem["w_hi"], 1)
                upto(pool, sem["w_hi"], seq, 3, k + 1)
                ins = pool.tensor_tensor(lo, raw, f32(hi), ALU.subtract)
                if k:
                    ins.then_inc(gu_split if k == 1 else down_split, 1)

            def net(seq, last=False):
                for g in range(GROUPS):
                    for c in range(4):
                        upto(pool, sem["hidden_hi_set"], seq, 16, 4 * g + c + 1)
                        upto(pool, sem["y_full"], seq, 8, 2 * g - 2)
                        pool.tensor_tensor(hidden_lo[g % 2][:, c], hidden[g % 2][:, c], f32(hidden_hi[g % 2][:, c]),
                                           ALU.subtract).then_inc(sem["hidden_lo_set"], 1)
                    if g < 3 and not last:
                        split_next(seq, g)

            net(Seq(0))
            with pool.Fori(0, EXPERTS // 2 - 1) as i:
                net(Seq(1, i))
                net(Seq(2, i))
            net(Seq(EXPERTS - 1))
            net(Seq(EXPERTS), last=True)

        @block.scalar
        def _(act):
            for g in range(GROUPS):
                act.wait_ge(sem["sT_full"], g + 1)
                act.copy(sT_hi[:, :, GROUP * g:GROUP * g + GROUP], y[:, g % 2]).then_inc(sem["sT_hi_set"], 1)
            act.wait_ge(sem["step"], 2)
            act.activation(gates["e"][:], gates["shifted"][:], ACT.Exp).then_inc(sem["exps"], 1)

            def net(seq):
                for g in range(GROUPS):
                    for c in range(4):
                        at = 4 * g + c
                        upto(act, sem["inner_full"], seq, 16, at + 1)
                        upto(act, sem["hidden_set"], seq, 16, at - 1)
                        act.activation(silu[:, c % 2, :], inner[:, 2 * (c % 2), :], ACT.Silu).then_inc(sem["silu_set"], 1)
                        if c:
                            high(seq, g, c - 1)
                    high(seq, g, 3)

            def high(seq, g, c):
                upto(act, sem["hidden_set"], seq, 16, 4 * g + c + 1)
                upto(act, sem["y_full"], seq, 8, 2 * g - 2)
                act.copy(hidden_hi[g % 2][:, c], hidden[g % 2][:, c]).then_inc(sem["hidden_hi_set"], 1)

            run(act, net)
            act.preload_act_table_set("natural_log_exp_and_others")
            for g in range(GROUPS):
                a, b = TILES * g, TILES * g + TILES
                act.wait_ge(sem["aggr"], g + 1)
                act.activation(lnv[:, a:b], mv[:, a:b, 1:2].squeeze(2), ACT.Ln, bias=eps[:]).then_inc(sem["ln_set"], 1)
                act.wait_ge(sem["ln_set"], g + 1)
                act.activation(r0[:, a:b], lnv[:, a:b], ACT.Exp, scale=-0.5).then_inc(sem["rsqrt0"], 1)

        @block.vector
        def _(dve):
            dve.memset(share[:, :, 0:1], 1.0)
            dve.memset(zeros[:], 0.0)
            for g in range(GROUPS):
                dve.wait_ge(sem["sT_hi_set"], g + 1)
                cols = slice(GROUP * g, GROUP * g + GROUP)
                dve.tensor_tensor(sT_lo[:, :, cols], y[:, g % 2], f32(sT_hi[:, :, cols]), ALU.subtract).then_inc(sem["sT_set"], 1)
                dve.wait_ge(sem["logits_full"], g + 1)
                dve.tensor_copy(logitsT[:, cols], inner[0:EXPERTS, g, :]).then_inc(sem["logits_read"], 1)

            done = [0]

            def then(ins):
                done[0] += 1
                ins.then_inc(sem["step"], 1)
                dve.wait_ge(sem["step"], done[0])

            def all8(t):
                return t[:].unsqueeze(2).broadcast_to([P, B, EXPERTS])

            order = descending[:].unsqueeze(1).broadcast_to([P, B, EXPERTS])
            logits = y[:, 0, 0, 0:B * EXPERTS].rearrange("p (t n) -> p t n", n=EXPERTS)
            dve.wait_ge(sem["gates_full"], 1)
            dve.wait_ge(sem["gate_loaded"], 32)
            then(dve.tensor_reduce(stat["max"][:], logits, AX.X, ALU.max))
            then(dve.tensor_tensor(gates["shifted"][:], logits, all8(stat["max"]), ALU.subtract))
            dve.wait_ge(sem["exps"], 1)
            then(dve.tensor_reduce(stat["sum"][:], gates["e"][:], AX.X, ALU.add))
            then(dve.reciprocal(stat["rsum"][:], stat["sum"][:]))
            then(dve.tensor_tensor(gates["p"][:], gates["e"][:], all8(stat["rsum"]), ALU.mult))
            then(dve.tensor_reduce(stat["p1"][:], gates["p"][:], AX.X, ALU.max))
            then(dve.tensor_tensor(gates["order"][:], gates["p"][:], all8(stat["p1"]), ALU.is_equal))
            then(dve.tensor_tensor(gates["order"][:], gates["order"][:], order, ALU.mult))
            then(dve.tensor_reduce(stat["o1"][:], gates["order"][:], AX.X, ALU.max))
            then(dve.tensor_tensor(gates["first"][:], gates["order"][:], all8(stat["o1"]), ALU.is_equal))
            then(dve.scalar_tensor_tensor(gates["rest"][:], gates["first"][:], -2.0, gates["p"][:], ALU.mult, ALU.add))
            then(dve.tensor_reduce(stat["p2"][:], gates["rest"][:], AX.X, ALU.max))
            then(dve.tensor_tensor(gates["order2"][:], gates["rest"][:], all8(stat["p2"]), ALU.is_equal))
            then(dve.tensor_tensor(gates["order2"][:], gates["order2"][:], order, ALU.mult))
            then(dve.tensor_reduce(stat["o2"][:], gates["order2"][:], AX.X, ALU.max))
            then(dve.tensor_tensor(gates["second"][:], gates["order2"][:], all8(stat["o2"]), ALU.is_equal))
            then(dve.tensor_tensor(gates["both"][:], gates["first"][:], gates["second"][:], ALU.add))
            then(dve.tensor_tensor(gates["w"][:], gates["p"][:], gates["both"][:], ALU.mult))
            then(dve.tensor_reduce(stat["wsum"][:], gates["w"][:], AX.X, ALU.add))
            then(dve.reciprocal(stat["rwsum"][:], stat["wsum"][:]))
            then(dve.tensor_tensor(share[:, :, 1:NETS], gates["w"][:], all8(stat["rwsum"]), ALU.mult))

            def add_outputs(seq, g):
                for bank in range(2):
                    upto(dve, sem["y_full"], seq, 8, 2 * g + bank + 1)
                    upto(dve, sem["y_read"], seq, 8, 2 * g)
                    for v in range(2):
                        t = TILES * g + 2 * bank + v
                        ins = dve.scalar_tensor_tensor(stream[:, t, :], y[:, g % 2, bank, D * v:D * v + D],
                                                       share[:, t, bass.ds(seq.at(1), 1)], stream[:, t, :], ALU.mult, ALU.add)
                    ins.then_inc(sem["y_read"], 1)

            def net(seq):
                for g in range(GROUPS):
                    for c in range(4):
                        at = 4 * g + c
                        upto(dve, sem["silu_set"], seq, 16, at + 1)
                        upto(dve, sem["hidden_lo_set"], seq, 16, at - 7)
                        dve.tensor_tensor(hidden[g % 2][:, c], silu[:, c % 2, :], inner[:, 2 * (c % 2) + 1, :], ALU.mult)\
                            .then_inc(sem["hidden_set"], 1)
                    if g:
                        add_outputs(seq, g - 1)
                    elif seq.off or seq.i is not None:
                        add_outputs(seq.back(1), GROUPS - 1)

            run(dve, net)
            chain = [0]

            def link(ins):
                chain[0] += 1
                ins.then_inc(sem["newton"], 1)
                dve.wait_ge(sem["newton"], chain[0])

            for g in range(GROUPS):
                if g == GROUPS - 1:
                    add_outputs(Seq(NETS - 1), GROUPS - 1)
                a, b = TILES * g, TILES * g + TILES
                dve.wait_ge(sem["y_read"], 8 * (NETS - 1) + 2 * g + 2)
                for t in range(a, b):
                    ins = dve.bn_stats(stats[:, t, :], stream[:, t, :])
                link(ins)
                for t in range(a, b):
                    ins = dve.bn_aggr(mv[:, t, :], stats[:, t, :])
                ins.then_inc(sem["aggr"], 1)
                dve.wait_ge(sem["rsqrt0"], g + 1)
                link(dve.tensor_tensor(t0[:, a:b], r0[:, a:b], r0[:, a:b], ALU.mult))
                link(dve.scalar_tensor_tensor(t1[:, a:b], mv[:, a:b, 1:2].squeeze(2), EPS, t0[:, a:b], ALU.add, ALU.mult))
                link(dve.tensor_scalar(t0[:, a:b], t1[:, a:b], -0.5, 1.5, ALU.mult, ALU.add))
                link(dve.tensor_tensor(rstd[:, a:b], t0[:, a:b], r0[:, a:b], ALU.mult))
                for t in range(a, b):
                    ins = dve.tensor_scalar(stream[:, t, :], stream[:, t, :], mv[:, t, 0:1], rstd[:, t:t + 1],
                                            ALU.subtract, ALU.mult)
                ins.then_inc(sem["normed"], 1)

        @block.tensor
        def _(pe):
            def turn_stream(g):
                if g >= 2:
                    pe.wait_ge(sem["sT_set"], g - 1)
                for k in range(2):
                    for t in range(TILES):
                        mm = pe.transpose(y[:, g % 2, k, P * t:P * t + P], stream[:, TILES * g + t, P * k:P * k + P], ident[:])
                mm.then_inc(sem["sT_full"], 1)

            turn_stream(0)
            pe.wait_ge(sem["gate_split"], 1)
            for g in range(GROUPS):
                if g + 1 < GROUPS:
                    turn_stream(g + 1)
                pe.wait_ge(sem["sT_set"], g + 1)
                cols = slice(GROUP * g, GROUP * g + GROUP)
                for k in range(2):
                    pe.matmul(inner[0:EXPERTS, g, :], gate_hi[:, k, :], sT_hi[:, k, cols], start=(k == 0), stop=False)
                    pe.matmul(inner[0:EXPERTS, g, :], gate_lo[:, k, :], sT_hi[:, k, cols], start=False, stop=False)
                    mm = pe.matmul(inner[0:EXPERTS, g, :], gate_hi[:, k, :], sT_lo[:, k, cols], start=False, stop=(k == 1))
                mm.then_inc(sem["logits_full"], 1)
            pe.wait_ge(sem["logits_read"], GROUPS)
            for t in range(B):
                mm = pe.transpose(y[:, 0, 0, EXPERTS * t:EXPERTS * t + EXPERTS], logitsT[:, P * t:P * t + P],
                                  ident[0:EXPERTS, 0:EXPERTS])
            mm.then_inc(sem["gates_full"], 1)

            def inner_products(seq, g):
                p = seq.odd
                cols = slice(GROUP * g, GROUP * g + GROUP)
                if g == 0:
                    upto(pe, gu_split, seq, 1, 1)
                for c in range(4):
                    upto(pe, sem["hidden_set"], seq, 16, 4 * g + c - 1)
                    for half in range(2):
                        bank = 2 * (c % 2) + half
                        at = slice(INNER * half + P * c, INNER * half + P * c + P)
                        for k in range(2):
                            pe.matmul(inner[:, bank, :], gu_hi[p][:, k, at], sT_hi[:, k, cols], start=(k == 0), stop=False)
                            pe.matmul(inner[:, bank, :], gu_hi[p][:, k, at], sT_lo[:, k, cols], start=False, stop=False)
                            mm = pe.matmul(inner[:, bank, :], gu_lo[p][:, k, at], sT_hi[:, k, cols], start=False, stop=(k == 1))
                    mm.then_inc(sem["inner_full"], 1)

            def outer_products(seq, g):
                p = seq.odd
                upto(pe, sem["hidden_lo_set"], seq, 16, 4 * g + 4)
                if g == 0:
                    upto(pe, down_split, seq, 1, 1)
                for bank in range(2):
                    upto(pe, sem["y_read"], seq, 8, 2 * (g - 2) + bank + 1)
                    for v in range(2):
                        t = 2 * bank + v
                        for c in range(4):
                            h_hi = hidden_hi[g % 2][:, c, P * t:P * t + P]
                            h_lo = hidden_lo[g % 2][:, c, P * t:P * t + P]
                            o = y[:, g % 2, bank, D * v:D * v + D]
                            pe.matmul(o, h_hi, down_hi[p][:, c, :], start=(c == 0), stop=False)
                            pe.matmul(o, h_hi, down_lo[p][:, c, :], start=False, stop=False)
                            mm = pe.matmul(o, h_lo, down_hi[p][:, c, :], start=False, stop=(c == 3))
                    mm.then_inc(sem["y_full"], 1)

            def net(seq):
                for g in range(GROUPS):
                    inner_products(seq, g)
                    if g:
                        outer_products(seq, g - 1)
                    elif seq.off or seq.i is not None:
                        outer_products(seq.back(1), GROUPS - 1)

            pe.wait_ge(sem["step"], 2)
            run(pe, net)
            outer_products(Seq(NETS - 1), GROUPS - 1)


def constants():
    c = np.zeros((P, 3 * P + 22 + EXPERTS), np.float32)
    q, r = np.arange(P), np.arange(P)
    c[:, 0:P] = np.eye(P)
    c[:, P:2 * P] = np.where(q[None, :] <= q[:, None], 0.0, MASKED)
    c[:, 2 * P:3 * P] = c[:, P:2 * P].T
    at = 3 * P
    for b in range(2):
        c[:, at + b] = np.where(r < 96, r % 32 // HD == b, (r < 96 + HEADS) & (r % 2 == b))
    for j in range(4):
        c[:, at + 2 + j] = np.where(r < 96, r % 32 // XD == j, r % 4 == j)
    for n in range(8):
        c[0:32, at + 6 + n] = -1.0 * ((r[:32] < HEADS) & (r[:32] // 2 == n))
        c[0:32, at + 14 + n] = -1.0 * (r[:32] // 4 == n)
    c[:, at + 22:] = np.arange(EXPERTS, 0, -1)
    return c


def kernel(x, ctx_512, L0_attn_Wqkv_w, L0_attn_Wqkv_b, L0_attn_out_w, L0_attn_out_b, L0_ffn_gate_w,
           L0_ffn_base_gate_up, L0_ffn_base_down, L0_ffn_expert_gate_up, L0_ffn_expert_down):
    import concourse.bacc as bacc
    from concourse.bass_utils import run_bass_kernel_spmd

    x = np.asarray(x).reshape(B * S, D)
    ctx = np.asarray(ctx_512).reshape(B * S, XKV * XD)
    ctxT = np.tile(ctx.reshape(B * S, 2, 32).transpose(2, 1, 0), (3, 1, 1))
    arrays = dict(
        x=x, xT=x.T, ctx=ctx, ctxT=ctxT, wqkvT=np.asarray(L0_attn_Wqkv_w).T, bqkv=L0_attn_Wqkv_b,
        woT=np.asarray(L0_attn_out_w).T, bo=L0_attn_out_b, gate_w=L0_ffn_gate_w, base_gu=L0_ffn_base_gate_up,
        base_down=L0_ffn_base_down, exp_gu=L0_ffn_expert_gate_up, exp_down=L0_ffn_expert_down, consts=constants())
    arrays = {f"in_{n}": np.ascontiguousarray(a) for n, a in arrays.items()}
    nc = bacc.Bacc("TRN2", target_bir_lowering=False, num_devices=1)
    args = [nc.dram_tensor(n, a.shape, mybir.dt.from_np(a.dtype), kind="ExternalInput").ap() for n, a in arrays.items()]
    args.append(nc.dram_tensor("out", (B * S, D), F32, kind="ExternalOutput").ap())
    decoder_layer(nc, *args)
    r = run_bass_kernel_spmd(nc, [arrays], core_ids=[0])
    return r.results[0]["out"].reshape(B, S, D)
```

```python
from contextlib import ExitStack

import numpy as np

import concourse.bass as bass
from concourse import mybir

F32 = mybir.dt.float32
F32R = mybir.dt.float32r
BF16 = mybir.dt.bfloat16
ALU = mybir.AluOpType
ACT = mybir.ActivationFunctionType
AX = mybir.AxisListType

B, S, D = 16, 128, 256
HEADS, HD = 16, 16
XKV, XG, XD = 8, 4, 8
INNER, EXPERTS = 512, 8
P = 128
QKV = D + 2 * HD
EPS = 1e-5
MASKED = -1e30
SCALE_S = float(HD) ** -0.5
SCALE_X = float(XD) ** -0.5
GROUP = 512
GROUPS = B * S // GROUP
TILES = GROUP // P
NORM_PARTS = [(0, B - TILES), (B - TILES, B)]
CONST_COLS = 3 * P + 22 + EXPERTS
NETS = EXPERTS + 1

PE_ORDER = [
    ("s_proj", 0, 1), ("c_max", 2, 0), ("s_main", 0, 2), ("s_turn", 0, 3), ("c_max", 3, 0), ("s_res", 0, 1),
    ("c_sum", 1, -1), ("s_main", 1, 2), ("c_shift", 0, 0), ("c_sum", 2, -1), ("s_max", 0, 3), ("c_sum", 3, -1),
    ("c_main", 0, 0), ("c_out", 0, -1), ("s_sum", 0, 2), ("c_main", 1, 0), ("c_out", 1, -1), ("s_max", 1, 3),
    ("c_turn", 0, 1), ("c_main", 2, 0), ("s_out", 0, 2), ("c_max", 0, 1), ("s_qkv", 0, 4), ("s_sum", 1, 2),
    ("s_shift", 0, 3), ("c_main", 3, 0), ("s_out", 1, 2), ("c_max", 1, 1), ("c_sum", 0, 0),
]
ACT_ORDER = [
    ("s_proj", 0, 1), ("c_high", 2, -1), ("c_keys", 0, 1), ("s_turn", 0, 3), ("s_exp", 0, 2), ("c_log", 0, -2),
    ("s_high", 0, 2), ("s_split", 0, 4), ("c_read", 0, -1), ("c_rsqrt", 0, -2), ("s_exp", 1, 2), ("s_log", 0, 1),
    ("s_rsqrt", 0, 1), ("s_high", 1, 2), ("c_read", 1, -1), ("c_rows", 0, 1), ("c_exp", 0, 0), ("s_read", 0, 2),
    ("c_exp", 1, 0), ("c_turn", 0, 1), ("c_high", 0, 0), ("c_exp", 2, 0), ("c_values", 0, 1), ("s_read", 1, 2),
    ("c_high", 1, 0), ("c_exp", 3, 0), ("s_rows", 0, 4),
]
DVE_ORDER = [
    ("s_den", 1, 1), ("s_out", 0, 1), ("s_out", 1, 1), ("c_max", 1, 0), ("s_rows", 0, 3), ("s_proj", 0, 1),
    ("c_max", 2, 0), ("c_aggr", 0, -2), ("c_keys", 0, 1), ("c_high", 3, -1), ("s_turn", 0, 3), ("c_max", 3, 0),
    ("s_res", 0, 1), ("s_stats", 0, 1), ("s_aggr", 0, 1), ("c_newton", 0, -2), ("c_shift", 0, 0), ("s_newton", 0, 1),
    ("s_newton", 1, 1), ("c_newton", 1, -2), ("s_newton", 2, 1), ("c_newton", 2, -2), ("s_ln", 0, 1), ("s_max", 0, 3),
    ("c_ln", 0, -2), ("c_rows", 0, 1), ("c_den", 0, -1), ("c_den", 1, -1), ("c_out", 0, -1), ("c_out", 1, -1),
    ("s_max", 1, 3), ("c_res", 0, -1), ("s_den", 0, 2), ("c_stats", 0, -1), ("c_max", 0, 1), ("s_bias", 0, 4),
    ("s_shift", 0, 3),
]
POOL_ORDER = [
    ("s_low", 0, 2), ("s_split", 0, 4), ("c_keys", 0, 1), ("s_low", 1, 2), ("c_low", 0, 0), ("x_bias", 0, 2),
    ("c_low", 1, 0), ("c_values", 0, 1), ("c_low", 2, 0), ("c_low", 3, 0), ("net0", 0, 4),
]
SP_ORDER = [
    ("load_xT", 0, 4), ("load_ctx", 0, 2), ("load_base", 0, 2), ("load_x", 0, 2),
]
DELTAS = [d for order in (PE_ORDER, ACT_ORDER, DVE_ORDER, POOL_ORDER, SP_ORDER) for _, _, d in order]
FIRST_STEP, LAST_STEP = -max(DELTAS), B - 1 - min(DELTAS)
UNROLL = 4
LOOP_FROM = 2 - min(DELTAS)
LOOP_STEPS = (B - max(DELTAS) - LOOP_FROM) // UNROLL * UNROLL

SCORE_USE = {"s_max": ("s_max_read", 2), "s_main": ("s_exp", 2), "c_max": ("c_max_read", 4), "c_main": ("c_exp", 4)}
PROB_USE = {"s_exp": ("s_summed", 2), "c_exp": ("c_summed", 4)}
SUM_USE = {"s_sum": ("s_sum_read", 2), "c_sum": ("c_sum_read", 2)}
MISC_USE = {
    "s_qkv": [("s_qkv_read", 1, 1)],
    "s_turn": [("s_q_read", 2, 1), ("s_q_read", 2, 2), ("s_k_read", 1, 1)],
    "s_shift": [("s_shift_read", 1, 1)],
    "s_out": [("s_out_read", 2, None)],
    "s_proj": [("s_ctx_read", 1, 1)],
    "s_res": [("s_res_read", 1, 1)],
    "c_turn": [("c_q_read", 2, 1), ("c_q_read", 2, 2)],
    "c_shift": [("c_shift_read", 1, 1)],
    "c_out": [("c_out_read", 2, None)],
}


class Seq:

    def __init__(self, off, i=None, stride=2):
        self.off, self.i, self.stride = off, i, stride

    def at(self, per, plus=0):
        v = per * self.off + plus
        return v if self.i is None else self.i * (self.stride * per) + v

    def back(self, n):
        return Seq(self.off - n, self.i, self.stride)

    @property
    def odd(self):
        return self.off % 2

    @property
    def exists(self):
        return 0 <= self.off < B if self.i is None else self.off >= 0


def wait(eng, sem, seq, per=1, upto=None):
    assert seq.i is None or seq.exists
    if seq.exists:
        eng.wait_ge(sem, seq.at(per, per if upto is None else upto))


class Ring:

    def __init__(self, slots, uses):
        self.slots, self.uses = slots, uses
        assert 2 * len(uses) % slots == 0

    def _at(self, stage, unit, part):
        return next(n for n, u in enumerate(self.uses) if u[:3] == (stage, unit, part))

    def slot(self, stage, unit, seq, part=0):
        n = self._at(stage, unit, part)
        return ((seq.off - self.uses[n][3]) * len(self.uses) + n) % self.slots

    def wait_free(self, eng, sems, stage, unit, seq, part=0):
        n = self._at(stage, unit, part)
        at = (seq.off - self.uses[n][3]) * len(self.uses) + n
        while True:
            at -= self.slots
            step, m = divmod(at, len(self.uses))
            _, _, _, delta, name, per, upto = self.uses[m]
            if step + delta < -2 * len(self.uses):
                return
            before = Seq(step + delta, seq.i, seq.stride)
            assert seq.i is None or before.exists
            if before.exists:
                eng.wait_ge(sems[name], before.at(per, upto))
                return


def rings():
    score, prob, summed, misc = [], [], [], []
    for stage, unit, delta in ACT_ORDER:
        if stage in PROB_USE:
            name, per = PROB_USE[stage]
            prob.append((stage, unit, 0, delta, name, per, unit + 1))
    for stage, unit, delta in PE_ORDER:
        if stage in SCORE_USE:
            name, per = SCORE_USE[stage]
            score.append((stage, unit, 0, delta, name, per, unit + 1))
        if stage == "s_sum" or stage == "c_sum" and unit % 2 == 0:
            name, per = SUM_USE[stage]
            summed.append((stage, unit, 0, delta, name, per, (unit if stage == "s_sum" else unit // 2) + 1))
        for part, (name, per, upto) in enumerate(MISC_USE.get(stage, [])):
            misc.append((stage, unit, part, delta, name, per, unit + 1 if upto is None else upto))
    return Ring(2, score), Ring(4, prob), Ring(2, summed), Ring(2, misc)


def decoder_layer(nc, x, xT, ctx, ctxT, wqkvT, bqkv, woT, bo, gate_w, base_gu, base_down, exp_gu, exp_down, consts, out):
    with ExitStack() as both:
        def sb(name, shape, dt=F32, scope=both):
            return scope.enter_context(nc.sbuf_tensor(name, shape, dt))

        stream = sb("stream", [P, B, D])
        raw_gu0, raw_down0 = sb("raw_gu0", [P, 2, 2 * INNER]), sb("raw_down0", [P, INNER // P, D])
        gu_hi0, gu_lo0 = sb("gu_hi0", [P, 2, 2 * INNER], F32R), sb("gu_lo0", [P, 2, 2 * INNER], F32R)
        down_hi0, down_lo0 = sb("down_hi0", [P, INNER // P, D], F32R), sb("down_lo0", [P, INNER // P, D], F32R)
        ident = sb("ident", [P, P])
        eps = sb("eps", [P, 1])
        raw_gate, descending = sb("raw_gate", [P, 2, EXPERTS]), sb("descending", [P, EXPERTS])
        gate_hi, gate_lo = sb("gate_hi", [P, 2, EXPERTS], F32R), sb("gate_lo", [P, 2, EXPERTS], F32R)
        router = (raw_gate, gate_hi, gate_lo, descending)
        raw_loaded = [both.enter_context(nc.semaphore(f"raw_loaded{p}")) for p in range(2)]
        gu_split = both.enter_context(nc.semaphore("gu_split"))
        down_split = both.enter_context(nc.semaphore("down_split"))
        weights0 = (raw_gu0, raw_down0, gu_hi0, gu_lo0, down_hi0, down_lo0, raw_loaded, gu_split, down_split)
        attention(nc, x, xT, ctx, ctxT, wqkvT, bqkv, woT, bo, consts, stream, ident, eps, base_gu, base_down,
                  gate_w, router, weights0)
        experts(nc, exp_gu, exp_down, stream, ident, eps, router, weights0, out)


def load_net(eng, net, raw_gu, raw_down, loaded, gu, down):
    g = gu if net is None else gu[bass.ds(net, 1)].squeeze(0) if not isinstance(net, int) else gu[net]
    d = down if net is None else down[bass.ds(net, 1)].squeeze(0) if not isinstance(net, int) else down[net]
    eng.dma_start(raw_gu[:], g.rearrange("(k p) n -> p k n", p=P)).then_inc(loaded, 16)
    eng.dma_start(raw_down[:], d.rearrange("(k p) n -> p k n", p=P)).then_inc(loaded, 16)


def attention(nc, x, xT, ctx, ctxT, wqkvT, bqkv, woT, bo, consts, stream, ident, eps, base_gu, base_down,
              gate_w, router, weights0):
    raw_gate, gate_hi, gate_lo, descending = router
    raw_gu0, raw_down0, gu_hi0, gu_lo0, down_hi0, down_lo0, raw_loaded, gu_split, down_split = weights0
    score_ring, prob_ring, sum_ring, misc_ring = rings()
    with ExitStack() as scope:
        def sb(name, shape, dt=F32):
            return scope.enter_context(nc.sbuf_tensor(name, shape, dt))

        def two(name, shape, dt=F32):
            return [sb(f"{name}{p}", shape, dt) for p in range(2)]

        scores = scope.enter_context(nc.psum_tensor("scores", [P, 2, 1024], F32))
        sums = scope.enter_context(nc.psum_tensor("sums", [P, 2, 512], F32))
        misc = scope.enter_context(nc.psum_tensor("misc", [P, 2, 512], F32))

        cst = sb("cst", [P, CONST_COLS - EXPERTS])
        ident_r, ident_b = sb("ident_r", [P, P], F32R), sb("ident_b", [P, P], BF16)
        mask_qk, mask_kq = sb("mask_qk", [P, 4, P], BF16), sb("mask_kq", [P, 4, P], BF16)
        blk_s, blk_c = cst[:, 3 * P:3 * P + 2], cst[:, 3 * P + 2:3 * P + 6]
        neg_s, neg_c = cst[0:32, 3 * P + 6:3 * P + 14], cst[0:32, 3 * P + 14:3 * P + 22]
        raw_wqkv, raw_wo = sb("raw_wqkv", [P, 2, QKV]), sb("raw_wo", [P, 2, D])
        wqkv_hi, wqkv_lo = sb("wqkv_hi", [P, 2, QKV], F32R), sb("wqkv_lo", [P, 2, QKV], F32R)
        wo_hi, wo_lo = sb("wo_hi", [P, 2, D], F32R), sb("wo_lo", [P, 2, D], F32R)
        b_qkv, b_o = sb("b_qkv", [P, QKV]), sb("b_o", [P, D])

        xT_in, x_in = two("xT_in", [P, 2, S]), two("x_in", [P, D])
        ctxT_in, ctx_in = two("ctxT_in", [96, 2, S]), two("ctx_in", [P, XKV * XD])
        xT_hi, xT_lo = two("xT_hi", [P, 2, S], F32R), two("xT_lo", [P, 2, S], F32R)
        x_bias = two("x_bias", [P, D])

        qkv = sb("qkv", [P, QKV])
        rows_s = sb("rows_s", [P, 9, 96], F32R)
        q_s = two("q_s", [P, 8, S], F32R)
        k_s = two("k_s", [P, 2, S], F32R)
        v_s = two("v_s", [P, 2, 192], F32R)
        max_s = sb("max_s", [P, 32])
        sumT_s = sb("sumT_s", [P, 2, 512])
        rden_s = sb("rden_s", [P, 2, 8])
        raw_s = sb("raw_s", [P, 2, 8, HD])
        ctx_s = two("ctx_s", [P, D])
        ctxT_hi, ctxT_lo = sb("ctxT_hi", [P, 2, S], F32R), sb("ctxT_lo", [P, 2, S], F32R)
        pre1, x1 = two("pre1_", [P, D]), [sb(f"x1_{p}", [P, D]) for p in range(UNROLL)]

        rows_c = sb("rows_c", [P, 8, 96], F32R)
        q_c = two("q_c", [P, 8, S], F32R)
        k_split = sb("k_split", [96, 2, S], F32R)
        k_c = two("k_c", [P, 2, 4, S], F32R)
        v_c = two("v_c", [P, 2, 640], F32R)
        max_c = sb("max_c", [P, 32])
        sumT_c = sb("sumT_c", [P, 2, 512])
        rden_c = sb("rden_c", [P, 2, 16])
        raw_c = sb("raw_c", [P, 2, 4, 4, XD])
        ctx_c = sb("ctx_c", [P, D])
        pre2 = two("pre2_", [P, D])

        prob, prob_hi, prob_lo = sb("prob", [P, 4, 1024]), sb("prob_hi", [P, 4, 1024], F32R), sb("prob_lo", [P, 4, 1024], F32R)
        norm = {k: dict(stats=sb(f"stats_{k}", [P, 6]), mv=sb(f"mv_{k}", [P, 2]), ln=sb(f"ln_{k}", [P, 1]),
                        r=sb(f"r_{k}", [P, 1]), t=sb(f"t_{k}", [P, 3])) for k in "sc"}

        names = """consts_loaded gate_loaded weights_loaded w_hi w_split wo_split tables values_set
            xT_hi_set xT_split x_biased s_qkv_full s_qkv_read s_rows_hi s_rows_lo s_q_full s_q_read s_k_full s_k_read
            s_max_full s_max_read s_shift_full s_shift_read s_main_full s_exp s_prob_hi s_prob_lo s_summed s_sum_read
            s_out_full s_out_read s_ctx s_ctx_full s_ctx_hi s_ctx_read s_res_full s_res_read s_stats s_mv s_ln s_rsqrt0
            s_newton x1_set
            ctx_k_hi ctx_k_lo ctx_k_set ctx_v_hi ctx_v_set c_rows_hi c_rows_lo c_q_full c_q_read c_max_full c_max_read c_shift_full
            c_shift_read c_main_full c_exp c_prob_hi c_prob_hi3 c_prob_lo c_summed c_sum_read c_out_full c_out_read c_ctx c_res
            c_stats c_mv c_ln c_rsqrt0 c_newton x2_set net0_hi""".split()
        sem = {n: scope.enter_context(nc.semaphore(n)) for n in names}
        xT_loaded = [scope.enter_context(nc.semaphore(f"xT_loaded{p}")) for p in range(2)]
        x_loaded = [scope.enter_context(nc.semaphore(f"x_loaded{p}")) for p in range(2)]
        ctx_loaded = [scope.enter_context(nc.semaphore(f"ctx_loaded{p}")) for p in range(2)]

        wo_loaded = scope.enter_context(nc.semaphore("wo_loaded"))

        def f32(ap):
            return ap.bitcast(F32)

        def run(eng, order, stages):
            def step(s, i=None):
                for stage, unit, delta in order:
                    seq = Seq(s + delta, i, UNROLL)
                    if seq.exists:
                        stages[stage](seq, unit)
            for s in range(FIRST_STEP, LOOP_FROM):
                step(s)
            with eng.Fori(0, LOOP_STEPS // UNROLL) as i:
                for u in range(UNROLL):
                    step(LOOP_FROM + u, i)
            for s in range(LOOP_FROM + LOOP_STEPS, LAST_STEP + 1):
                step(s)

        def wait_loaded(eng, sems, seq, loads=1):
            v = 16 * loads * (seq.off // 2 + 1)
            eng.wait_ge(sems[seq.odd], v if seq.i is None else seq.i * (8 * loads * seq.stride) + v)

        def high_part(eng, k, seq, unit):
            m = prob_ring.slot(f"{k}_exp", unit, seq)
            wait(eng, sem[f"{k}_exp"], seq, {"s": 2, "c": 4}[k], unit + 1)
            if (k, unit) == ("c", 3):
                eng.tensor_copy(prob_hi[:, m, :], prob[:, m, :]).then_inc(sem["c_prob_hi3"], 1)
            else:
                eng.copy(prob_hi[:, m, :], prob[:, m, :]).then_inc(sem[f"{k}_prob_hi"], 1)

        def wait_high(eng, k, seq, unit):
            if (k, unit) == ("c", 3):
                wait(eng, sem["c_prob_hi3"], seq)
            else:
                wait(eng, sem[f"{k}_prob_hi"], seq, {"s": 2, "c": 3}[k], unit + 1)

        block = scope.enter_context(nc.Block())

        @block.sync
        def _(sp):
            sp.dma_start(raw_wqkv[:], wqkvT.rearrange("(k p) n -> p k n", p=P)).then_inc(sem["weights_loaded"], 16)
            sp.dma_start(cst[:], consts[:, 0:CONST_COLS - EXPERTS]).then_inc(sem["consts_loaded"], 16)
            sp.dma_start(b_qkv[:], bqkv.partition_broadcast(P)).then_inc(sem["weights_loaded"], 16)

            def load_wo():
                sp.dma_start(raw_wo[:], woT.rearrange("(k p) n -> p k n", p=P)).then_inc(wo_loaded, 16)
                sp.dma_start(b_o[:], bo.partition_broadcast(P)).then_inc(wo_loaded, 16)

            def load_xT(seq, unit):
                tokens = bass.ds(seq.at(S), S)
                wait(sp, sem["xT_split"], seq.back(2))
                sp.dma_start(xT_in[seq.odd][:], xT.rearrange("(k p) t -> p k t", p=P)[:, :, tokens])\
                    .then_inc(xT_loaded[seq.odd], 16)
                if seq.i is None and seq.off == 0:
                    load_wo()

            def load_x(seq, unit):
                tokens = bass.ds(seq.at(S), S)
                wait(sp, sem["x_biased"], seq.back(2))
                sp.dma_start(x_in[seq.odd][:], x[tokens, :]).then_inc(x_loaded[seq.odd], 16)

            def load_ctx(seq, unit):
                tokens = bass.ds(seq.at(S), S)
                wait(sp, sem["ctx_k_lo"], seq.back(2))
                wait(sp, sem["ctx_v_set"], seq.back(2))
                sp.dma_start(ctxT_in[seq.odd][:], ctxT[:, :, tokens]).then_inc(ctx_loaded[seq.odd], 16)
                sp.dma_start(ctx_in[seq.odd][:], ctx[tokens, :]).then_inc(ctx_loaded[seq.odd], 16)

            def load_base(seq, unit):
                if seq.i is None and seq.off == 0:
                    load_net(sp, None, raw_gu0, raw_down0, raw_loaded[0], base_gu, base_down)
                    sp.dma_start(raw_gate[:], gate_w.rearrange("(k p) n -> p k n", p=P)).then_inc(sem["gate_loaded"], 16)
                    sp.dma_start(descending[:], consts[:, CONST_COLS - EXPERTS:]).then_inc(sem["gate_loaded"], 16)

            run(sp, SP_ORDER, dict(load_xT=load_xT, load_x=load_x, load_ctx=load_ctx, load_base=load_base))

        @block.gpsimd
        def _(pool):
            for p in range(2):
                pool.memset(f32(v_s[p][:]), 0.0)
                zero = pool.memset(f32(v_c[p][:]), 0.0)
            zero.then_inc(sem["values_set"], 1)
            pool.wait_ge(sem["values_set"], 1)
            for p in range(2):
                pool.memset(f32(v_s[p][:, :, HD:HD + 1]), 1.0)
                one = pool.memset(f32(v_c[p][:].rearrange("p a (j s) -> p a j s", j=4)[:, :, :, XD:XD + 1]), 1.0)
            one.then_inc(sem["values_set"], 1)
            def s_split(seq, unit):
                p = seq.odd
                wait(pool, sem["xT_hi_set"], seq)
                pool.tensor_tensor(xT_lo[p][:], xT_in[p][:], f32(xT_hi[p][:]), ALU.subtract).then_inc(sem["xT_split"], 1)
                if seq.i is None and seq.off == 0:
                    pool.wait_ge(sem["w_hi"], 2)
                    pool.tensor_tensor(wo_lo[:], raw_wo[:], f32(wo_hi[:]), ALU.subtract).then_inc(sem["wo_split"], 1)

            def s_low(seq, unit):
                n = prob_ring.slot("s_exp", unit, seq)
                wait_high(pool, "s", seq, unit)
                pool.tensor_tensor(prob_lo[:, n, :], prob[:, n, :], f32(prob_hi[:, n, :]), ALU.subtract).then_inc(sem["s_prob_lo"], 1)

            def bias(seq, unit):
                p = seq.odd
                wait_loaded(pool, x_loaded, seq)
                if seq.i is None and seq.off == 0:
                    pool.wait_ge(wo_loaded, 32)
                wait(pool, sem["s_res_read"], seq.back(2))
                pool.tensor_tensor(x_bias[p][:], x_in[p][:], b_o[:], ALU.add).then_inc(sem["x_biased"], 1)

            def c_low(seq, unit):
                n = prob_ring.slot("c_exp", unit, seq)
                wait_high(pool, "c", seq, unit)
                pool.tensor_tensor(prob_lo[:, n, :], prob[:, n, :], f32(prob_hi[:, n, :]), ALU.subtract).then_inc(sem["c_prob_lo"], 1)

            def c_keys(seq, unit):
                p = seq.odd
                wait(pool, sem["ctx_k_lo"], seq)
                wait(pool, sem["c_main_full"], seq.back(2), 4)
                for a in range(2):
                    ins = pool.tensor_tensor(
                        k_c[p][0:96, a], f32(k_split[:, a, :]).unsqueeze(1).broadcast_to([96, 4, S]),
                        blk_c[0:96].unsqueeze(2).broadcast_to([96, 4, S]), ALU.mult)
                ins.then_inc(sem["ctx_k_set"], 1)

            def c_values(seq, unit):
                p = seq.odd
                place = v_c[p][:].rearrange("p a (j s) -> p a j s", j=4)
                wait(pool, sem["ctx_v_hi"], seq)
                pool.tensor_tensor(place[:, :, :, XD + 1:2 * XD + 1], ctx_in[p][:].rearrange("p (a j d) -> p a j d", a=2, j=4),
                                   f32(place[:, :, :, 0:XD]), ALU.subtract).then_inc(sem["ctx_v_set"], 1)

            def net0(seq, unit):
                if seq.i is not None or seq.off >= 4:
                    return
                k = seq.off % 2
                hi, lo, raw = ((gu_hi0[:, k, :], gu_lo0[:, k, :], raw_gu0[:, k, :]) if seq.off < 2 else
                               (down_hi0[:, 2 * k:2 * k + 2], down_lo0[:, 2 * k:2 * k + 2], raw_down0[:, 2 * k:2 * k + 2]))
                pool.wait_ge(raw_loaded[0], 32)
                pool.tensor_scalar(hi, raw, 1.0, None, ALU.mult).then_inc(sem["net0_hi"], 1)
                pool.wait_ge(sem["net0_hi"], seq.off + 1)
                low = pool.tensor_tensor(lo, raw, f32(hi), ALU.subtract)
                if k:
                    low.then_inc(gu_split if seq.off < 2 else down_split, 1)
                if seq.off == 3:
                    pool.wait_ge(sem["gate_loaded"], 32)
                    pool.tensor_scalar(gate_hi[:], raw_gate[:], 1.0, None, ALU.mult).then_inc(sem["net0_hi"], 1)
                    pool.wait_ge(sem["net0_hi"], 5)
                    pool.tensor_tensor(gate_lo[:], raw_gate[:], f32(gate_hi[:]), ALU.subtract)

            run(pool, POOL_ORDER, dict(s_split=s_split, net0=net0, x_bias=bias, s_low=s_low, c_low=c_low, c_keys=c_keys, c_values=c_values))

        @block.scalar
        def _(act):
            def c_keys(seq, unit):
                p = seq.odd
                wait_loaded(act, ctx_loaded, seq, 2)
                wait(act, sem["ctx_k_set"], seq.back(1))
                act.copy(k_split[:], ctxT_in[p][:]).then_inc(sem["ctx_k_hi"], 1)

            def c_values(seq, unit):
                p = seq.odd
                wait_loaded(act, ctx_loaded, seq, 2)
                wait(act, sem["c_summed"], seq.back(2), 4)
                act.copy(v_c[p][:].rearrange("p a (j s) -> p a j s", j=4)[:, :, :, 0:XD],
                         ctx_in[p][:].rearrange("p (a j d) -> p a j d", a=2, j=4)).then_inc(sem["ctx_v_hi"], 1)

            def s_split(seq, unit):
                p = seq.odd
                wait_loaded(act, xT_loaded, seq)
                wait(act, sem["s_qkv_full"], seq.back(2))
                act.copy(xT_hi[p][:], xT_in[p][:]).then_inc(sem["xT_hi_set"], 1)
                if seq.i is None and seq.off == 0:
                    act.wait_ge(wo_loaded, 32)
                    act.copy(wo_hi[:], raw_wo[:]).then_inc(sem["w_hi"], 1)

            def s_rows(seq, unit):
                p = seq.odd
                wait(act, sem["s_qkv_read"], seq)
                wait(act, sem["s_k_full"], seq.back(1))
                wait(act, sem["s_summed"], seq.back(2), 2)
                q = qkv[:, 0:D].rearrange("p (n c) -> p n c", c=32)
                act.copy(rows_s[:, 0:8, 0:32], q)
                act.copy(rows_s[:, 0:8, 64:96], q)
                act.copy(rows_s[:, 8, 0:64].rearrange("p (r d) -> p r d", d=HD), qkv[:, D:D + HD].unsqueeze(1).broadcast_to([P, 4, HD]))
                act.copy(v_s[p][:, :, 0:HD], qkv[:, D + HD:QKV].unsqueeze(1).broadcast_to([P, 2, HD])).then_inc(sem["s_rows_hi"], 1)

            def s_turn(seq, unit):
                wait(act, sem["s_main_full"], seq.back(2), 2)
                for u in range(2):
                    n = misc_ring.slot("s_turn", 0, seq, u)
                    wait(act, sem["s_q_full"], seq, 2, u + 1)
                    act.copy(q_s[seq.odd][0:96, 4 * u:4 * u + 4, :], misc[0:96, n, :].rearrange("p (n t) -> p n t", n=4))\
                        .then_inc(sem["s_q_read"], 1)

            def exp_unit(stage, scores_stage, unit, seq, per, scale, full, exped):
                n, m = score_ring.slot(scores_stage, unit, seq), prob_ring.slot(stage, unit, seq)
                wait(act, sem[full], seq, per, unit + 1)
                prob_ring.wait_free(act, sem, stage, unit, seq)
                act.activation(prob[:, m, :], scores[:, n, :], ACT.Exp, scale=scale).then_inc(sem[exped], 1)

            def s_exp(seq, unit):
                exp_unit("s_exp", "s_main", unit, seq, 2, SCALE_S, "s_main_full", "s_exp")

            def c_exp(seq, unit):
                exp_unit("c_exp", "c_main", unit, seq, 4, SCALE_X, "c_main_full", "c_exp")

            def s_high(seq, unit):
                high_part(act, "s", seq, unit)

            def c_high(seq, unit):
                high_part(act, "c", seq, unit)

            def s_read(seq, unit):
                n = sum_ring.slot("s_sum", unit, seq)
                wait(act, sem["s_summed"], seq, 2, unit + 1)
                wait(act, sem["s_out_full"], seq.back(1), 2, unit + 1)
                act.copy(sumT_s[:, unit, :], sums[:, n, :]).then_inc(sem["s_sum_read"], 1)

            def c_read(seq, a):
                n = sum_ring.slot("c_sum", 2 * a, seq)
                wait(act, sem["c_summed"], seq, 4, 2 * a + 2)
                wait(act, sem["c_out_full"], seq.back(1), 2, a + 1)
                act.copy(sumT_c[:, a, :], sums[:, n, :]).then_inc(sem["c_sum_read"], 1)

            def s_proj(seq, unit):
                n = misc_ring.slot("s_proj", 0, seq)
                wait(act, sem["s_ctx_full"], seq)
                wait(act, sem["s_res_full"], seq.back(1))
                act.copy(ctxT_hi[:], misc[:, n, 0:2 * S].rearrange("p (k t) -> p k t", k=2)).then_inc(sem["s_ctx_hi"], 1)

            def log(k, seq):
                wait(act, sem[f"{k}_mv"], seq)
                wait(act, sem[f"{k}_rsqrt0"], seq.back(1))
                act.activation(norm[k]["ln"][:], norm[k]["mv"][:, 1:2], ACT.Ln, bias=eps[:]).then_inc(sem[f"{k}_ln"], 1)

            def rsqrt(k, seq):
                wait(act, sem[f"{k}_ln"], seq)
                wait(act, sem[f"{k}_newton"], seq.back(1), 3)
                act.activation(norm[k]["r"][:], norm[k]["ln"][:], ACT.Exp, scale=-0.5).then_inc(sem[f"{k}_rsqrt0"], 1)

            def s_log(seq, unit):
                log("s", seq)

            def s_rsqrt(seq, unit):
                rsqrt("s", seq)

            def c_log(seq, unit):
                log("c", seq)

            def c_rsqrt(seq, unit):
                rsqrt("c", seq)

            def c_rows(seq, unit):
                wait(act, sem["x1_set"], seq)
                wait(act, sem["c_q_full"], seq.back(1), 2)
                for part in (0, 2):
                    for a in range(2):
                        ins = act.copy(
                            rows_c[:, 4 * a:4 * a + 4, 32 * part:32 * part + 32].rearrange("p g (j d) -> p g j d", j=4),
                            x1[seq.off % UNROLL][:, P * a:P * a + P].rearrange("p (j g d) -> p g j d", j=4, g=4))
                ins.then_inc(sem["c_rows_hi"], 1)

            def c_turn(seq, unit):
                wait(act, sem["c_main_full"], seq.back(2), 4)
                for u in range(2):
                    n = misc_ring.slot("c_turn", 0, seq, u)
                    wait(act, sem["c_q_full"], seq, 2, u + 1)
                    act.copy(q_c[seq.odd][0:96, 4 * u:4 * u + 4, :], misc[0:96, n, :].rearrange("p (n t) -> p n t", n=4))\
                        .then_inc(sem["c_q_read"], 1)

            act.preload_act_table_set("natural_log_exp_and_others")
            act.wait_ge(sem["weights_loaded"], 32)
            act.copy(wqkv_hi[:], raw_wqkv[:]).then_inc(sem["w_hi"], 1)
            act.wait_ge(sem["tables"], 1)
            act.wait_ge(sem["values_set"], 2)
            run(act, ACT_ORDER, dict(s_split=s_split, s_rows=s_rows, s_turn=s_turn, s_exp=s_exp, s_high=s_high, s_read=s_read,
                                     s_proj=s_proj, s_log=s_log, s_rsqrt=s_rsqrt, c_keys=c_keys, c_values=c_values, c_rows=c_rows,
                                     c_turn=c_turn, c_exp=c_exp, c_high=c_high, c_read=c_read, c_log=c_log, c_rsqrt=c_rsqrt))

        @block.vector
        def _(dve):
            dve.memset(max_s[:], 0.0)
            dve.memset(eps[:], EPS).then_inc(sem["tables"], 1)
            dve.wait_ge(sem["consts_loaded"], 16)
            dve.tensor_copy(ident_r[:], cst[:, 0:P]).then_inc(sem["tables"], 1)
            dve.wait_ge(sem["w_hi"], 1)
            dve.tensor_tensor(wqkv_lo[:], raw_wqkv[:], f32(wqkv_hi[:]), ALU.subtract).then_inc(sem["w_split"], 1)
            dve.tensor_copy(ident[:], cst[:, 0:P])
            dve.tensor_copy(ident_b[:], cst[:, 0:P])
            dve.tensor_copy(mask_qk[:], cst[:, P:2 * P].unsqueeze(1).broadcast_to([P, 4, P]))
            dve.tensor_copy(mask_kq[:], cst[:, 2 * P:3 * P].unsqueeze(1).broadcast_to([P, 4, P]))
            for p in range(2):
                dve.tensor_copy(k_s[p][96:128], blk_s[96:128].unsqueeze(2).broadcast_to([32, 2, S]))
                for a in range(2):
                    ins = dve.tensor_copy(k_c[p][96:128, a], blk_c[96:128].unsqueeze(2).broadcast_to([32, 4, S]))
            ins.then_inc(sem["tables"], 1)

            def s_bias(seq, unit):
                n = misc_ring.slot("s_qkv", 0, seq)
                wait(dve, sem["s_qkv_full"], seq)
                wait(dve, sem["s_rows_lo"], seq.back(1))
                dve.tensor_tensor(qkv[:], misc[:, n, 0:QKV], b_qkv[:], ALU.add).then_inc(sem["s_qkv_read"], 1)

            def s_rows(seq, unit):
                p = seq.odd
                wait(dve, sem["s_rows_hi"], seq)
                dve.tensor_tensor(rows_s[:, 0:8, 32:64], qkv[:, 0:D].rearrange("p (n c) -> p n c", c=32),
                                  f32(rows_s[:, 0:8, 0:32]), ALU.subtract)
                dve.tensor_tensor(rows_s[:, 8, 64:96].rearrange("p (r d) -> p r d", d=HD),
                                  qkv[:, D:D + HD].unsqueeze(1).broadcast_to([P, 2, HD]),
                                  f32(rows_s[:, 8, 0:32]).rearrange("p (r d) -> p r d", d=HD), ALU.subtract)
                dve.tensor_tensor(v_s[p][:, :, HD + 1:2 * HD + 1], qkv[:, D + HD:QKV].unsqueeze(1).broadcast_to([P, 2, HD]),
                                  f32(v_s[p][:, :, 0:HD]), ALU.subtract).then_inc(sem["s_rows_lo"], 1)

            def s_turn(seq, unit):
                n = misc_ring.slot("s_turn", 0, seq, 2)
                wait(dve, sem["s_k_full"], seq)
                wait(dve, sem["s_main_full"], seq.back(2), 2)
                dve.tensor_tensor(k_s[seq.odd][0:96], misc[0:96, n, 0:S].unsqueeze(1).broadcast_to([96, 2, S]),
                                  blk_s[0:96].unsqueeze(2).broadcast_to([96, 2, S]), ALU.mult).then_inc(sem["s_k_read"], 1)

            def row_max(stage, unit, seq, per, full, read, out_, shifted):
                n = score_ring.slot(stage, unit, seq)
                wait(dve, sem[full], seq, per, unit + 1)
                if unit == 0:
                    wait(dve, sem[shifted], seq.back(1))
                dve.tensor_reduce(out_[:, 8 * unit:8 * unit + 8], scores[:, n, :].rearrange("p (h k) -> p h k", k=S),
                                  AX.X, ALU.max).then_inc(sem[read], 1)

            def s_max(seq, unit):
                row_max("s_max", unit, seq, 2, "s_max_full", "s_max_read", max_s, "s_shift_full")

            def c_max(seq, unit):
                row_max("c_max", unit, seq, 4, "c_max_full", "c_max_read", max_c, "c_shift_full")

            def shift_rows(stage, seq, q, neg, full, read):
                n = misc_ring.slot(stage, 0, seq)
                wait(dve, sem[full], seq)
                dve.tensor_tensor(q[seq.odd][96:128], misc[0:32, n, 0:S].unsqueeze(1).broadcast_to([32, 8, S]),
                                  neg.unsqueeze(2).broadcast_to([32, 8, S]), ALU.mult).then_inc(sem[read], 1)

            def s_shift(seq, unit):
                shift_rows("s_shift", seq, q_s, neg_s, "s_shift_full", "s_shift_read")

            def c_shift(seq, unit):
                shift_rows("c_shift", seq, q_c, neg_c, "c_shift_full", "c_shift_read")

            def s_den(seq, b):
                n = misc_ring.slot("s_out", b, seq)
                part = misc[:, n, :].rearrange("p (i h s) -> p i h s", i=4, h=2)
                wait(dve, sem["s_out_full"], seq, 2, b + 1)
                wait(dve, sem["s_ctx"], seq.back(1), 2, b + 1)
                dve.reciprocal(rden_s[:, b, :].rearrange("p (h i) -> p i h", h=2), part[:, :, :, HD:HD + 1].squeeze(3))
                both_parts = part[:, :, :, 0:2 * (HD + 1)].rearrange("p i h (two d) -> p i h d two", two=2)[:, :, :, 0:HD, :]
                dve.tensor_reduce(raw_s[:, b].rearrange("p (h i) d -> p i h d", h=2), both_parts, AX.X, ALU.add)\
                    .then_inc(sem["s_out_read"], 1)

            def s_out(seq, b):
                wait(dve, sem["s_out_read"], seq, 2, b + 1)
                wait(dve, sem["s_ctx_full"], seq.back(2))
                dve.tensor_tensor(ctx_s[seq.odd][:].rearrange("p (n b d) -> p n b d", b=2, d=HD)[:, :, b, :], raw_s[:, b],
                                  rden_s[:, b, :].unsqueeze(2).broadcast_to([P, 8, HD]), ALU.mult).then_inc(sem["s_ctx"], 1)

            def c_high(seq, unit):
                high_part(dve, "c", seq, unit)

            def s_proj(seq, unit):
                n = misc_ring.slot("s_proj", 0, seq)
                wait(dve, sem["s_ctx_hi"], seq)
                dve.tensor_tensor(ctxT_lo[:], misc[:, n, 0:2 * S].rearrange("p (k t) -> p k t", k=2), f32(ctxT_hi[:]),
                                  ALU.subtract).then_inc(sem["s_ctx_read"], 1)

            def s_res(seq, unit):
                n = misc_ring.slot("s_res", 0, seq)
                wait(dve, sem["s_res_full"], seq)
                wait(dve, sem["x_biased"], seq)
                wait(dve, sem["x1_set"], seq.back(2))
                dve.tensor_tensor(pre1[seq.odd][:], misc[:, n, 0:D], x_bias[seq.odd][:], ALU.add).then_inc(sem["s_res_read"], 1)

            def s_stats(seq, unit):
                wait(dve, sem["s_res_read"], seq)
                stats("s", seq, pre1[seq.odd])

            def c_stats(seq, unit):
                wait(dve, sem["c_res"], seq)
                stats("c", seq, pre2[seq.odd])

            def stats(k, seq, pre):
                wait(dve, sem[f"{k}_mv"], seq.back(1))
                dve.bn_stats(norm[k]["stats"][:], pre[:]).then_inc(sem[f"{k}_stats"], 1)

            def s_aggr(seq, unit):
                mean_var("s", seq)

            def c_aggr(seq, unit):
                mean_var("c", seq)

            def mean_var(k, seq):
                wait(dve, sem[f"{k}_newton"], seq.back(1), 3)
                wait(dve, sem[f"{k}_ln"], seq.back(1))
                wait(dve, sem["x1_set" if k == "s" else "x2_set"], seq.back(1))
                wait(dve, sem[f"{k}_stats"], seq)
                dve.memset(norm[k]["t"][:, 0:1], 0.0)
                dve.bn_aggr(norm[k]["mv"][:], norm[k]["stats"][:]).then_inc(sem[f"{k}_mv"], 1)

            def newton(k, seq, unit):
                r, t, mv, done = norm[k]["r"], norm[k]["t"], norm[k]["mv"], sem[f"{k}_newton"]
                if unit == 0:
                    wait(dve, sem[f"{k}_rsqrt0"], seq)
                    wait(dve, sem["x1_set" if k == "s" else "x2_set"], seq.back(1))
                    dve.tensor_scalar(t[:, 0:1], mv[:, 1:2], EPS, r[:], ALU.add, ALU.mult).then_inc(done, 1)
                elif unit == 1:
                    wait(dve, done, seq, 3, 1)
                    dve.tensor_scalar(t[:, 1:2], t[:, 0:1], r[:], -0.5, ALU.mult, ALU.mult).then_inc(done, 1)
                else:
                    wait(dve, done, seq, 3, 2)
                    dve.scalar_tensor_tensor(t[:, 2:3], t[:, 1:2], 1.5, r[:], ALU.add, ALU.mult).then_inc(done, 1)

            def s_newton(seq, unit):
                newton("s", seq, unit)

            def c_newton(seq, unit):
                newton("c", seq, unit)

            def s_ln(seq, unit):
                wait(dve, sem["s_newton"], seq, 3)
                if seq.i is not None or seq.off >= UNROLL:
                    wait(dve, sem["c_res"], seq.back(UNROLL))
                dve.tensor_scalar(x1[seq.off % UNROLL][:], pre1[seq.odd][:], norm["s"]["mv"][:, 0:1], norm["s"]["t"][:, 2:3],
                                  ALU.subtract, ALU.mult).then_inc(sem["x1_set"], 1)

            def c_keys(seq, unit):
                p = seq.odd
                wait(dve, sem["ctx_k_hi"], seq)
                dve.tensor_tensor(k_split[64:96], ctxT_in[p][64:96], f32(k_split[64:96]), ALU.subtract).then_inc(sem["ctx_k_lo"], 1)

            def c_rows(seq, unit):
                wait(dve, sem["c_rows_hi"], seq)
                for a in range(2):
                    ins = dve.tensor_tensor(
                        rows_c[:, 4 * a:4 * a + 4, 32:64].rearrange("p g (j d) -> p g j d", j=4),
                        x1[seq.off % UNROLL][:, P * a:P * a + P].rearrange("p (j g d) -> p g j d", j=4, g=4),
                        f32(rows_c[:, 4 * a:4 * a + 4, 0:32]).rearrange("p g (j d) -> p g j d", j=4), ALU.subtract)
                ins.then_inc(sem["c_rows_lo"], 1)

            def c_den(seq, a):
                n = misc_ring.slot("c_out", a, seq)
                part = misc[:, n, :].rearrange("p (g j s) -> p g j s", g=4, j=4)
                wait(dve, sem["c_out_full"], seq, 2, a + 1)
                wait(dve, sem["c_ctx"], seq.back(1), 2, a + 1)
                dve.reciprocal(rden_c[:, a, :].rearrange("p (g j) -> p g j", g=4), part[:, :, :, XD:XD + 1].squeeze(3))
                both_parts = part[:, :, :, 0:2 * (XD + 1)].rearrange("p g j (two d) -> p g j d two", two=2)[:, :, :, 0:XD, :]
                dve.tensor_reduce(raw_c[:, a], both_parts, AX.X, ALU.add).then_inc(sem["c_out_read"], 1)

            def c_out(seq, a):
                wait(dve, sem["c_out_read"], seq, 2, a + 1)
                wait(dve, sem["c_res"], seq.back(1))
                dve.tensor_tensor(ctx_c[:, P * a:P * a + P].rearrange("p (j g d) -> p g j d", j=4, g=4), raw_c[:, a],
                                  rden_c[:, a, :].rearrange("p (g j) -> p g j", g=4).unsqueeze(3).broadcast_to([P, 4, 4, XD]),
                                  ALU.mult).then_inc(sem["c_ctx"], 1)

            def c_res(seq, unit):
                wait(dve, sem["c_ctx"], seq, 2)
                wait(dve, sem["x1_set"], seq)
                wait(dve, sem["x2_set"], seq.back(2))
                dve.tensor_tensor(pre2[seq.odd][:], ctx_c[:], x1[seq.off % UNROLL][:], ALU.add).then_inc(sem["c_res"], 1)

            def c_ln(seq, unit):
                wait(dve, sem["c_newton"], seq, 3)
                dve.tensor_scalar(stream[:, bass.ds(seq.at(1), 1), :].squeeze(1), pre2[seq.odd][:], norm["c"]["mv"][:, 0:1],
                                  norm["c"]["t"][:, 2:3], ALU.subtract, ALU.mult).then_inc(sem["x2_set"], 1)

            dve.wait_ge(sem["values_set"], 2)
            dve.wait_ge(sem["weights_loaded"], 32)
            run(dve, DVE_ORDER, dict(c_high=c_high, s_bias=s_bias, s_rows=s_rows, s_turn=s_turn, s_max=s_max, s_shift=s_shift, s_out=s_out,
                                     s_proj=s_proj, s_res=s_res, s_ln=s_ln, c_keys=c_keys, c_rows=c_rows, c_max=c_max,
                                     c_shift=c_shift, c_out=c_out, c_res=c_res, c_ln=c_ln, s_den=s_den, c_den=c_den, s_stats=s_stats,
                                     c_stats=c_stats, s_aggr=s_aggr, c_aggr=c_aggr, s_newton=s_newton, c_newton=c_newton))

        @block.tensor
        def _(pe):
            def three(out_, a_hi, a_lo, w_hi, w_lo, first, last):
                pe.matmul(out_, a_hi, w_hi, start=first, stop=False)
                pe.matmul(out_, a_hi, w_lo, start=False, stop=False)
                return pe.matmul(out_, a_lo, w_hi, start=False, stop=last)

            def s_qkv(seq, unit):
                p, n = seq.odd, misc_ring.slot("s_qkv", 0, seq)
                wait(pe, sem["xT_split"], seq)
                misc_ring.wait_free(pe, sem, "s_qkv", 0, seq)
                for k in range(2):
                    mm = three(misc[:, n, 0:QKV], xT_hi[p][:, k, :], xT_lo[p][:, k, :], wqkv_hi[:, k, :], wqkv_lo[:, k, :],
                               k == 0, k == 1)
                mm.then_inc(sem["s_qkv_full"], 1)

            def s_turn(seq, unit):
                wait(pe, sem["s_rows_lo"], seq)
                if seq.i is None and seq.off == 0:
                    pe.wait_ge(sem["tables"], 3)
                for u in range(2):
                    n = misc_ring.slot("s_turn", 0, seq, u)
                    misc_ring.wait_free(pe, sem, "s_turn", 0, seq, u)
                    for j in range(4):
                        mm = pe.transpose(misc[0:96, n, S * j:S * j + S].bitcast(F32R), rows_s[:, 4 * u + j, :], ident_r[:])
                    mm.then_inc(sem["s_q_full"], 1)
                n = misc_ring.slot("s_turn", 0, seq, 2)
                misc_ring.wait_free(pe, sem, "s_turn", 0, seq, 2)
                pe.transpose(misc[0:96, n, 0:S].bitcast(F32R), rows_s[:, 8, :], ident_r[:]).then_inc(sem["s_k_full"], 1)

            def s_max(seq, unit):
                p, n = seq.odd, score_ring.slot("s_max", unit, seq)
                wait(pe, sem["s_q_read"], seq, 2, unit + 1)
                wait(pe, sem["s_k_read"], seq)
                score_ring.wait_free(pe, sem, "s_max", unit, seq)
                for bank in range(2):
                    at = 512 * bank
                    pe.matmul(scores[:, n, at:at + 512], ident_b[:], mask_qk[:], start=True, stop=False)
                    for v in range(2):
                        mm = pe.matmul(scores[:, n, at + 256 * v:at + 256 * v + 256], q_s[p][0:96, 4 * unit + 2 * bank + v, :],
                                       k_s[p][0:96], start=False, stop=(v == 1))
                mm.then_inc(sem["s_max_full"], 1)

            def shift(stage, seq, maxima, read, per, full):
                n = misc_ring.slot(stage, 0, seq)
                wait(pe, sem[read], seq, per)
                misc_ring.wait_free(pe, sem, stage, 0, seq)
                pe.transpose(misc[0:32, n, 0:S], maxima[:], ident[:]).then_inc(sem[full], 1)

            def s_shift(seq, unit):
                shift("s_shift", seq, max_s, "s_max_read", 2, "s_shift_full")

            def c_shift(seq, unit):
                shift("c_shift", seq, max_c, "c_max_read", 4, "c_shift_full")

            def s_main(seq, b):
                p, n = seq.odd, score_ring.slot("s_main", b, seq)
                wait(pe, sem["s_shift_read"], seq)
                score_ring.wait_free(pe, sem, "s_main", b, seq)
                for bank in range(2):
                    at = 512 * bank
                    pe.matmul(scores[:, n, at:at + 512], ident_b[:], mask_kq[:], start=True, stop=False)
                    mm = pe.matmul(scores[:, n, at:at + 512], k_s[p][:, b, :], q_s[p][:, 4 * bank:4 * bank + 4, :],
                                   start=False, stop=True)
                mm.then_inc(sem["s_main_full"], 1)

            def s_sum(seq, b):
                p, n, m = seq.odd, sum_ring.slot("s_sum", b, seq), prob_ring.slot("s_exp", b, seq)
                wait(pe, sem["s_prob_lo"], seq, 2, b + 1)
                sum_ring.wait_free(pe, sem, "s_sum", b, seq)
                v = v_s[p][:].rearrange("p h s -> p (h s)")
                for h in range(2):
                    w = v[:, P * h:P * h + P]
                    pe.matmul(sums[:, n, :], w, prob_hi[:, m, 512 * h:512 * h + 512], start=(h == 0), stop=False)
                    mm = pe.matmul(sums[:, n, :], w, prob_lo[:, m, 512 * h:512 * h + 512], start=False, stop=(h == 1))
                mm.then_inc(sem["s_summed"], 1)

            def turn_sums(stage, seq, unit, source, read, full):
                n = misc_ring.slot(stage, unit, seq)
                wait(pe, sem[read], seq, 2, unit + 1)
                misc_ring.wait_free(pe, sem, stage, unit, seq)
                for j in range(4):
                    mm = pe.transpose(misc[:, n, S * j:S * j + S], source[:, unit, S * j:S * j + S], ident[:])
                mm.then_inc(sem[full], 1)

            def s_out(seq, b):
                turn_sums("s_out", seq, b, sumT_s, "s_sum_read", "s_out_full")

            def c_out(seq, a):
                turn_sums("c_out", seq, a, sumT_c, "c_sum_read", "c_out_full")

            def s_proj(seq, unit):
                n = misc_ring.slot("s_proj", 0, seq)
                wait(pe, sem["s_ctx"], seq, 2)
                misc_ring.wait_free(pe, sem, "s_proj", 0, seq)
                for k in range(2):
                    mm = pe.transpose(misc[:, n, S * k:S * k + S], ctx_s[seq.odd][:, P * k:P * k + P], ident[:])
                mm.then_inc(sem["s_ctx_full"], 1)

            def s_res(seq, unit):
                n = misc_ring.slot("s_res", 0, seq)
                wait(pe, sem["s_ctx_read"], seq)
                if seq.i is None and seq.off == 0:
                    pe.wait_ge(sem["wo_split"], 1)
                misc_ring.wait_free(pe, sem, "s_res", 0, seq)
                for k in range(2):
                    mm = three(misc[:, n, 0:D], ctxT_hi[:, k, :], ctxT_lo[:, k, :], wo_hi[:, k, :], wo_lo[:, k, :],
                               k == 0, k == 1)
                mm.then_inc(sem["s_res_full"], 1)

            def c_turn(seq, unit):
                wait(pe, sem["c_rows_lo"], seq)
                for u in range(2):
                    n = misc_ring.slot("c_turn", 0, seq, u)
                    misc_ring.wait_free(pe, sem, "c_turn", 0, seq, u)
                    for j in range(4):
                        mm = pe.transpose(misc[0:96, n, S * j:S * j + S].bitcast(F32R), rows_c[:, 4 * u + j, :], ident_r[:])
                    mm.then_inc(sem["c_q_full"], 1)

            def c_max(seq, unit):
                p, n = seq.odd, score_ring.slot("c_max", unit, seq)
                wait(pe, sem["c_q_read"], seq, 2, unit // 2 + 1)
                wait(pe, sem["ctx_k_set"], seq)
                score_ring.wait_free(pe, sem, "c_max", unit, seq)
                for v in range(2):
                    mm = pe.matmul(scores[:, n, 512 * v:512 * v + 512], q_c[p][0:96, 2 * unit + v, :],
                                   k_c[p][0:96, unit // 2], start=True, stop=True)
                mm.then_inc(sem["c_max_full"], 1)

            def c_main(seq, unit):
                p, n, a = seq.odd, score_ring.slot("c_main", unit, seq), unit // 2
                wait(pe, sem["c_shift_read"], seq)
                score_ring.wait_free(pe, sem, "c_main", unit, seq)
                for v in range(2):
                    mm = pe.matmul(scores[:, n, 512 * v:512 * v + 512], k_c[p][:, a, 2 * (unit % 2) + v, :],
                                   q_c[p][:, 4 * a:4 * a + 4, :], start=True, stop=True)
                mm.then_inc(sem["c_main_full"], 1)

            def c_sum(seq, unit):
                p, a, m = seq.odd, unit // 2, prob_ring.slot("c_exp", unit, seq)
                n = sum_ring.slot("c_sum", 2 * a, seq)
                wait(pe, sem["c_prob_lo"], seq, 4, unit + 1)
                wait(pe, sem["ctx_v_set"], seq)
                if unit % 2 == 0:
                    sum_ring.wait_free(pe, sem, "c_sum", unit, seq)
                for v in range(2):
                    j = 2 * (unit % 2) + v
                    w = v_c[p][:, a, P * j:P * j + P]
                    pe.matmul(sums[:, n, :], w, prob_hi[:, m, 512 * v:512 * v + 512], start=(j == 0), stop=False)
                    mm = pe.matmul(sums[:, n, :], w, prob_lo[:, m, 512 * v:512 * v + 512], start=False, stop=(j == 3))
                mm.then_inc(sem["c_summed"], 1)

            pe.wait_ge(sem["w_split"], 1)
            run(pe, PE_ORDER, dict(s_qkv=s_qkv, s_turn=s_turn, s_max=s_max, s_shift=s_shift, s_main=s_main, s_sum=s_sum, s_out=s_out,
                         s_proj=s_proj, s_res=s_res, c_turn=c_turn, c_max=c_max, c_shift=c_shift, c_main=c_main,
                         c_sum=c_sum, c_out=c_out))


def experts(nc, exp_gu, exp_down, stream, ident, eps, router, weights0, out):
    raw_gate, gate_hi, gate_lo, descending = router
    raw_gu0, raw_down0, gu_hi0, gu_lo0, down_hi0, down_lo0, raw_loaded, gu_split, down_split = weights0
    with ExitStack() as scope:
        def sb(name, shape, dt=F32):
            return scope.enter_context(nc.sbuf_tensor(name, shape, dt))

        inner = scope.enter_context(nc.psum_tensor("inner", [P, 4, 512], F32))
        y = scope.enter_context(nc.psum_tensor("y", [P, 2, 2, 512], F32))

        raw_gu = [raw_gu0, sb("raw_gu1", [P, 2, 2 * INNER])]
        raw_down = [raw_down0, sb("raw_down1", [P, INNER // P, D])]
        gu_hi = [gu_hi0, sb("gu_hi1", [P, 2, 2 * INNER], F32R)]
        gu_lo = [gu_lo0, sb("gu_lo1", [P, 2, 2 * INNER], F32R)]
        down_hi = [down_hi0, sb("down_hi1", [P, INNER // P, D], F32R)]
        down_lo = [down_lo0, sb("down_lo1", [P, INNER // P, D], F32R)]
        sT_hi, sT_lo = sb("sT_hi", [P, 2, B * S], F32R), sb("sT_lo", [P, 2, B * S], F32R)
        logitsT = sb("logitsT", [EXPERTS, B * S])
        gates = {n: sb(f"gate_{n}", [P, B, EXPERTS]) for n in "shifted e p order first rest order2 second both w".split()}
        stat = {n: sb(f"stat_{n}", [P, B]) for n in "max sum rsum p1 o1 p2 o2 wsum rwsum".split()}
        share = sb("share", [P, B, NETS])
        silu = sb("silu", [P, 2, GROUP])
        hidden = [sb(f"hidden{p}", [P, 4, GROUP]) for p in range(2)]
        hidden_hi = [sb(f"hidden_hi{p}", [P, 4, GROUP], F32R) for p in range(2)]
        hidden_lo = [sb(f"hidden_lo{p}", [P, 4, GROUP], F32R) for p in range(2)]
        zeros = sb("zeros", [P, 1024])
        stats, mv = sb("stats", [P, B, 6]), sb("mv", [P, B, 2])
        lnv, r0, t0, t1, rstd = (sb(n, [P, B]) for n in ("lnv", "r0", "t0", "t1", "rstd"))

        names = """sT_full sT_hi_set sT_set logits_full logits_read gates_full step exps
            inner_full silu_set hidden_set hidden_hi_set hidden_lo_set y_full y_read w_hi stats_set aggr ln_set rsqrt0 newton
            normed stored""".split()
        sem = {n: scope.enter_context(nc.semaphore("b_" + n)) for n in names}

        def f32(ap):
            return ap.bitcast(F32)

        def run(eng, net):
            net(Seq(0))
            with eng.Fori(0, EXPERTS // 2 - 1) as i:
                net(Seq(1, i))
                net(Seq(2, i))
            net(Seq(EXPERTS - 1))
            net(Seq(EXPERTS))

        def upto(eng, s, seq, per, plus):
            if seq.i is not None or per * seq.off + plus > 0:
                eng.wait_ge(s, seq.at(per, plus))

        def first(seq):
            return seq.i is None and seq.off == 0

        block = scope.enter_context(nc.Block())

        @block.sync
        def _(sp):
            def load(seq):
                sp.wait_ge(gu_split, seq.at(1, -1))
                sp.wait_ge(down_split, seq.at(1, -1))
                load_net(sp, seq.at(1, -1), raw_gu[seq.odd], raw_down[seq.odd], raw_loaded[seq.odd], exp_gu, exp_down)

            load_net(sp, 0, raw_gu[1], raw_down[1], raw_loaded[1], exp_gu, exp_down)
            load(Seq(2))
            with sp.Fori(0, (EXPERTS - 2) // 2) as i:
                load(Seq(3, i))
                load(Seq(4, i))
            tiles = out.rearrange("(t p) d -> p t d", p=P)
            stores = [(0, 4), (4, 8), (8, 12), (12, 14), (14, 16)]
            for a, b in stores:
                sp.wait_ge(sem["normed"], b // 2)
                sp.dma_start(tiles[:, a:b, :], stream[:, a:b, :]).then_inc(sem["stored"], 16)
            sp.wait_ge(sem["stored"], 16 * len(stores))

        @block.gpsimd
        def _(pool):
            def split_next(seq, k):
                q = 1 - seq.odd
                if k == 0:
                    upto(pool, sem["y_full"], seq, 8, 0)
                    nxt = 32 * ((seq.off + 1) // 2 + 1)
                    pool.wait_ge(raw_loaded[q], nxt if seq.i is None else seq.i * 32 + nxt)
                hi, lo, raw = ((gu_hi[q][:, k, :], gu_lo[q][:, k, :], raw_gu[q][:, k, :]) if k < 2 else
                               (down_hi[q][:], down_lo[q][:], raw_down[q][:]))
                pool.tensor_tensor(hi, raw, zeros[:, 0:1024] if k < 2 else zeros[:, 0:1024].rearrange("p (a b) -> p a b", b=D),
                                   ALU.add).then_inc(sem["w_hi"], 1)
                upto(pool, sem["w_hi"], seq, 3, k + 1)
                ins = pool.tensor_tensor(lo, raw, f32(hi), ALU.subtract)
                if k:
                    ins.then_inc(gu_split if k == 1 else down_split, 1)

            def net(seq, last=False):
                for g in range(GROUPS):
                    for c in range(4):
                        upto(pool, sem["hidden_hi_set"], seq, 16, 4 * g + c + 1)
                        upto(pool, sem["y_full"], seq, 8, 2 * g - 2)
                        pool.tensor_tensor(hidden_lo[g % 2][:, c], hidden[g % 2][:, c], f32(hidden_hi[g % 2][:, c]),
                                           ALU.subtract).then_inc(sem["hidden_lo_set"], 1)
                    if g < 3 and not last:
                        split_next(seq, g)

            net(Seq(0))
            with pool.Fori(0, EXPERTS // 2 - 1) as i:
                net(Seq(1, i))
                net(Seq(2, i))
            net(Seq(EXPERTS - 1))
            net(Seq(EXPERTS), last=True)

        @block.scalar
        def _(act):
            def stream_high(g):
                act.wait_ge(sem["sT_full"], g + 1)
                act.copy(sT_hi[:, :, GROUP * g:GROUP * g + GROUP], y[:, g % 2]).then_inc(sem["sT_hi_set"], 1)

            stream_high(0)

            def net(seq):
                for g in range(GROUPS):
                    if first(seq) and g + 1 < GROUPS:
                        stream_high(g + 1)
                    for c in range(4):
                        at = 4 * g + c
                        upto(act, sem["inner_full"], seq, 16, at + 1)
                        upto(act, sem["hidden_set"], seq, 16, at - 1)
                        act.activation(silu[:, c % 2, :], inner[:, 2 * (c % 2), :], ACT.Silu).then_inc(sem["silu_set"], 1)
                        if c:
                            high(seq, g, c - 1)
                        if first(seq) and (g, c) == (GROUPS - 1, 2):
                            act.wait_ge(sem["step"], 2)
                            act.activation(gates["e"][:], gates["shifted"][:], ACT.Exp).then_inc(sem["exps"], 1)
                    high(seq, g, 3)

            def high(seq, g, c):
                upto(act, sem["hidden_set"], seq, 16, 4 * g + c + 1)
                upto(act, sem["y_full"], seq, 8, 2 * g - 2)
                act.copy(hidden_hi[g % 2][:, c], hidden[g % 2][:, c]).then_inc(sem["hidden_hi_set"], 1)

            run(act, net)
            act.preload_act_table_set("natural_log_exp_and_others")
            for n, (a, b) in enumerate(NORM_PARTS):
                act.wait_ge(sem["aggr"], n + 1)
                act.activation(lnv[:, a:b], mv[:, a:b, 1:2].squeeze(2), ACT.Ln, bias=eps[:]).then_inc(sem["ln_set"], 1)
                act.wait_ge(sem["ln_set"], n + 1)
                act.activation(r0[:, a:b], lnv[:, a:b], ACT.Exp, scale=-0.5).then_inc(sem["rsqrt0"], 1)

        @block.vector
        def _(dve):
            dve.memset(share[:, :, 0:1], 1.0)
            dve.memset(zeros[:], 0.0)

            def stream_low(g):
                dve.wait_ge(sem["sT_hi_set"], g + 1)
                cols = slice(GROUP * g, GROUP * g + GROUP)
                dve.tensor_tensor(sT_lo[:, :, cols], y[:, g % 2], f32(sT_hi[:, :, cols]), ALU.subtract).then_inc(sem["sT_set"], 1)

            def read_logits(g):
                dve.wait_ge(sem["logits_full"], g + 1)
                dve.tensor_copy(logitsT[:, GROUP * g:GROUP * g + GROUP], y[0:EXPERTS, g % 2, 1, :]).then_inc(sem["logits_read"], 1)

            stream_low(0)
            read_logits(0)

            done = [0]

            def then(ins):
                done[0] += 1
                ins.then_inc(sem["step"], 1)
                dve.wait_ge(sem["step"], done[0])

            def all8(t):
                return t[:].unsqueeze(2).broadcast_to([P, B, EXPERTS])

            order = descending[:].unsqueeze(1).broadcast_to([P, B, EXPERTS])
            logits = y[:, 1, 0, 0:B * EXPERTS].rearrange("p (t n) -> p t n", n=EXPERTS)
            def shift_logits():
                dve.wait_ge(sem["gates_full"], 1)
                then(dve.tensor_reduce(stat["max"][:], logits, AX.X, ALU.max))
                then(dve.tensor_tensor(gates["shifted"][:], logits, all8(stat["max"]), ALU.subtract))

            def shares():
                dve.wait_ge(sem["exps"], 1)
                then(dve.tensor_reduce(stat["sum"][:], gates["e"][:], AX.X, ALU.add))
                then(dve.reciprocal(stat["rsum"][:], stat["sum"][:]))
                then(dve.tensor_tensor(gates["p"][:], gates["e"][:], all8(stat["rsum"]), ALU.mult))
                then(dve.tensor_reduce(stat["p1"][:], gates["p"][:], AX.X, ALU.max))
                then(dve.tensor_tensor(gates["order"][:], gates["p"][:], all8(stat["p1"]), ALU.is_equal))
                then(dve.tensor_tensor(gates["order"][:], gates["order"][:], order, ALU.mult))
                then(dve.tensor_reduce(stat["o1"][:], gates["order"][:], AX.X, ALU.max))
                then(dve.tensor_tensor(gates["first"][:], gates["order"][:], all8(stat["o1"]), ALU.is_equal))
                then(dve.scalar_tensor_tensor(gates["rest"][:], gates["first"][:], -2.0, gates["p"][:], ALU.mult, ALU.add))
                then(dve.tensor_reduce(stat["p2"][:], gates["rest"][:], AX.X, ALU.max))
                then(dve.tensor_tensor(gates["order2"][:], gates["rest"][:], all8(stat["p2"]), ALU.is_equal))
                then(dve.tensor_tensor(gates["order2"][:], gates["order2"][:], order, ALU.mult))
                then(dve.tensor_reduce(stat["o2"][:], gates["order2"][:], AX.X, ALU.max))
                then(dve.tensor_tensor(gates["second"][:], gates["order2"][:], all8(stat["o2"]), ALU.is_equal))
                then(dve.tensor_tensor(gates["both"][:], gates["first"][:], gates["second"][:], ALU.add))
                then(dve.tensor_tensor(gates["w"][:], gates["p"][:], gates["both"][:], ALU.mult))
                then(dve.tensor_reduce(stat["wsum"][:], gates["w"][:], AX.X, ALU.add))
                then(dve.reciprocal(stat["rwsum"][:], stat["wsum"][:]))
                then(dve.tensor_tensor(share[:, :, 1:NETS], gates["w"][:], all8(stat["rwsum"]), ALU.mult))

            def add_outputs(seq, g):
                for bank in range(2):
                    upto(dve, sem["y_full"], seq, 8, 2 * g + bank + 1)
                    upto(dve, sem["y_read"], seq, 8, 2 * g)
                    for v in range(2):
                        t = TILES * g + 2 * bank + v
                        ins = dve.scalar_tensor_tensor(stream[:, t, :], y[:, g % 2, bank, D * v:D * v + D],
                                                       share[:, t, bass.ds(seq.at(1), 1)], stream[:, t, :], ALU.mult, ALU.add)
                    ins.then_inc(sem["y_read"], 1)
                    if seq.i is None and seq.off == NETS - 1:
                        dve.wait_ge(sem["y_read"], seq.at(8, 2 * g + bank + 1))
                        for v in range(2):
                            t = TILES * g + 2 * bank + v
                            ins = dve.bn_stats(stats[:, t, :], stream[:, t, :])
                        ins.then_inc(sem["stats_set"], 1)

            def net(seq):
                for g in range(GROUPS):
                    if first(seq) and g + 1 < GROUPS:
                        stream_low(g + 1)
                    for c in range(4):
                        at = 4 * g + c
                        upto(dve, sem["silu_set"], seq, 16, at + 1)
                        upto(dve, sem["hidden_lo_set"], seq, 16, at - 7)
                        dve.tensor_tensor(hidden[g % 2][:, c], silu[:, c % 2, :], inner[:, 2 * (c % 2) + 1, :], ALU.mult)\
                            .then_inc(sem["hidden_set"], 1)
                        if first(seq) and (g, c) == (GROUPS - 1, 1):
                            shift_logits()
                    if first(seq):
                        if g + 1 < GROUPS:
                            read_logits(g + 1)
                        else:
                            shares()
                    if g:
                        add_outputs(seq, g - 1)
                    elif seq.off or seq.i is not None:
                        add_outputs(seq.back(1), GROUPS - 1)

            run(dve, net)
            chain = [0]

            def link(ins):
                chain[0] += 1
                ins.then_inc(sem["newton"], 1)
                dve.wait_ge(sem["newton"], chain[0])

            def normalize(a, b):
                for t in range(a, b):
                    ins = dve.tensor_scalar(stream[:, t, :], stream[:, t, :], mv[:, t, 0:1], rstd[:, t:t + 1],
                                            ALU.subtract, ALU.mult)
                    if t % 2:
                        ins.then_inc(sem["normed"], 1)

            for n, (a, b) in enumerate(NORM_PARTS):
                if n == 1:
                    add_outputs(Seq(NETS - 1), GROUPS - 1)
                dve.wait_ge(sem["stats_set"], b // 2)
                for t in range(a, b):
                    ins = dve.bn_aggr(mv[:, t, :], stats[:, t, :])
                ins.then_inc(sem["aggr"], 1)
                if n == 1:
                    normalize(a - TILES, a)
                dve.wait_ge(sem["rsqrt0"], n + 1)
                link(dve.scalar_tensor_tensor(t0[:, a:b], mv[:, a:b, 1:2].squeeze(2), EPS, r0[:, a:b], ALU.add, ALU.mult))
                link(dve.scalar_tensor_tensor(t1[:, a:b], t0[:, a:b], -0.5, r0[:, a:b], ALU.mult, ALU.mult))
                link(dve.scalar_tensor_tensor(rstd[:, a:b], t1[:, a:b], 1.5, r0[:, a:b], ALU.add, ALU.mult))
                normalize(a, b - TILES if n == 0 else b)

        @block.tensor
        def _(pe):
            def turn_stream(g):
                if g >= 2:
                    pe.wait_ge(sem["sT_set"], g - 1)
                    pe.wait_ge(sem["logits_read"], g - 1)
                for k in range(2):
                    for t in range(TILES):
                        mm = pe.transpose(y[:, g % 2, k, P * t:P * t + P], stream[:, TILES * g + t, P * k:P * k + P], ident[:])
                mm.then_inc(sem["sT_full"], 1)

            def router_logits(g):
                pe.wait_ge(sem["sT_set"], g + 1)
                cols = slice(GROUP * g, GROUP * g + GROUP)
                o = y[0:EXPERTS, g % 2, 1, :]
                for k in range(2):
                    pe.matmul(o, gate_hi[:, k, :], sT_hi[:, k, cols], start=(k == 0), stop=False)
                    pe.matmul(o, gate_lo[:, k, :], sT_hi[:, k, cols], start=False, stop=False)
                    mm = pe.matmul(o, gate_hi[:, k, :], sT_lo[:, k, cols], start=False, stop=(k == 1))
                mm.then_inc(sem["logits_full"], 1)

            def turn_logits():
                pe.wait_ge(sem["logits_read"], GROUPS)
                pe.wait_ge(sem["y_read"], 4)
                for t in range(B):
                    mm = pe.transpose(y[:, 1, 0, EXPERTS * t:EXPERTS * t + EXPERTS], logitsT[:, P * t:P * t + P],
                                      ident[0:EXPERTS, 0:EXPERTS])
                mm.then_inc(sem["gates_full"], 1)

            turn_stream(0)
            router_logits(0)

            def inner_products(seq, g):
                p = seq.odd
                cols = slice(GROUP * g, GROUP * g + GROUP)
                if g == 0:
                    upto(pe, gu_split, seq, 1, 1)
                for c in range(4):
                    upto(pe, sem["hidden_set"], seq, 16, 4 * g + c - 1)
                    for half in range(2):
                        bank = 2 * (c % 2) + half
                        at = slice(INNER * half + P * c, INNER * half + P * c + P)
                        for k in range(2):
                            pe.matmul(inner[:, bank, :], gu_hi[p][:, k, at], sT_hi[:, k, cols], start=(k == 0), stop=False)
                            pe.matmul(inner[:, bank, :], gu_hi[p][:, k, at], sT_lo[:, k, cols], start=False, stop=False)
                            mm = pe.matmul(inner[:, bank, :], gu_lo[p][:, k, at], sT_hi[:, k, cols], start=False, stop=(k == 1))
                    mm.then_inc(sem["inner_full"], 1)
                    if first(seq) and (g, c) == (GROUPS - 1, 1):
                        turn_logits()

            def outer_products(seq, g):
                p = seq.odd
                upto(pe, sem["hidden_lo_set"], seq, 16, 4 * g + 4)
                if g == 0:
                    upto(pe, down_split, seq, 1, 1)
                for bank in range(2):
                    if first(seq) and bank == 1:
                        pe.wait_ge(sem["logits_read"], min(g + 3, GROUPS))
                    upto(pe, sem["y_read"], seq, 8, 2 * (g - 2) + bank + 1)
                    for v in range(2):
                        t = 2 * bank + v
                        for c in range(4):
                            h_hi = hidden_hi[g % 2][:, c, P * t:P * t + P]
                            h_lo = hidden_lo[g % 2][:, c, P * t:P * t + P]
                            o = y[:, g % 2, bank, D * v:D * v + D]
                            pe.matmul(o, h_hi, down_hi[p][:, c, :], start=(c == 0), stop=False)
                            pe.matmul(o, h_hi, down_lo[p][:, c, :], start=False, stop=False)
                            mm = pe.matmul(o, h_lo, down_hi[p][:, c, :], start=False, stop=(c == 3))
                    mm.then_inc(sem["y_full"], 1)

            def net(seq):
                for g in range(GROUPS):
                    ahead = first(seq) and g + 1 < GROUPS
                    if ahead:
                        turn_stream(g + 1)
                    inner_products(seq, g)
                    if ahead:
                        router_logits(g + 1)
                    if g:
                        outer_products(seq, g - 1)
                    elif not first(seq):
                        outer_products(seq.back(1), GROUPS - 1)
                if first(seq):
                    pe.wait_ge(sem["step"], 2)

            run(pe, net)
            outer_products(Seq(NETS - 1), GROUPS - 1)


def constants():
    c = np.zeros((P, CONST_COLS), np.float32)
    q, r = np.arange(P), np.arange(P)
    c[:, 0:P] = np.eye(P)
    c[:, P:2 * P] = np.where(q[None, :] <= q[:, None], 0.0, MASKED)
    c[:, 2 * P:3 * P] = c[:, P:2 * P].T
    at = 3 * P
    for b in range(2):
        c[:, at + b] = np.where(r < 96, r % 32 // HD == b, (r < 96 + HEADS) & (r % 2 == b))
    for j in range(4):
        c[:, at + 2 + j] = np.where(r < 96, r % 32 // XD == j, r % 4 == j)
    for n in range(8):
        c[0:32, at + 6 + n] = -1.0 * ((r[:32] < HEADS) & (r[:32] // 2 == n))
        c[0:32, at + 14 + n] = -1.0 * (r[:32] // 4 == n)
    c[:, CONST_COLS - EXPERTS:] = np.arange(EXPERTS, 0, -1)
    return c


def kernel(x, ctx_512, L0_attn_Wqkv_w, L0_attn_Wqkv_b, L0_attn_out_w, L0_attn_out_b, L0_ffn_gate_w,
           L0_ffn_base_gate_up, L0_ffn_base_down, L0_ffn_expert_gate_up, L0_ffn_expert_down):
    import concourse.bacc as bacc
    from concourse.bass_utils import run_bass_kernel_spmd

    x = np.asarray(x).reshape(B * S, D)
    ctx = np.asarray(ctx_512).reshape(B * S, XKV * XD)
    ctxT = np.tile(ctx.reshape(B * S, 2, 32).transpose(2, 1, 0), (3, 1, 1))
    arrays = dict(
        x=x, xT=x.T, ctx=ctx, ctxT=ctxT, wqkvT=np.asarray(L0_attn_Wqkv_w).T, bqkv=L0_attn_Wqkv_b,
        woT=np.asarray(L0_attn_out_w).T, bo=L0_attn_out_b, gate_w=L0_ffn_gate_w, base_gu=L0_ffn_base_gate_up,
        base_down=L0_ffn_base_down, exp_gu=L0_ffn_expert_gate_up, exp_down=L0_ffn_expert_down, consts=constants())
    arrays = {f"in_{n}": np.ascontiguousarray(a) for n, a in arrays.items()}
    nc = bacc.Bacc("TRN2", target_bir_lowering=False, num_devices=1)
    args = [nc.dram_tensor(n, a.shape, mybir.dt.from_np(a.dtype), kind="ExternalInput").ap() for n, a in arrays.items()]
    args.append(nc.dram_tensor("out", (B * S, D), F32, kind="ExternalOutput").ap())
    decoder_layer(nc, *args)
    r = run_bass_kernel_spmd(nc, [arrays], core_ids=[0])
    return r.results[0]["out"].reshape(B, S, D)
```
